# Optimizing a Trainium2 kernel written in Bass

```python
import numpy as np
import jax
import jax.numpy as jnp

def _softmax(x, axis=-1):
    return jax.nn.softmax(x, axis=axis)

def _gelu(x):
    return jax.nn.gelu(x, approximate=True)

def _silu(x):
    return jax.nn.silu(x)

def _sigmoid(x):
    return jax.nn.sigmoid(x)

def _layernorm(x, axis=-1, eps=1e-05):
    m = jnp.mean(x, axis=axis, keepdims=True)
    v = jnp.var(x, axis=axis, keepdims=True)
    return (x - m) / jnp.sqrt(v + eps)

def _scatter_add(tgt, idx, src, axis=0):
    return tgt.at[idx].add(src)

def _segment_sum(src, seg, n):
    return jax.ops.segment_sum(src, seg, n)
kernel_name = 'mk_vit_tower_cls_d2_tok_img256_r4_a3536b'

def setup_inputs(seed: int=0):
    np.random.seed(seed)
    _w = jnp.asarray

    def _rec_inputs():
        import jax
        import jax.numpy as jnp
        _rk = jax.random.key(seed)
        x = -0.000928989 + 1.00043 * jax.random.normal(jax.random.fold_in(_rk, 1), (32, 64, 64, 1), jnp.float32)
        cls_tok = 0.02 * jax.random.normal(jax.random.fold_in(_rk, 5), (1, 1, 64), jnp.float32)
        return (x, cls_tok)
    x, cls_tok = _rec_inputs()

    def _L0_tok_setup():
        import jax, jax.numpy as jnp
        import numpy as np
        B, S, D_A, D_V, D_U, L, M1, M2 = (16, 64, 3, 32, 1, 4, 12, 12)
        MID = 4 * D_U

        def conv1x1(x, w, b):
            return jnp.einsum('bixy,oi->boxy', x, w) + b[None, :, None, None]

        def fourier_layer(x, fw_i):
            Bm, C, M, N = x.shape
            x_ft = jnp.fft.rfft2(x, s=(M, N), norm='ortho')
            w_lo = fw_i[0, ..., 0] + 1j * fw_i[0, ..., 1]
            w_hi = fw_i[1, ..., 0] + 1j * fw_i[1, ..., 1]
            lo = jnp.einsum('bixy,ioxy->boxy', x_ft[:, :, :M1, :M2], w_lo)
            hi = jnp.einsum('bixy,ioxy->boxy', x_ft[:, :, -M1:, :M2], w_hi)
            out_ft = jnp.zeros(x_ft.shape, dtype=x_ft.dtype)
            out_ft = out_ft.at[:, :, :M1, :M2].set(lo)
            out_ft = out_ft.at[:, :, -M1:, :M2].set(hi)
            return jnp.fft.irfft2(out_ft, s=(M, N), norm='ortho')

        def make_grid(b, sx, sy):
            gx = jnp.broadcast_to(jnp.linspace(0.0, 1.0, sx)[None, :, None], (b, sx, sy))
            gy = jnp.broadcast_to(jnp.linspace(0.0, 1.0, sy)[None, None, :], (b, sx, sy))
            return jnp.stack([gx, gy], axis=-1)
        key = jax.random.key(seed)
        ks = jax.random.split(key, 12)
        sc_v = 1.0 / np.sqrt(D_V)
        inp = {'x': jax.random.normal(ks[0], (B, S, S, D_A - 2), dtype=jnp.float32), 'p_w': jax.random.normal(ks[1], (D_V, D_A), dtype=jnp.float32) / np.sqrt(D_A), 'p_b': jnp.zeros((D_V,), dtype=jnp.float32), 'fw': jax.random.normal(ks[2], (L, 2, D_V, D_V, M1, M2, 2), dtype=jnp.float32) * sc_v, 'w1_w': jax.random.normal(ks[3], (L, D_V, D_V), dtype=jnp.float32) * sc_v, 'w1_b': jnp.zeros((L, D_V), dtype=jnp.float32), 'w2_w': jax.random.normal(ks[4], (L, D_V, D_V), dtype=jnp.float32) * sc_v, 'w2_b': jnp.zeros((L, D_V), dtype=jnp.float32), 'q1_w': jax.random.normal(ks[5], (MID, D_V), dtype=jnp.float32) * sc_v, 'q1_b': jnp.zeros((MID,), dtype=jnp.float32), 'q2_w': jax.random.normal(ks[6], (D_U, MID), dtype=jnp.float32) / np.sqrt(MID), 'q2_b': jnp.zeros((D_U,), dtype=jnp.float32)}
        return inp
    _L0_tok_all = _L0_tok_setup()
    _L0_tok_in = {k: v for k, v in _L0_tok_all.items() if k in ('p_w', 'p_b', 'fw', 'w1_w', 'w1_b', 'w2_w', 'w2_b', 'q1_w', 'q1_b', 'q2_w', 'q2_b')}
    del _L0_tok_all

    def _L0_attn_setup():
        import jax, jax.numpy as jnp
        import numpy as np
        HEAD_SIZE = 64
        HEAD_SIZE_R = HEAD_SIZE // 4
        HEAD_SIZE_C = HEAD_SIZE - HEAD_SIZE_R
        N_EMBD = 64

        def rope(x, start_pos=0):
            B, T, d = x.shape
            half = d // 2
            theta = 1.0 / 10000.0 ** (jnp.arange(half, dtype=x.dtype) / half)
            idx = jnp.arange(start_pos, start_pos + T, dtype=x.dtype)[:, None] * theta[None, :]
            sin, cos = (jnp.sin(idx), jnp.cos(idx))
            xs = x.reshape(B, T, half, 2)
            x1, x2 = (xs[..., 0], xs[..., 1])
            rot = jnp.stack([x1 * cos - x2 * sin, x1 * sin + x2 * cos], axis=-1)
            return rot.reshape(B, T, d)

        def _reference_tuple_inner(x, Wq_comp, Wkv_comp, Wqc, Wqr, Wkc, Wkr, Wv):
            c_q = x @ Wq_comp
            c_kv = x @ Wkv_comp
            q_c = c_q @ Wqc
            q_r = rope(c_q @ Wqr, start_pos=0)
            q = jnp.concatenate([q_c, q_r], axis=-1)
            k_c = c_kv @ Wkc
            k_r = rope(c_kv @ Wkr, start_pos=0)
            k = jnp.concatenate([k_c, k_r], axis=-1)
            v = c_kv @ Wv
            scale = 1.0 / jnp.sqrt(jnp.asarray(HEAD_SIZE, dtype=x.dtype))
            wei = jnp.einsum('bqd,bkd->bqk', q, k) * scale
            T_q = q.shape[1]
            mask = jnp.tril(jnp.ones((T_q, T_q), dtype=bool))
            wei = jnp.where(mask, wei, jnp.asarray(-jnp.inf, dtype=wei.dtype))
            wei = jax.nn.softmax(wei, axis=-1)
            out = jnp.einsum('bqk,bkd->bqd', wei, v)
            return (out, (k, v))
        key = jax.random.key(seed)
        ks = jax.random.split(key, 8)
        B, T = (32, 512)
        s = 0.05
        return {'x': jax.random.normal(ks[0], (B, T, N_EMBD), dtype=jnp.float32), 'Wq_comp': jax.random.normal(ks[1], (N_EMBD, N_EMBD), dtype=jnp.float32) * s, 'Wkv_comp': jax.random.normal(ks[2], (N_EMBD, N_EMBD), dtype=jnp.float32) * s, 'Wqc': jax.random.normal(ks[3], (N_EMBD, HEAD_SIZE_C), dtype=jnp.float32) * s, 'Wqr': jax.random.normal(ks[4], (N_EMBD, HEAD_SIZE_R), dtype=jnp.float32) * s, 'Wkc': jax.random.normal(ks[5], (N_EMBD, HEAD_SIZE_C), dtype=jnp.float32) * s, 'Wkr': jax.random.normal(ks[6], (N_EMBD, HEAD_SIZE_R), dtype=jnp.float32) * s, 'Wv': jax.random.normal(ks[7], (N_EMBD, HEAD_SIZE), dtype=jnp.float32) * s}
    _L0_attn_all = _L0_attn_setup()
    _L0_attn_in = {k: v for k, v in _L0_attn_all.items() if k in ('Wq_comp', 'Wkv_comp', 'Wqc', 'Wqr', 'Wkc', 'Wkr', 'Wv')}
    del _L0_attn_all

    def _L0_ffn_setup():
        import jax, jax.numpy as jnp
        import numpy as np
        B, S, D = (8, 1024, 64)
        H = 4 * D
        CAPACITY = 0.5
        key = jax.random.key(seed)
        ks = jax.random.split(key, 6)
        x = jax.random.normal(ks[0], (B, S, D), dtype=jnp.float32)
        attention_mask = jnp.zeros((B, 1, 1, S), dtype=jnp.float32)
        wr = jax.random.normal(ks[1], (D, 1), dtype=jnp.float32) * 0.02
        br = jnp.zeros((1,), dtype=jnp.float32)
        w1 = jax.random.normal(ks[2], (D, H), dtype=jnp.float32) * 0.02
        b1 = jnp.zeros((H,), dtype=jnp.float32)
        w2 = jax.random.normal(ks[3], (H, D), dtype=jnp.float32) * 0.02
        b2 = jnp.zeros((D,), dtype=jnp.float32)
        return {'x': x, 'attention_mask': attention_mask, 'wr': wr, 'br': br, 'w1': w1, 'b1': b1, 'w2': w2, 'b2': b2}
    _L0_ffn_all = _L0_ffn_setup()
    _L0_ffn_in = {k: v for k, v in _L0_ffn_all.items() if k in ('attention_mask', 'wr', 'br', 'w1', 'b1', 'w2', 'b2')}
    del _L0_ffn_all

    def _L1_attn_setup():
        import jax, jax.numpy as jnp
        import numpy as np
        TEMPERATURE = 1.0
        W_BLEND = 0.8
        EPS = 1e-12

        def _l2norm(x):
            n = jnp.sqrt(jnp.sum(x * x, axis=-1, keepdims=True))
            return x / jnp.maximum(n, EPS)
        key = jax.random.key(seed)
        feats = jax.random.normal(key, (4, 512, 64), dtype=jnp.float32)
        return {'feats': feats}
    _L1_attn_all = _L1_attn_setup()
    _L1_attn_in = {k: v for k, v in _L1_attn_all.items() if k in ()}
    del _L1_attn_all

    def _L1_ffn_setup():
        import jax, jax.numpy as jnp
        import numpy as np
        DIM = 64
        HEADS = 8
        NUM_KEYS = 64
        NUM_KV = NUM_KEYS ** 2
        PK_TOPK = 16
        FINAL_TOPK = 16
        DIM_KEY = DIM // 2
        P = 2

        def _pk(x, Wq_pk, pk_keys):
            b, n, _ = x.shape
            q = (x @ Wq_pk).reshape(b, n, P, HEADS, DIM_KEY).transpose(2, 0, 1, 3, 4)
            sim = jnp.einsum('pbnhd,pkhd->pbnhk', q, pk_keys)
            scores, idx = jax.lax.top_k(sim, PK_TOPK)
            idx0 = idx[0]
            idx1 = idx[1] * NUM_KEYS
            index = (idx0[..., :, None] + idx1[..., None, :]).reshape(b, n, HEADS, PK_TOPK * PK_TOPK)
            score = (scores[0][..., :, None] + scores[1][..., None, :]).reshape(b, n, HEADS, PK_TOPK * PK_TOPK)
            final_scores, pk_idx = jax.lax.top_k(score, FINAL_TOPK)
            final_indices = jnp.take_along_axis(index, pk_idx, axis=-1)
            final_scores = jax.nn.softmax(final_scores, axis=-1)
            return (final_scores, final_indices)
        key = jax.random.key(seed)
        ks = jax.random.split(key, 7)
        b, n = (2, 256)
        std = 0.02
        x = jax.random.normal(ks[0], (b, n, DIM), dtype=jnp.float32)
        Wq_pk = jax.random.normal(ks[1], (DIM, P * HEADS * DIM_KEY), dtype=jnp.float32) * std
        pk_keys = jax.random.normal(ks[2], (P, NUM_KEYS, HEADS, DIM_KEY), dtype=jnp.float32) * std
        Wq = jax.random.normal(ks[3], (DIM, HEADS * DIM), dtype=jnp.float32) * std
        keys_table = jax.random.normal(ks[4], (NUM_KV * HEADS, DIM), dtype=jnp.float32) * std
        values_table = jax.random.normal(ks[5], (NUM_KV * HEADS, DIM), dtype=jnp.float32) * std
        Wo = jax.random.normal(ks[6], (DIM * HEADS, DIM), dtype=jnp.float32) * std
        return {'x': x, 'Wq_pk': Wq_pk, 'pk_keys': pk_keys, 'Wq': Wq, 'keys_table': keys_table, 'values_table': values_table, 'Wo': Wo}
    _L1_ffn_all = _L1_ffn_setup()
    _L1_ffn_in = {k: v for k, v in _L1_ffn_all.items() if k in ('Wq_pk', 'pk_keys', 'Wq', 'keys_table', 'values_table', 'Wo')}
    del _L1_ffn_all
    return {'x': x, 'cls_tok': cls_tok, 'L0_tok_p_w': _L0_tok_in['p_w'], 'L0_tok_p_b': _L0_tok_in['p_b'], 'L0_tok_fw': _L0_tok_in['fw'], 'L0_tok_w1_w': _L0_tok_in['w1_w'], 'L0_tok_w1_b': _L0_tok_in['w1_b'], 'L0_tok_w2_w': _L0_tok_in['w2_w'], 'L0_tok_w2_b': _L0_tok_in['w2_b'], 'L0_tok_q1_w': _L0_tok_in['q1_w'], 'L0_tok_q1_b': _L0_tok_in['q1_b'], 'L0_tok_q2_w': _L0_tok_in['q2_w'], 'L0_tok_q2_b': _L0_tok_in['q2_b'], 'L0_attn_Wq_comp': _L0_attn_in['Wq_comp'], 'L0_attn_Wkv_comp': _L0_attn_in['Wkv_comp'], 'L0_attn_Wqc': _L0_attn_in['Wqc'], 'L0_attn_Wqr': _L0_attn_in['Wqr'], 'L0_attn_Wkc': _L0_attn_in['Wkc'], 'L0_attn_Wkr': _L0_attn_in['Wkr'], 'L0_attn_Wv': _L0_attn_in['Wv'], 'L0_ffn_attention_mask': _L0_ffn_in['attention_mask'], 'L0_ffn_wr': _L0_ffn_in['wr'], 'L0_ffn_br': _L0_ffn_in['br'], 'L0_ffn_w1': _L0_ffn_in['w1'], 'L0_ffn_b1': _L0_ffn_in['b1'], 'L0_ffn_w2': _L0_ffn_in['w2'], 'L0_ffn_b2': _L0_ffn_in['b2'], 'L1_ffn_Wq_pk': _L1_ffn_in['Wq_pk'], 'L1_ffn_pk_keys': _L1_ffn_in['pk_keys'], 'L1_ffn_Wq': _L1_ffn_in['Wq'], 'L1_ffn_keys_table': _L1_ffn_in['keys_table'], 'L1_ffn_values_table': _L1_ffn_in['values_table'], 'L1_ffn_Wo': _L1_ffn_in['Wo']}

def reference(x, cls_tok, L0_tok_p_w, L0_tok_p_b, L0_tok_fw, L0_tok_w1_w, L0_tok_w1_b, L0_tok_w2_w, L0_tok_w2_b, L0_tok_q1_w, L0_tok_q1_b, L0_tok_q2_w, L0_tok_q2_b, L0_attn_Wq_comp, L0_attn_Wkv_comp, L0_attn_Wqc, L0_attn_Wqr, L0_attn_Wkc, L0_attn_Wkr, L0_attn_Wv, L0_ffn_attention_mask, L0_ffn_wr, L0_ffn_br, L0_ffn_w1, L0_ffn_b1, L0_ffn_w2, L0_ffn_b2, L1_ffn_Wq_pk, L1_ffn_pk_keys, L1_ffn_Wq, L1_ffn_keys_table, L1_ffn_values_table, L1_ffn_Wo):
    import jax
    import jax.numpy as jnp

    def _L0_tok_ref(x, p_w, p_b, fw, w1_w, w1_b, w2_w, w2_b, q1_w, q1_b, q2_w, q2_b):
        import jax, jax.numpy as jnp
        import numpy as np
        B, S, D_A, D_V, D_U, L, M1, M2 = (16, 64, 3, 32, 1, 4, 12, 12)
        MID = 4 * D_U

        def conv1x1(x, w, b):
            return jnp.einsum('bixy,oi->boxy', x, w) + b[None, :, None, None]

        def fourier_layer(x, fw_i):
            Bm, C, M, N = x.shape
            x_ft = jnp.fft.rfft2(x, s=(M, N), norm='ortho')
            w_lo = fw_i[0, ..., 0] + 1j * fw_i[0, ..., 1]
            w_hi = fw_i[1, ..., 0] + 1j * fw_i[1, ..., 1]
            lo = jnp.einsum('bixy,ioxy->boxy', x_ft[:, :, :M1, :M2], w_lo)
            hi = jnp.einsum('bixy,ioxy->boxy', x_ft[:, :, -M1:, :M2], w_hi)
            out_ft = jnp.zeros(x_ft.shape, dtype=x_ft.dtype)
            out_ft = out_ft.at[:, :, :M1, :M2].set(lo)
            out_ft = out_ft.at[:, :, -M1:, :M2].set(hi)
            return jnp.fft.irfft2(out_ft, s=(M, N), norm='ortho')

        def make_grid(b, sx, sy):
            gx = jnp.broadcast_to(jnp.linspace(0.0, 1.0, sx)[None, :, None], (b, sx, sy))
            gy = jnp.broadcast_to(jnp.linspace(0.0, 1.0, sy)[None, None, :], (b, sx, sy))
            return jnp.stack([gx, gy], axis=-1)
        b, sx, sy = (x.shape[0], x.shape[1], x.shape[2])
        grid = make_grid(b, sx, sy)
        h = jnp.concatenate([x, grid], axis=-1)
        h = jnp.transpose(h, (0, 3, 1, 2))
        h = conv1x1(h, p_w, p_b)
        for i in range(L):
            x1 = fourier_layer(h, fw[i])
            x1 = jax.nn.relu(conv1x1(x1, w1_w[i], w1_b[i]))
            x1 = conv1x1(x1, w2_w[i], w2_b[i])
            h = h + x1
        h = conv1x1(h, q1_w, q1_b)
        h = jax.nn.relu(h)
        h = conv1x1(h, q2_w, q2_b)
        return jnp.squeeze(h)

    def _L0_attn_ref(x, Wq_comp, Wkv_comp, Wqc, Wqr, Wkc, Wkr, Wv):
        import jax, jax.numpy as jnp
        import numpy as np
        HEAD_SIZE = 64
        HEAD_SIZE_R = HEAD_SIZE // 4
        HEAD_SIZE_C = HEAD_SIZE - HEAD_SIZE_R
        N_EMBD = 64

        def rope(x, start_pos=0):
            B, T, d = x.shape
            half = d // 2
            theta = 1.0 / 10000.0 ** (jnp.arange(half, dtype=x.dtype) / half)
            idx = jnp.arange(start_pos, start_pos + T, dtype=x.dtype)[:, None] * theta[None, :]
            sin, cos = (jnp.sin(idx), jnp.cos(idx))
            xs = x.reshape(B, T, half, 2)
            x1, x2 = (xs[..., 0], xs[..., 1])
            rot = jnp.stack([x1 * cos - x2 * sin, x1 * sin + x2 * cos], axis=-1)
            return rot.reshape(B, T, d)

        def _reference_tuple_inner(x, Wq_comp, Wkv_comp, Wqc, Wqr, Wkc, Wkr, Wv):
            c_q = x @ Wq_comp
            c_kv = x @ Wkv_comp
            q_c = c_q @ Wqc
            q_r = rope(c_q @ Wqr, start_pos=0)
            q = jnp.concatenate([q_c, q_r], axis=-1)
            k_c = c_kv @ Wkc
            k_r = rope(c_kv @ Wkr, start_pos=0)
            k = jnp.concatenate([k_c, k_r], axis=-1)
            v = c_kv @ Wv
            scale = 1.0 / jnp.sqrt(jnp.asarray(HEAD_SIZE, dtype=x.dtype))
            wei = jnp.einsum('bqd,bkd->bqk', q, k) * scale
            T_q = q.shape[1]
            mask = jnp.tril(jnp.ones((T_q, T_q), dtype=bool))
            wei = jnp.where(mask, wei, jnp.asarray(-jnp.inf, dtype=wei.dtype))
            wei = jax.nn.softmax(wei, axis=-1)
            out = jnp.einsum('bqk,bkd->bqd', wei, v)
            return (out, (k, v))
        return _reference_tuple_inner(x, Wq_comp, Wkv_comp, Wqc, Wqr, Wkc, Wkr, Wv)[0]

    def _L0_ffn_ref(x, attention_mask, wr, br, w1, b1, w2, b2):
        import jax, jax.numpy as jnp
        import numpy as np
        B, S, D = (8, 1024, 64)
        H = 4 * D
        CAPACITY = 0.5
        b, s, d = x.shape
        weights = (jnp.einsum('bsd,do->bso', x, wr) + br)[..., 0]
        k = max(1, int(CAPACITY * s))
        kk = k - 1 if k > 1 else 1
        _, idx = jax.lax.top_k(weights, k)
        sel_idx = idx[:, :kk]
        sel = jnp.take_along_axis(x, sel_idx[:, :, None], axis=1)
        h = jax.nn.gelu(jnp.einsum('bkd,dh->bkh', sel, w1) + b1)
        y = jnp.einsum('bkh,hd->bkd', h, w2) + b2
        w_sel = jnp.take_along_axis(weights, sel_idx, axis=1)
        y = y * w_sel[..., None]
        batch_idx = jnp.arange(b)[:, None]
        processed = jnp.zeros_like(x).at[batch_idx, sel_idx].set(y)
        return processed + x

    def _L1_attn_ref(feats):
        import jax, jax.numpy as jnp
        import numpy as np
        TEMPERATURE = 1.0
        W_BLEND = 0.8
        EPS = 1e-12

        def _l2norm(x):
            n = jnp.sqrt(jnp.sum(x * x, axis=-1, keepdims=True))
            return x / jnp.maximum(n, EPS)
        B, N, C = feats.shape
        f = _l2norm(feats.reshape(B * N, C))
        scores = jnp.matmul(f, f.T) / TEMPERATURE
        attn = jax.nn.softmax(scores, axis=-1)
        feats_att = jnp.matmul(attn, f)
        feats_fcm = f * W_BLEND + feats_att * (1.0 - W_BLEND)
        return _l2norm(feats_fcm.reshape(B, N, C))

    def _L1_ffn_ref(x, Wq_pk, pk_keys, Wq, keys_table, values_table, Wo):
        import jax, jax.numpy as jnp
        import numpy as np
        DIM = 64
        HEADS = 8
        NUM_KEYS = 64
        NUM_KV = NUM_KEYS ** 2
        PK_TOPK = 16
        FINAL_TOPK = 16
        DIM_KEY = DIM // 2
        P = 2

        def _pk(x, Wq_pk, pk_keys):
            b, n, _ = x.shape
            q = (x @ Wq_pk).reshape(b, n, P, HEADS, DIM_KEY).transpose(2, 0, 1, 3, 4)
            sim = jnp.einsum('pbnhd,pkhd->pbnhk', q, pk_keys)
            scores, idx = jax.lax.top_k(sim, PK_TOPK)
            idx0 = idx[0]
            idx1 = idx[1] * NUM_KEYS
            index = (idx0[..., :, None] + idx1[..., None, :]).reshape(b, n, HEADS, PK_TOPK * PK_TOPK)
            score = (scores[0][..., :, None] + scores[1][..., None, :]).reshape(b, n, HEADS, PK_TOPK * PK_TOPK)
            final_scores, pk_idx = jax.lax.top_k(score, FINAL_TOPK)
            final_indices = jnp.take_along_axis(index, pk_idx, axis=-1)
            final_scores = jax.nn.softmax(final_scores, axis=-1)
            return (final_scores, final_indices)
        b, n, d = x.shape
        q = (x @ Wq).reshape(b, n, HEADS, DIM) * DIM ** (-0.5)
        kv_scores, indices = _pk(x, Wq_pk, pk_keys)
        offsets = jnp.arange(HEADS, dtype=indices.dtype) * NUM_KV
        ind = indices + offsets[None, None, :, None]
        k = jnp.einsum('bnhk,bnhkd->bnhd', kv_scores, keys_table[ind])
        v = jnp.einsum('bnhk,bnhkd->bnhd', kv_scores, values_table[ind])
        sim = jnp.einsum('bihd,bjhd->bhij', q, k)
        neg = -jnp.finfo(sim.dtype).max
        causal = jnp.tril(jnp.ones((n, n), dtype=bool))
        sim = jnp.where(causal, sim, neg)
        attn = jax.nn.softmax(sim, axis=-1)
        out = jnp.einsum('bhij,bjhd->bhid', attn, v)
        out = out.transpose(0, 2, 1, 3).reshape(b, n, HEADS * DIM)
        return out @ Wo
    h = _L0_tok_ref(x, L0_tok_p_w, L0_tok_p_b, L0_tok_fw, L0_tok_w1_w, L0_tok_w1_b, L0_tok_w2_w, L0_tok_w2_b, L0_tok_q1_w, L0_tok_q1_b, L0_tok_q2_w, L0_tok_q2_b)
    h = jnp.concatenate([jnp.broadcast_to(cls_tok, (h.shape[0], 1, h.shape[2])), h], axis=1)
    h = h + _L0_attn_ref(_layernorm(h, axis=-1), L0_attn_Wq_comp, L0_attn_Wkv_comp, L0_attn_Wqc, L0_attn_Wqr, L0_attn_Wkc, L0_attn_Wkr, L0_attn_Wv)
    h = h + _L0_ffn_ref(_layernorm(h, axis=-1), L0_ffn_attention_mask, L0_ffn_wr, L0_ffn_br, L0_ffn_w1, L0_ffn_b1, L0_ffn_w2, L0_ffn_b2)
    h = h + _L1_attn_ref(_layernorm(h, axis=-1))
    h = h + _L1_ffn_ref(_layernorm(h, axis=-1), L1_ffn_Wq_pk, L1_ffn_pk_keys, L1_ffn_Wq, L1_ffn_keys_table, L1_ffn_values_table, L1_ffn_Wo)
    return h

_drawn_inputs = setup_inputs


def setup_inputs(seed=0):
    import zlib

    import numpy as np

    out = dict(_drawn_inputs(seed))
    spreads = {'L0_tok_p_b': (0.0, 0.1),
     'L0_tok_w1_b': (0.0, 0.1),
     'L0_tok_w2_b': (0.0, 0.1),
     'L0_tok_q1_b': (0.0, 0.1),
     'L0_ffn_b1': (0.0, 0.8),
     'L0_ffn_b2': (0.0, 0.8)}
    factors = {'L0_attn_Wq_comp': 8.0,
     'L0_attn_Wqc': 8.0,
     'L0_attn_Wqr': 8.0,
     'L0_attn_Wkc': 8.0,
     'L0_attn_Wkr': 8.0,
     'L0_ffn_wr': 8.0,
     'L0_ffn_w1': 8.0,
     'L0_ffn_w2': 8.0,
     'L1_ffn_Wq_pk': 25.534,
     'L1_ffn_pk_keys': 26.156,
     'L1_ffn_Wq': 64.0,
     'L1_ffn_keys_table': 64.0,
     'L1_ffn_values_table': 24.763,
     'L1_ffn_Wo': 24.256}
    for name, (base, spread) in spreads.items():
        noise = np.random.default_rng([zlib.crc32(name.encode()), seed]).standard_normal(out[name].shape)
        drawn = base * np.exp(spread * noise) if base else spread * noise
        out[name] = jnp.asarray(drawn.astype(out[name].dtype))
    for name, factor in factors.items():
        out[name] = (out[name] * factor).astype(out[name].dtype)
    return out
```

```python
from contextlib import ExitStack

import numpy as np
import concourse.bass as bass
from concourse import mybir

F32 = mybir.dt.float32
U32 = mybir.dt.uint32
BF16 = mybir.dt.bfloat16
ALU = mybir.AluOpType
ACT = mybir.ActivationFunctionType
AX = mybir.AxisListType

B = 32
S = 64
CH = 32
LAYERS = 4
KY = 12
KX = 24
NQ = 4
T = S + 1
PAIRS = B // 2
CHUNKS = 4
PPC = PAIRS // CHUNKS
BPC = B // CHUNKS
OG = CH // 4
YH = 2
KYP = KY // 2
MODES = KYP * KX
N = BPC * S

CONSTS = {}


def _part(name, array):
    CONSTS[name] = np.asarray(array, np.float64)


def _tables():
    kx = np.array(list(range(KX // 2)) + list(range(S - KX // 2, S)))
    ky = np.arange(KY)
    px = np.arange(S)
    ax = 2 * np.pi * np.outer(kx, px) / S
    ay = 2 * np.pi * np.outer(ky, px) / S
    _part("ident", np.eye(128))
    ixr, ixi = np.zeros((128, 128)), np.zeros((128, 128))
    for b in range(2):
        r, c = slice(24 * b, 24 * b + 24), slice(64 * b, 64 * b + 64)
        ixr[r, c], ixi[r, c] = np.cos(ax), np.sin(ax)
        r = slice(64 + 24 * b, 64 + 24 * b + 24)
        ixr[r, c], ixi[r, c] = -np.sin(ax), np.cos(ax)
    _part("inv_x_re", ixr)
    _part("inv_x_im", ixi)
    w = np.where(ky == 0, 1.0, 2.0)[:, None] / S
    for h in range(YH):
        ys = slice(32 * h, 32 * h + 32)
        inv, fwd = np.zeros((96, 128)), np.zeros((128, 96))
        for o in range(4):
            inv[24 * o:24 * o + 12, 32 * o:32 * o + 32] = (w * np.cos(ay))[:, ys]
            inv[24 * o + 12:24 * o + 24, 32 * o:32 * o + 32] = (-w * np.sin(ay))[:, ys]
            fwd[32 * o:32 * o + 32, 24 * o:24 * o + 12] = np.cos(ay)[:, ys].T / S
            fwd[32 * o:32 * o + 32, 24 * o + 12:24 * o + 24] = -np.sin(ay)[:, ys].T / S
        _part(f"inv_y{h}", inv)
        _part(f"fwd_y{h}", fwd)
    _part("fwd_y_in", np.concatenate([np.cos(ay).T, -np.sin(ay).T], 1) / S)
    cos, sin = np.zeros((128, 64)), np.zeros((128, 64))
    for b in range(2):
        cos[64 * b:64 * b + 64, 32 * b:32 * b + 24] = np.cos(ax).T
        sin[64 * b:64 * b + 64, 32 * b:32 * b + 24] = np.sin(ax).T
    _part("fwd_x_cos", cos)
    _part("fwd_x_sin", sin)
    _part("fwd_x_nsin", -sin)
    _part("eye32", np.tile(np.eye(32), (4, 1)))
    grid = np.linspace(0.0, 1.0, S).astype(np.float32)
    for h in range(YH):
        m = np.zeros((67, 32))
        m[32 * h:32 * h + 32] = np.eye(32)
        m[64:66] = 1.0
        m[66] = grid[32 * h:32 * h + 32]
        _part(f"base{h}", m)
    sign = np.ones((128, 1))
    sign[32:64] = sign[96:128] = -1.0
    _part("sign", sign)
    sel = np.zeros((24, KYP, 2, 2))
    for p in range(KYP):
        for m in range(2):
            for c in range(2):
                sel[12 * c + 2 * p + m, p, m, c] = 1.0
    _part("pick_mode", sel.reshape(24, -1))
    _part("pick_part", np.kron(np.eye(4), np.ones((3, 1))))
    one = np.ones(S)
    fy = np.exp(-1j * ay) / S
    fx = np.exp(-1j * ax)
    gx = np.outer(fx @ grid, fy @ one)
    gy = np.outer(fx @ one, fy @ grid)
    g1 = np.outer(fx @ one, fy @ one)
    k = np.zeros((2, 2, 3, KYP, KX))
    for m in range(2):
        for j, g in enumerate((gx, gy, g1)):
            k[m, 0, j] = g.real[:, m::2].T
            k[m, 1, j] = g.imag[:, m::2].T
    _part("coords_hat", k.reshape(12, -1))


_tables()
COL = {}
_at = 0
for _n, _a in CONSTS.items():
    COL[_n] = (_at, _a.shape[0], _a.shape[1])
    _at += _a.shape[1]
CONST_COLS = _at


def const_table():
    t = np.zeros((128, CONST_COLS), np.float32)
    for n, a in CONSTS.items():
        c, r, w = COL[n]
        t[:r, c:c + w] = a
    return t


def grow(ap, axis, n):
    shape = list(ap.shape)
    return ap.unsqueeze(axis).to_broadcast(shape[:axis] + [n] + shape[axis:])


def wait_for(m, eng, sem, value):
    eng.wait_ge(sem, value)
    if not isinstance(value, int):
        eng.sem_inc(m["waits"], 1)


def spectrum_of_input(nc, io, m):
    with ExitStack() as ctx:
        def sb(name, shape):
            return ctx.enter_context(nc.sbuf_tensor(name, shape, F32))

        def sem(name):
            return ctx.enter_context(nc.semaphore(name))

        cst = m["const"]
        xin = sb("xin", [67, B * S])
        w2raw = sb("w2raw", [CH, LAYERS, CH])
        w2wide = sb("w2wide", [CH, LAYERS, CH, 32])
        q1t = sb("q1t", [CH + 1, NQ])
        lift = sb("lift", [CH + 1, 67])
        b2all = sb("b2all", [CH, LAYERS])
        b2sum = sb("b2sum", [CH, 1])
        head_in = sb("head_in", [67, NQ])
        base = sb("base", [67, YH, NQ, 32])
        lift_x = sb("lift_x", [24, CH])
        lift_c = sb("lift_c", [12, CH])
        pick_x = sb("pick_x", [24, KYP, 4, CH])
        pick_c = sb("pick_c", [12, 4, CH])
        a0 = sb("a0", [24, B * S])
        a0t = sb("a0t", [128, PAIRS, 2, KY])
        x0 = sb("x0", [64, PAIRS, 2, KY])
        x0t = sb("x0t", [24, KX, B])
        bank = [ctx.enter_context(nc.psum_tensor(f"prep_bank{i}", [128, 512], F32)) for i in range(2)]

        loads = sem("small_loads")
        zeroed = sem("mixers_zeroed")
        blocks = sem("mixer_blocks_loaded")
        filled = sem("prep_bank_filled")
        taken = sem("prep_bank_taken")
        made = sem("prep_weights_made")
        SMALL = 11

        HEAD_IN, HEAD_W, SHARE, FWD_Y, TURN_X, FWD_X, TURN_K, SPREAD = 0, 1, 2, 10, 14, 15, 17, 19

        with nc.Block() as block:
            @block.sync
            def _(sp):
                sp.dma_start(cst[:, :], io["const"]).then_inc(loads, 16)
                sp.dma_start(xin[:, :], io["xin"]).then_inc(loads, 16)
                sp.dma_start(lift[:, :], io["lift"]).then_inc(loads, 16)
                sp.dma_start(q1t[:, :], io["q1t"]).then_inc(loads, 16)
                sp.dma_start(w2raw[:, :, :], io["w2"].rearrange("l p o -> p l o")).then_inc(loads, 16)
                sp.dma_start(b2all[:, :], io["b2t"]).then_inc(loads, 16)
                sp.dma_start(lift_x[:, :], io["lift_x"].partition_broadcast(24).rearrange("p a o -> p (a o)")).then_inc(loads, 16)
                sp.dma_start(lift_c[:, :], io["lift_c"]).then_inc(loads, 16)
                sp.dma_start(m["dc1"][:, :], io["b1t"]).then_inc(loads, 16)
                sp.dma_start(m["dc2"][:, :], io["b2t"]).then_inc(loads, 16)
                sp.dma_start(m["q2col"][:, :], io["q2col"]).then_inc(loads, 16)
                sp.wait_ge(zeroed, 1)
                for i in range(4):
                    r = slice(32 * i, 32 * i + 32)
                    sp.dma_start(m["mix1"][r, :, r], io["w1t"].rearrange("l p o -> p l o")).then_inc(blocks, 16)
                    sp.dma_start(m["mix2"][r, :, r], io["w2t"].rearrange("l p o -> p l o")).then_inc(blocks, 16)
                sp.wait_ge(blocks, 16 * 8)
                sp.wait_ge(loads, 16 * SMALL)

            @block.gpsimd
            def _(pool):
                nc.gpsimd.memset(m["mix1"][:, :, :], 0.0)
                nc.gpsimd.memset(m["inv_in"][:, :, :, :], 0.0)
                nc.gpsimd.memset(m["mix2"][:, :, :], 0.0).then_inc(zeroed, 1)

            @block.tensor
            def _(pe):
                pe.wait_ge(loads, 16 * SMALL)
                pe.wait_ge(made, 2)
                pe.matmul(bank[HEAD_IN % 2][0:67, 0:NQ], lift[:, :], q1t[:, :]).then_inc(filled, 1)
                for l in range(LAYERS):
                    for g in range(OG):
                        c = (l * OG + g) * NQ
                        ins = pe.matmul(bank[HEAD_W % 2][:, c:c + NQ], w2wide[:, l, 4 * g:4 * g + 4].rearrange("p o y -> p (o y)"), q1t[0:CH, :])
                ins.then_inc(filled, 1)
                pe.wait_ge(made, 4)
                for h in range(YH):
                    for n in range(4):
                        step = SHARE + 4 * h + n
                        pe.wait_ge(taken, step - 1)
                        pe.matmul(bank[step % 2][:, :], base[:, h].rearrange("p q y -> p (q y)"), xin[:, 512 * n:512 * n + 512])\
                          .then_inc(filled, 1)
                c, r, w = COL["fwd_y_in"]
                for n in range(4):
                    step = FWD_Y + n
                    pe.wait_ge(taken, step - 1)
                    pe.matmul(bank[step % 2][0:24, :], cst[0:64, c:c + w], xin[0:64, 512 * n:512 * n + 512]).then_inc(filled, 1)
                pe.wait_ge(taken, TURN_X)
                for q in range(PAIRS):
                    ins = pe.transpose(bank[TURN_X % 2][:, 24 * q:24 * q + 24], a0[:, 128 * q:128 * q + 128], cst[0:24, 0:24])
                ins.then_inc(filled, 1)
                pe.wait_ge(taken, FWD_X)
                for part, names in enumerate(((("fwd_x_cos", 0), ("fwd_x_sin", 1)), (("fwd_x_cos", 1), ("fwd_x_nsin", 0)))):
                    for i, (name, src) in enumerate(names):
                        k = COL[name][0]
                        ins = pe.matmul(bank[(FWD_X + part) % 2][0:64, 0:PAIRS * KY], cst[:, k:k + 64], a0t[:, :, src, :],
                                        start=(i == 0), stop=(i == 1))
                    ins.then_inc(filled, 1)
                pe.wait_ge(taken, TURN_K)
                for half in range(2):
                    for q in range(8):
                        ins = pe.transpose(bank[(TURN_K + half) % 2][0:24, 64 * q:64 * q + 64],
                                           x0[0:64, 8 * half + q].rearrange("p c k -> p (c k)"), cst[0:64, 0:64])
                    ins.then_inc(filled, 1)
                pe.wait_ge(taken, SPREAD)
                k = COL["coords_hat"][0]
                for y in range(KYP):
                    for half in range(2):
                        step = SPREAD + 2 * y + half
                        pe.wait_ge(taken, step - 1)
                        pe.matmul(bank[step % 2][:, 0:384], pick_x[:, y].rearrange("p a o -> p (a o)"),
                                  x0t[:, 12 * half:12 * half + 12, :].rearrange("p k b -> p (k b)"), start=True, stop=False)
                        kk = k + y * KX + 12 * half
                        pe.matmul(bank[step % 2][:, 0:384], pick_c[:, :, :].rearrange("p a o -> p (a o)"),
                                  grow(cst[0:12, kk:kk + 12], 2, B), start=False, stop=True).then_inc(filled, 1)

            @block.vector
            def _(dve):
                dve.wait_ge(loads, 16 * SMALL)
                dve.tensor_reduce(b2sum[:, :], b2all[:, :], AX.X, ALU.add).then_inc(made, 1)
                dve.wait_ge(made, 1)
                dve.tensor_copy(w2wide[:, :, :, :].rearrange("p l o y -> p (l o) y"),
                                grow(w2raw[:, :, :].rearrange("p l o -> p (l o)"), 2, 32))
                dve.tensor_tensor(lift[0:CH, 65:66], lift[0:CH, 65:66], b2sum[:, :], ALU.add).then_inc(made, 1)
                dve.wait_ge(filled, HEAD_IN + 1)
                dve.tensor_copy(head_in[:, :], bank[HEAD_IN % 2][0:67, 0:NQ]).then_inc(taken, 1)
                dve.wait_ge(taken, 1)
                for h in range(YH):
                    c = COL[f"base{h}"][0]
                    ins = dve.tensor_tensor(base[:, h], grow(cst[0:67, c:c + 32], 1, NQ), grow(head_in[:, :], 2, 32), ALU.mult)
                ins.then_inc(made, 1)
                c = COL["pick_mode"][0]
                dve.tensor_tensor(pick_x[:, :, :, :].rearrange("p y a o -> p (y a) o"),
                                  grow(cst[0:24, c:c + 24], 2, CH), grow(lift_x[:, :], 1, 24), ALU.mult)
                c = COL["pick_part"][0]
                dve.tensor_tensor(pick_c[:, :, :], grow(cst[0:12, c:c + 4], 2, CH), grow(lift_c[:, :], 1, 4), ALU.mult).then_inc(made, 1)
                dve.wait_ge(filled, HEAD_W + 1)
                dve.tensor_copy(m["head_w"][:, :, :], bank[HEAD_W % 2][:, 0:128].rearrange("p (l c) -> p l c", l=LAYERS)).then_inc(taken, 1)
                for h in range(YH):
                    for n in range(4):
                        step = SHARE + 4 * h + n
                        dve.wait_ge(filled, step + 1)
                        dve.tensor_copy(m["qacc"][:, h, 512 * n:512 * n + 512], bank[step % 2][:, :]).then_inc(taken, 1)
                for n in range(4):
                    step = FWD_Y + n
                    dve.wait_ge(filled, step + 1)
                    dve.tensor_copy(a0[:, 512 * n:512 * n + 512], bank[step % 2][0:24, :]).then_inc(taken, 1)
                dve.wait_ge(filled, TURN_X + 1)
                dve.tensor_copy(a0t[:, :, :, :].rearrange("p q c k -> p (q c k)"), bank[TURN_X % 2][:, 0:384]).then_inc(taken, 1)
                for part in range(2):
                    dve.wait_ge(filled, FWD_X + part + 1)
                    dve.tensor_copy(x0[:, :, part, :], bank[(FWD_X + part) % 2][0:64, 0:PAIRS * KY].rearrange("p (q k) -> p q k", k=KY))\
                       .then_inc(taken, 1)
                for half in range(2):
                    dve.wait_ge(filled, TURN_K + half + 1)
                    dve.tensor_copy(x0t[:, :, 16 * half:16 * half + 16],
                                    bank[(TURN_K + half) % 2][0:24, :].rearrange("p (b k) -> p k b", k=32)[:, 0:KX]).then_inc(taken, 1)
                for y in range(KYP):
                    for half in range(2):
                        step = SPREAD + 2 * y + half
                        dve.wait_ge(filled, step + 1)
                        dve.tensor_copy(m["spec"][:, y, 12 * half:12 * half + 12, :].rearrange("p k b -> p (k b)"), bank[step % 2][:, 0:384])\
                           .then_inc(taken, 1)


BLOCKS = 12
BM = MODES // BLOCKS
BN = BM * B
PLAN_MIX, PLAN_TURN = 2 * BLOCKS, 2 * PAIRS
HEADPART = PLAN_MIX + BLOCKS + PLAN_TURN
FULL, SHORT = 48, 32
TAIL = BLOCKS
ITEMS = HEADPART + CHUNKS * FULL + TAIL
ACT_ITEMS = (HEADPART + 1) // 2 + CHUNKS * FULL // 2
DVE_ITEMS = ITEMS - ACT_ITEMS


def by_act(j):
    return j // 2 + 1


def by_dve(j):
    return (j + 1) // 2


def fourier_layers(nc, io, m):
    with ExitStack() as ctx:
        def sb(name, shape):
            return ctx.enter_context(nc.sbuf_tensor(name, shape, F32))

        def sem(name):
            return ctx.enter_context(nc.semaphore(name))

        cst, spec, inv_in, qacc = m["const"], m["spec"], m["inv_in"], m["qacc"]
        mixw = sb("mixw", [128, MODES, 2, CH])
        g = sb("mixed", [128, MODES * B])
        g2 = sb("mixed_w1", [128, MODES * B])
        z = sb("z", [128, PPC, CH, 2, KY])
        zt = sb("zt", [96, OG, N])
        act_y = g2[0:96, 0:OG * N].rearrange("p (g n) -> p g n", g=OG)
        r = sb("relu", [128, 4, N])
        at = sb("act_t", [128, PPC, OG * 4, 2, KY])
        fx = sb("act_x", [128, 2, KY, 2, CH])
        w1 = sb("w1_now", [128, 128])
        w2 = sb("w2_now", [128, 128])
        hw = sb("head_now", [128, OG * NQ, 32])
        dc = sb("dc_now", [CH, 2])
        bank = [ctx.enter_context(nc.psum_tensor(f"bank{i}", [128, 512], F32)) for i in range(8)]
        qb, yb, ring = bank[0:2], bank[2:4], bank[4:8]

        weights_in = sem("mix_weights_loaded")
        signed = sem("mix_weights_signed")
        ready = sem("layer_weights_ready")
        full = sem("ring_filled")
        ta = sem("ring_taken_by_act")
        td = sem("ring_taken_by_dve")
        dc_in = sem("dc_bias_added")
        y_full = sem("fwd_y_filled")
        ya = sem("fwd_y_taken_by_act")
        yd = sem("fwd_y_taken_by_dve")
        q_full = sem("head_filled")
        q_in = sem("head_added")

        gv = g2[:, :].rearrange("p (k b x) -> p k b x", k=KYP, b=B)
        ft = g[:, :].rearrange("p (k x b) -> p k x b", k=KYP, b=B)
        specf = spec[:, :, :, :].rearrange("p k x b -> p (k x b)")
        mixf = mixw[:, :, :, :].rearrange("p m c o -> p m (c o)")

        def C(name, rows=128):
            c, _, w = COL[name]
            return cst[0:rows, c:c + w]

        def bases(l):
            return l * ITEMS, l * ACT_ITEMS + 1, l * DVE_ITEMS + 1

        def chunk_bases(l, ch, size):
            f, a, d = bases(l)
            return f + HEADPART + ch * size, a + by_act(HEADPART - 1) + ch * (size // 2), d + by_dve(HEADPART - 1) + ch * (size // 2)

        def pe_layer(pe, l, last):
            f, a, d = bases(l)

            def taken(j, a=a, d=d):
                wait_for(m, pe, ta, a + by_act(j))
                if j > 0:
                    wait_for(m, pe, td, d + by_dve(j))

            def slot(j, a=a, d=d):
                if j < 4:
                    if j == 0:
                        wait_for(m, pe, ta, a)
                        wait_for(m, pe, td, d)
                elif j % 2 == 0:
                    wait_for(m, pe, ta, a + by_act(j - 4))
                else:
                    wait_for(m, pe, td, d + by_dve(j - 4))

            wait_for(m, pe, signed, l + 1)
            wait_for(m, pe, ready, l + 1)
            j = 0
            for blk in range(BLOCKS):
                for mem in range(2):
                    slot(j)
                    rows = slice(64 * mem, 64 * mem + 64)
                    for i in range(BM):
                        mode = BM * blk + i
                        ins = pe.matmul(ring[j % 4][rows, B * i:B * i + B], mixf[rows, mode], specf[rows, B * mode:B * mode + B])
                    ins.then_inc(full, 1)
                    j += 1
            ins = None
            for blk in range(BLOCKS):
                slot(j)
                taken(2 * blk + 1)
                ins = pe.matmul(ring[j % 4][:, 0:BN], w1[:, :], g[:, BN * blk:BN * blk + BN])
                ins.then_inc(full, 1)
                j += 1
            taken(j - 1)
            wait_for(m, pe, dc_in, 2 * l + 2)
            for p in range(PAIRS):
                for half in range(2):
                    slot(j)
                    for i in range(3):
                        ins = pe.transpose(ring[j % 4][0:48, 128 * i:128 * i + 128],
                                           gv[:, 3 * half + i, 2 * p:2 * p + 2, :].rearrange("p b x -> p (b x)"), C("ident"))
                    ins.then_inc(full, 1)
                    j += 1
            assert j == HEADPART
            size = SHORT if last else FULL
            with pe.Fori(0, CHUNKS) as ch:
                pe_chunk(pe, l, ch, last, size)
            if last:
                return
            fc, ac, dcount = chunk_bases(l, CHUNKS, size)
            wait_for(m, pe, ta, ac)
            wait_for(m, pe, td, dcount)
            for blk in range(TAIL):
                if blk >= 4:
                    wait_for(m, pe, td, dcount + blk - 3)
                pe.matmul(ring[blk % 4][:, 0:BN], w2[:, :], g[:, BN * blk:BN * blk + BN]).then_inc(full, 1)

        def pe_chunk(pe, l, ch, last, size):
            f, a, d = chunk_bases(l, ch, size)
            n = l * CHUNKS + ch

            def taken(j):
                wait_for(m, pe, ta, a + by_act(j))
                if j > 0:
                    wait_for(m, pe, td, d + by_dve(j))

            def slot(j):
                if j == 0:
                    wait_for(m, pe, ta, a)
                    wait_for(m, pe, td, d)
                elif j >= 4 and j % 2 == 0:
                    wait_for(m, pe, ta, a + by_act(j - 4))
                elif j >= 4:
                    wait_for(m, pe, td, d + by_dve(j - 4))

            def b(j):
                return ring[j % 4]

            j = 0
            for p in range(PPC):
                rhs = inv_in[0:112, bass.ds(ch * PPC + p, 1)].rearrange("p a k o -> p (a k o)")
                for c in range(2):
                    slot(j)
                    pe.matmul(b(j)[:, 0:384], C("inv_x_im" if c else "inv_x_re", 112), rhs).then_inc(full, 1)
                    j += 1
            taken(j - 1)
            for og in range(OG):
                slot(j)
                for p in range(PPC):
                    ins = pe.transpose(b(j)[0:96, 128 * p:128 * p + 128],
                                       z[:, p, 4 * og:4 * og + 4].rearrange("p o c k -> p (o c k)"), C("ident"))
                ins.then_inc(full, 1)
                j += 1
            first = j

            def inv_y(k):
                slot(first + k)
                if k % 2 == 0:
                    taken(8 + k // 2)
                pe.matmul(b(first + k)[:, :], C(f"inv_y{k % 2}", 96), zt[:, k // 2]).then_inc(full, 1)

            wait_for(m, pe, q_in, 2 * n + 1)
            inv_y(0)
            inv_y(1)
            for k in range(2 * OG):
                if k + 2 < 2 * OG:
                    inv_y(k + 2)
                og, h = k // 2, k % 2
                taken(first + k)
                ins = pe.matmul(qb[h][:, :], hw[:, NQ * og:NQ * og + NQ].rearrange("p q y -> p (q y)"), r[:, k % 4],
                                start=(og == 0), stop=(og == OG - 1))
                if og == OG - 1:
                    ins.then_inc(q_full, 1)
                if not last:
                    if h == 0 and og >= 2:
                        wait_for(m, pe, ya if og % 2 == 0 else yd, (l * CHUNKS + ch) * 4 + og // 2)
                    ins = pe.matmul(yb[og % 2][0:96, :], C(f"fwd_y{h}"), r[:, k % 4], start=(h == 0), stop=(h == 1))
                    if h == 1:
                        ins.then_inc(y_full, 1)
            j = first + 2 * OG
            if last:
                return
            wait_for(m, pe, ya, n * 4 + 4)
            wait_for(m, pe, yd, n * 4 + 4)
            for p in range(PPC):
                for half in range(2):
                    slot(j)
                    for i in range(4):
                        ins = pe.transpose(b(j)[:, 96 * i:96 * i + 96], act_y[:, 4 * half + i, 128 * p:128 * p + 128],
                                           C("ident")[0:96, 0:96])
                    ins.then_inc(full, 1)
                    j += 1
            for pp in range(2):
                taken(24 + 8 + 4 * pp + 3)
                for c in range(2):
                    slot(j)
                    names = ("fwd_x_cos", "fwd_x_sin") if c == 0 else ("fwd_x_nsin", "fwd_x_cos")
                    for mem in range(2):
                        for src in range(2):
                            ins = pe.matmul(b(j)[64 * mem:64 * mem + 64, 0:384], C(names[src]),
                                            at[:, 2 * pp + mem, :, src, :], start=(src == 0), stop=(src == 1))
                    ins.then_inc(full, 1)
                    j += 1
            for pp in range(2):
                taken(40 + 2 * pp + 1)
                for half in range(2):
                    slot(j)
                    for i in range(3):
                        k = 2 * (3 * half + i)
                        ins = pe.transpose(b(j)[:, 128 * i:128 * i + 128],
                                           fx[:, pp, k:k + 2].rearrange("p k c o -> p (k c o)"), C("ident"))
                    ins.then_inc(full, 1)
                    j += 1
            assert j == FULL

        def take_layer(e, copy, relu, me, l, last):
            done = (ta, td)[me]
            f, a, d = bases(l)

            def item(j, steps, f=f):
                if j % 2 != me:
                    return
                e.wait_ge(full, f + j + 1)
                for s in steps[:-1]:
                    s()
                steps[-1]().then_inc(done, 1)

            j = 0
            for blk in range(BLOCKS):
                for mem in range(2):
                    rows = slice(64 * mem, 64 * mem + 64)
                    item(j, [lambda j=j, rows=rows, blk=blk: copy(g[rows, BN * blk:BN * blk + BN], ring[j % 4][rows, 0:BN])])
                    j += 1
            for blk in range(BLOCKS):
                item(j, [lambda j=j, blk=blk: copy(
                    gv[:, blk // 2, :, BM * (blk % 2):BM * (blk % 2) + BM].rearrange("p b x -> p x b"),
                    ring[j % 4][:, 0:BN].rearrange("p (x b) -> p x b", b=B))])
                if blk == 0 and me == 1:
                    e.wait_ge(ta, a + by_act(j))
                    e.wait_ge(ready, l + 1)
                    e.tensor_scalar(gv[0:CH, 0, :, 0], gv[0:CH, 0, :, 0], dc[:, 0:1], None, ALU.add).then_inc(dc_in, 1)
                j += 1
            for p in range(PAIRS):
                for half in range(2):
                    steps = []
                    for c in range(2):
                        steps.append(lambda j=j, c=c, p=p, half=half: copy(
                            inv_in[64 * c:64 * c + 48, p, 6 * half:6 * half + 6, :],
                            ring[j % 4][0:48, 0:384].rearrange("p (k c o) -> p k c o", c=2, o=CH)[:, :, c, :]))
                    item(j, steps)
                    j += 1
            size = SHORT if last else FULL
            with e.Fori(0, CHUNKS) as ch:
                take_chunk(e, copy, relu, me, l, ch, last, size)
            if last or me == 0:
                return
            fc, ac, dcount = chunk_bases(l, CHUNKS, size)
            for blk in range(TAIL):
                e.wait_ge(full, fc + blk + 1)
                e.tensor_tensor(specf[:, BN * blk:BN * blk + BN], ring[blk % 4][:, 0:BN],
                                specf[:, BN * blk:BN * blk + BN], ALU.add).then_inc(td, 1)
            e.wait_ge(td, dcount + 1)
            e.tensor_scalar(specf[0:CH, 0:B], specf[0:CH, 0:B], dc[:, 1:2], None, ALU.add).then_inc(dc_in, 1)

        def take_chunk(e, copy, relu, me, l, ch, last, size):
            f, a, d = chunk_bases(l, ch, size)
            done = (ta, td)[me]
            n = l * CHUNKS + ch

            def b(j):
                return ring[j % 4]

            def item(j, step):
                if j % 2 != me:
                    return
                e.wait_ge(full, f + j + 1)
                step().then_inc(done, 1)

            j = 0
            for p in range(PPC):
                for c in range(2):
                    item(j, lambda: copy(z[:, p, :, c, :].rearrange("p o k -> p k o"),
                                         b(j)[:, 0:384].rearrange("p (k o) -> p k o", o=CH)))
                    j += 1
            for og in range(OG):
                item(j, lambda: copy(zt[:, og], b(j)[0:96, :]))
                j += 1

            def take_y(og):
                if last or og % 2 != me:
                    return
                e.wait_ge(y_full, n * OG + og + 1)
                copy(act_y[:, og], yb[og % 2][0:96, :]).then_inc((ya, yd)[me], 1)

            for k in range(2 * OG):
                item(j, lambda: relu(r[:, k % 4], b(j)[:, :]))
                j += 1
                if k % 2 == 1 and k >= 3:
                    take_y(k // 2 - 1)
            take_y(OG - 1)
            if me == 1:
                for h in range(2):
                    e.wait_ge(q_full, 2 * n + h + 1)
                    e.tensor_tensor(qacc[:, h, bass.ds(ch * N, N)], qb[h][:, :], qacc[:, h, bass.ds(ch * N, N)],
                                    ALU.add).then_inc(q_in, 1)
            if last:
                return
            for p in range(PPC):
                for half in range(2):
                    item(j, lambda: copy(at[:, p, 16 * half:16 * half + 16].rearrange("p o c k -> p (o c k)"), b(j)[:, 0:384]))
                    j += 1
            for pp in range(2):
                for c in range(2):
                    item(j, lambda: copy(fx[:, pp, :, c, :].rearrange("p k o -> p o k"),
                                         b(j)[:, 0:384].rearrange("p (o k) -> p o k", k=KY)))
                    j += 1
            for pp in range(2):
                for half in range(2):
                    item(j, lambda: copy(
                        ft[:, 3 * half:3 * half + 3, :, bass.ds(ch * BPC + 4 * pp, 4)].rearrange("p k x b -> p k b x"),
                        b(j)[:, 0:384].rearrange("p (k b x) -> p k b x", k=3, b=4)[:, :, :, 0:KX]))
                    j += 1

        with nc.Block() as block:
            def load(sp, l):
                src = io["mixw"][bass.ds(l, 1)].rearrange("l p m -> p (l m)")
                sp.dma_start(mixw[:, :, :, :].rearrange("p m c o -> p (m c o)"), src).then_inc(weights_in, 16)

            @block.sync
            def _(sp):
                load(sp, 0)
                with sp.Fori(1, LAYERS) as l:
                    sp.wait_ge(full, (l - 1) * ITEMS + PLAN_MIX)
                    load(sp, l)

            @block.gpsimd
            def _(pool):
                with pool.Fori(0, LAYERS) as l:
                    wait_for(m, pool, weights_in, 16 * l + 16)
                    pool.tensor_scalar(mixw[:, :, 0, :], mixw[:, :, 0, :], C("sign")[:, 0:1], None, ALU.mult).then_inc(signed, 1)

            @block.tensor
            def _(pe):
                with pe.Fori(0, LAYERS - 1) as l:
                    pe_layer(pe, l, False)
                pe_layer(pe, LAYERS - 1, True)

            @block.scalar
            def _(act):
                def copy(o, i):
                    return act.activation(o, i, ACT.Copy)

                def relu(o, i):
                    return act.activation(o, i, ACT.Relu)

                act.sem_inc(ta, 1)
                with act.Fori(0, LAYERS - 1) as l:
                    take_layer(act, copy, relu, 0, l, False)
                take_layer(act, copy, relu, 0, LAYERS - 1, True)

            @block.vector
            def _(dve):
                def relu(o, i):
                    return dve.tensor_scalar(o, i, 0.0, None, ALU.max)

                def small_weights(l):
                    at_l = bass.ds(l, 1)
                    dve.wait_ge(dc_in, 2 * l + 1)
                    dve.tensor_copy(w1[:, :], m["mix1"][:, at_l, :].rearrange("p l o -> p (l o)"))
                    dve.tensor_copy(w2[:, :], m["mix2"][:, at_l, :].rearrange("p l o -> p (l o)"))
                    dve.tensor_scalar(dc[:, 0:1], m["dc1"][:, at_l], float(S), None, ALU.mult)
                    dve.tensor_scalar(dc[:, 1:2], m["dc2"][:, at_l], float(S), None, ALU.mult)
                    dve.tensor_tensor(hw[:, :, :], grow(C("eye32"), 1, OG * NQ),
                                      grow(m["head_w"][:, at_l, :].rearrange("p l c -> p (l c)"), 2, 32), ALU.mult).then_inc(ready, 1)

                for start_at_one in (td, dc_in, q_in):
                    dve.sem_inc(start_at_one, 1)
                with dve.Fori(0, LAYERS - 1) as l:
                    small_weights(l)
                    take_layer(dve, dve.tensor_copy, relu, 1, l, False)
                small_weights(LAYERS - 1)
                take_layer(dve, dve.tensor_copy, relu, 1, LAYERS - 1, True)


def tower_head(nc, io, m):
    with ExitStack() as ctx:
        h, qacc = m["h"], m["qacc"]
        wq = ctx.enter_context(nc.sbuf_tensor("head_out_w", [128, 32], F32))
        q2b = ctx.enter_context(nc.sbuf_tensor("q2b", [S, 1], F32))
        bank = [ctx.enter_context(nc.psum_tensor(f"tok{i}", [128, 512], F32)) for i in range(4)]
        loads = ctx.enter_context(nc.semaphore("head_loads"))
        wready = ctx.enter_context(nc.semaphore("head_w_ready"))
        relued = ctx.enter_context(nc.semaphore("head_relued"))
        full = ctx.enter_context(nc.semaphore("tok_filled"))
        taken = ctx.enter_context(nc.semaphore("tok_taken"))
        with nc.Block() as block:
            @block.sync
            def _(sp):
                sp.dma_start(q2b[:, :], io["q2b"].partition_broadcast(S).rearrange("p a b -> p (a b)")).then_inc(loads, 16)
                sp.dma_start(h[S:T, :, :], grow(io["cls"], 1, B)).then_inc(loads, 16)
                sp.wait_ge(loads, 32)

            @block.vector
            def _(dve):
                c = COL["eye32"][0]
                dve.tensor_scalar(wq[:, :], m["const"][:, c:c + 32], m["q2col"][:, 0:1], None, ALU.mult).then_inc(wready, 1)
                for i in range(4):
                    cols = slice(512 * i, 512 * i + 512)
                    dve.tensor_scalar(qacc[:, :, cols], qacc[:, :, cols], 0.0, None, ALU.max).then_inc(relued, 1)
                dve.wait_ge(loads, 32)
                for i in range(4):
                    dve.wait_ge(full, i + 1)
                    dve.tensor_scalar(h[0:S, 8 * i:8 * i + 8, :].rearrange("p b y -> p (b y)"), bank[i][0:S, :], q2b[:, 0:1], None,
                                      ALU.add).then_inc(taken, 1)

            @block.tensor
            def _(pe):
                pe.wait_ge(wready, 1)
                for i in range(4):
                    pe.wait_ge(relued, i + 1)
                    for b in range(8):
                        for yh in range(2):
                            c = 64 * (8 * i + b)
                            ins = pe.matmul(bank[i][0:S, 64 * b + 32 * yh:64 * b + 32 * yh + 32], qacc[:, yh, c:c + 64], wq[:, :])
                    ins.then_inc(full, 1)


TOK = B * T
GB = 7
GROUPS = [(b, min(GB, B - b)) for b in range(0, B, GB)]
NG = len(GROUPS)
VB = 512 // S
EPS = 1e-5
TINY = 1e-24
NEG = -1e30
KK = T // 2 - 1
HID = 256
TOKC = {}


def _token_tables():
    pos = np.concatenate([np.arange(1, T), [0]])
    TOKC["ident"] = np.eye(128)
    TOKC["causal"] = np.where(pos[None, :] <= pos[:, None], 0.0, NEG)
    TOKC["before"] = (pos[None, :] < pos[:, None]) * 1.0
    half = 8
    theta = (1.0 / 10000.0 ** (np.arange(half, dtype=np.float32) / half)).astype(np.float32)
    ang = np.outer(theta, pos.astype(np.float32)).astype(np.float32).astype(np.float64)
    cos, sin = np.ones((64, T)), np.zeros((64, T))
    cos[48:] = np.repeat(np.cos(ang), 2, 0)
    sin[48:] = np.repeat(np.sin(ang), 2, 0) * np.tile([[-1.0], [1.0]], (half, 1))
    TOKC["rope_cos"] = np.tile(cos, (2, 1))
    TOKC["rope_sin"] = np.tile(sin, (2, 1))


_token_tables()
TCOL = {}
_at = 0
for _n, _a in TOKC.items():
    TCOL[_n] = (_at, _a.shape[0], _a.shape[1])
    _at += _a.shape[1]
TOKC_COLS = _at


def token_table():
    t = np.zeros((128, TOKC_COLS), np.float32)
    for n, a in TOKC.items():
        c, r, w = TCOL[n]
        t[:r, c:c + w] = a
    return t


def tc(m, name, rows=None):
    c, r, w = TCOL[name]
    return m["tok_const"][0:rows or r, c:c + w]


class Chain:

    def __init__(self, eng, sem, base=0, m=None):
        self.eng, self.sem, self.base, self.n, self.m = eng, sem, base, 0, m

    def __call__(self, ins):
        self.n += 1
        ins.then_inc(self.sem, 1)
        self.eng.wait_ge(self.sem, self.base + self.n)
        if self.m:
            self.eng.sem_inc(self.m["waits"], 1)


def norm_sems(ctx, nc, name):
    return {k: ctx.enter_context(nc.semaphore(f"{name}_{k}")) for k in ("input", "squared", "spread", "rooted", "done", "chain")}


def norm_vector(dve, n, k, link, x, y, sq, s, centre=True):
    mean, v, root, rec, tmp = (s[:, 32 * i:32 * i + 32] for i in range(5))
    if centre:
        link(dve.tensor_reduce(mean, x, AX.X, ALU.add))
        link(dve.tensor_scalar(mean, mean, 1.0 / S, None, ALU.mult))
        dve.tensor_tensor(y, x, grow(mean, 2, S), ALU.subtract).then_inc(n["input"], 1)
    dve.wait_ge(n["squared"], k)
    link(dve.tensor_reduce(v, sq, AX.X, ALU.add))
    if centre:
        dve.tensor_scalar(v, v, 1.0 / S, EPS, ALU.mult, ALU.add).then_inc(n["spread"], 1)
    else:
        dve.tensor_scalar(v, v, TINY, None, ALU.max).then_inc(n["spread"], 1)
    dve.wait_ge(n["rooted"], k)
    link(dve.reciprocal(rec, root))
    link(dve.tensor_tensor(tmp, v, rec, ALU.mult))
    link(dve.tensor_tensor(tmp, tmp, root, ALU.add))
    link(dve.tensor_scalar(tmp, tmp, 0.5, None, ALU.mult))
    link(dve.reciprocal(rec, tmp))
    dve.tensor_tensor(y, y if centre else x, grow(rec, 2, S), ALU.mult).then_inc(n["done"], 1)
    dve.wait_ge(n["done"], k)


def norm_scalar(act, n, k, y, sq, s):
    act.wait_ge(n["input"], k)
    act.activation(sq, y, ACT.Square).then_inc(n["squared"], 1)
    act.wait_ge(n["spread"], k)
    act.activation(s[:, 64:96], s[:, 32:64], ACT.Sqrt).then_inc(n["rooted"], 1)


def turn_tokens(pe, ident, x, bank, full, n=0):
    for g, (b0, nb) in enumerate(GROUPS):
        for i in range(nb):
            ins = pe.transpose(bank[g][0:S, T * i:T * i + T], x[:, b0 + i, :], ident[0:T, 0:T])
        ins.then_inc(full, 1)


def take_turned(act, xt, bank, full, taken):
    for g, (b0, nb) in enumerate(GROUPS):
        act.wait_ge(full, g + 1)
        act.activation(xt[:, T * b0:T * (b0 + nb)], bank[g][0:S, 0:T * nb], ACT.Copy).then_inc(taken, 1)


def attend_sems(ctx, nc, name):
    names = ("scores_full", "scores_taken", "maxed", "shifted", "exped", "summed", "inverted", "probs",
             "turned_full", "turned_taken", "out_full", "out_taken")
    return {k: ctx.enter_context(nc.semaphore(f"{name}_{k}")) for k in names}


def attend_tensor(pe, a, k, ident, qt, kt, v, probs, probs_t, bank):
    pe.wait_ge(a["out_taken"], 4 * k)
    for g, (b0, nb) in enumerate(GROUPS):
        for i in range(nb):
            ins = pe.matmul(bank[g][0:T, T * i:T * i + T], qt(b0 + i), kt(b0 + i))
        ins.then_inc(a["scores_full"], 1)
    pe.wait_ge(a["probs"], k + 1)
    for g, (b0, nb) in enumerate(GROUPS):
        for i in range(nb):
            ins = pe.transpose(bank[g][0:T, T * i:T * i + T], probs[:, b0 + i, :], ident[0:T, 0:T])
        ins.then_inc(a["turned_full"], 1)
    pe.wait_ge(a["turned_taken"], NG * k + NG)
    for g in range(B // VB):
        for i in range(VB):
            b = VB * g + i
            ins = pe.matmul(bank[(5, 6, 7, 0)[g]][0:T, S * i:S * i + S], probs_t[:, b, :], v(b))
        ins.then_inc(a["out_full"], 1)


def attend_vector(dve, a, k, m, scale, h, probs, s, bank):
    mx, z = s[:, 0:32], s[:, 32:64]
    for g, (b0, nb) in enumerate(GROUPS):
        dve.wait_ge(a["scores_full"], NG * k + g + 1)
        dve.scalar_tensor_tensor(out=probs[:, b0:b0 + nb, :], in0=bank[g][0:T, 0:T * nb].rearrange("p (b t) -> p b t", t=T),
                                 scalar=scale, in1=grow(tc(m, "causal"), 1, nb), op0=ALU.mult, op1=ALU.add)\
           .then_inc(a["scores_taken"], 1)
    dve.wait_ge(a["scores_taken"], NG * k + NG)
    dve.tensor_reduce(mx, probs, AX.X, ALU.max).then_inc(a["maxed"], 1)
    dve.wait_ge(a["maxed"], k + 1)
    dve.tensor_tensor(probs, probs, grow(mx, 2, T), ALU.subtract).then_inc(a["shifted"], 1)
    dve.wait_ge(a["exped"], k + 1)
    dve.tensor_reduce(z, probs, AX.X, ALU.add).then_inc(a["summed"], 1)
    dve.wait_ge(a["summed"], k + 1)
    dve.reciprocal(z, z).then_inc(a["inverted"], 1)
    dve.wait_ge(a["inverted"], k + 1)
    dve.tensor_tensor(probs, probs, grow(z, 2, T), ALU.mult).then_inc(a["probs"], 1)
    for g in range(B // VB):
        dve.wait_ge(a["out_full"], B // VB * k + g + 1)
        dve.tensor_tensor(h[:, VB * g:VB * g + VB, :].rearrange("p b d -> p (b d)"), bank[(5, 6, 7, 0)[g]][0:T, :],
                          h[:, VB * g:VB * g + VB, :].rearrange("p b d -> p (b d)"), ALU.add).then_inc(a["out_taken"], 1)
    dve.wait_ge(a["out_taken"], B // VB * k + B // VB)


def attend_scalar(act, a, k, probs, probs_t, bank):
    act.wait_ge(a["shifted"], k + 1)
    act.activation(probs[:, :, :], probs[:, :, :], ACT.Exp).then_inc(a["exped"], 1)
    for g, (b0, nb) in enumerate(GROUPS):
        act.wait_ge(a["turned_full"], NG * k + g + 1)
        act.activation(probs_t[:, b0:b0 + nb, :].rearrange("p b t -> p (b t)"), bank[g][0:T, 0:T * nb], ACT.Copy)\
           .then_inc(a["turned_taken"], 1)


def latent_attention(nc, io, m):
    with ExitStack() as ctx:
        def sb(name, shape):
            return ctx.enter_context(nc.sbuf_tensor("la_" + name, shape, F32))

        def sem(name):
            return ctx.enter_context(nc.semaphore("la_" + name))

        h, xn, sq, s, xt, probs, probs_t = (m[k] for k in ("h", "xn", "sq", "stats", "xt", "probs", "probs_t"))
        wdown = sb("wdown", [S, 2, S])
        wup = sb("wup", [S, 320])
        wq = sb("wq", [S, 320])
        qt, kt = sb("qt", [S, TOK]), sb("kt", [S, TOK])
        v = sb("v", [T, B, S])
        rot = sb("rot", [128, 2, GB * T])
        bank = [ctx.enter_context(nc.psum_tensor(f"la_bank{i}", [128, 512], F32)) for i in range(8)]
        loads, wfull, wtaken, tfull, ttaken = sem("loads"), sem("wfull"), sem("wtaken"), sem("tfull"), sem("ttaken")
        qfull, qrot, qtaken, vfull, vtaken, halves = sem("qfull"), sem("qrot"), sem("qtaken"), sem("vfull"), sem("vtaken"), sem("halves")
        n = norm_sems(ctx, nc, "la_norm")
        a = attend_sems(ctx, nc, "la")
        ident = tc(m, "ident")

        with nc.Block() as block:
            @block.sync
            def _(sp):
                sp.dma_start(m["tok_const"][:, :], io["tok_const"]).then_inc(loads, 16)
                sp.dma_start(wdown[:, :, :], io["la_down"]).then_inc(loads, 16)
                sp.dma_start(wup[:, :], io["la_up"]).then_inc(loads, 16)
                sp.wait_ge(loads, 48)

            @block.tensor
            def _(pe):
                pe.wait_ge(loads, 48)
                pe.matmul(bank[7][0:S, 0:128], wdown[:, 0, :], wup[:, 0:128])
                pe.matmul(bank[7][0:S, 128:320], wdown[:, 1, :], wup[:, 128:320]).then_inc(wfull, 1)
                pe.wait_ge(n["done"], 1)
                turn_tokens(pe, ident, xn, bank, tfull)
                pe.wait_ge(wtaken, 1)
                for g, (b0, nb) in enumerate(GROUPS):
                    c = slice(T * b0, T * (b0 + nb))
                    if g == 0:
                        pe.wait_ge(ttaken, NG)
                    p = 2 * (g % 2)
                    if g >= 2:
                        pe.wait_ge(halves, g - 1)
                    for w in range(2):
                        ins = pe.matmul(bank[p + w][:, 0:T * nb], wq[:, 128 * w:128 * w + 128], xt[:, c])
                    ins.then_inc(qfull, 1)
                for g in range(B // VB):
                    if g == 1:
                        pe.wait_ge(halves, NG)
                    for i in range(VB):
                        b = VB * g + i
                        ins = pe.matmul(bank[4 + g][0:T, S * i:S * i + S], xt[:, T * b:T * b + T], wq[:, 256:320])
                    ins.then_inc(vfull, 1)
                pe.wait_ge(vtaken, B // VB)
                pe.wait_ge(qtaken, 2 * NG)
                attend_tensor(pe, a, 0, ident, lambda b: qt[:, T * b:T * b + T], lambda b: kt[:, T * b:T * b + T],
                              lambda b: v[:, b, :], probs, probs_t, bank)

            @block.vector
            def _(dve):
                link = Chain(dve, n["chain"])
                norm_vector(dve, n, 1, link, h[:, :, :], xn[:, :, :], sq[:, :, :], s)
                dve.wait_ge(loads, 48)
                for g, (b0, nb) in enumerate(GROUPS):
                    dve.wait_ge(qfull, g + 1)
                    if g >= 2:
                        dve.wait_ge(qtaken, 2 * g - 2)
                    p = 2 * (g % 2)
                    for w, table in enumerate(("rope_cos", "rope_sin")):
                        ins = dve.tensor_tensor(rot[:, w, 0:T * nb].rearrange("p (b t) -> p b t", t=T),
                                                bank[p + w][:, 0:T * nb].rearrange("p (b t) -> p b t", t=T),
                                                grow(tc(m, table), 1, nb), ALU.mult)
                    ins.then_inc(halves, 1)
                    dve.wait_ge(halves, g + 1)
                    c = slice(T * b0, T * (b0 + nb))
                    dve.tensor_tensor(qt[:, c], rot[0:S, 0, 0:T * nb], rot[0:S, 1, 0:T * nb], ALU.add).then_inc(qtaken, 1)
                    dve.tensor_tensor(kt[:, c], rot[S:128, 0, 0:T * nb], rot[S:128, 1, 0:T * nb], ALU.add).then_inc(qtaken, 1)
                    dve.wait_ge(qtaken, 2 * g + 2)
                attend_vector(dve, a, 0, m, 0.125, h, probs[:, :, :], s, bank)

            @block.scalar
            def _(act):
                norm_scalar(act, n, 1, xn[:, :, :], sq[:, :, :], s)
                act.wait_ge(wfull, 1)
                for i, o in enumerate((0, 128, 64, 192)):
                    act.activation(wq[:, o:o + 64], bank[7][0:S, 64 * i:64 * i + 64], ACT.Copy)
                act.activation(wq[:, 256:320], bank[7][0:S, 256:320], ACT.Copy).then_inc(wtaken, 1)
                take_turned(act, xt, bank, tfull, ttaken)
                for g in range(B // VB):
                    act.wait_ge(vfull, g + 1)
                    act.activation(v[:, VB * g:VB * g + VB, :].rearrange("p b d -> p (b d)"), bank[4 + g][0:T, :], ACT.Copy)\
                       .then_inc(vtaken, 1)
                attend_scalar(act, a, 0, probs, probs_t, bank)


def routed_feed_forward(nc, io, m):
    with ExitStack() as ctx:
        def sb(name, shape):
            return ctx.enter_context(nc.sbuf_tensor("ff_" + name, shape, F32))

        def sem(name):
            return ctx.enter_context(nc.semaphore("ff_" + name))

        h, xn, sq, s, xt, probs = (m[k] for k in ("h", "xn", "sq", "stats", "xt", "probs"))
        wr, wr_wide, br = sb("wr", [S, 1]), sb("wr_wide", [S, T]), sb("br", [T, 1])
        w1, b1, w2, b2 = sb("w1", [S, HID]), sb("b1", [128, 2]), sb("w2", [128, 2, S]), sb("b2", [S, 1])
        hid = sb("hid", [128, 2, TOK])
        yt = sb("yt", [S, TOK])
        ties = sb("ties", [T, B, T])
        bank = [ctx.enter_context(nc.psum_tensor(f"ff_bank{i}", [128, 512], F32)) for i in range(8)]
        loads, tfull, ttaken, wide = sem("loads"), sem("tfull"), sem("ttaken"), sem("wide")
        rfull, rtaken, hfull, htaken, yfull, ytaken, ofull, otaken = (sem(x) for x in (
            "rfull", "rtaken", "hfull", "htaken", "yfull", "ytaken", "ofull", "otaken"))
        n = norm_sems(ctx, nc, "ff_norm")
        ident = tc(m, "ident")

        with nc.Block() as block:
            @block.sync
            def _(sp):
                sp.dma_start(wr[:, :], io["ff_wr"]).then_inc(loads, 16)
                sp.dma_start(br[:, :], io["ff_br"].partition_broadcast(T).rearrange("p a b -> p (a b)")).then_inc(loads, 16)
                sp.dma_start(w1[:, :], io["ff_w1"]).then_inc(loads, 16)
                sp.dma_start(b1[:, :], io["ff_b1"]).then_inc(loads, 16)
                sp.dma_start(w2[:, :, :], io["ff_w2"].rearrange("(i p) d -> p i d", i=2)).then_inc(loads, 16)
                sp.dma_start(b2[:, :], io["ff_b2"]).then_inc(loads, 16)
                sp.wait_ge(loads, 96)

            @block.tensor
            def _(pe):
                pe.wait_ge(loads, 96)
                pe.wait_ge(wide, 1)
                pe.wait_ge(n["done"], 1)
                turn_tokens(pe, ident, xn, bank, tfull)
                pe.wait_ge(ttaken, NG)
                for g, (b0, nb) in enumerate(GROUPS):
                    pe.matmul(bank[g][0:T, 0:T * nb], wr_wide[:, :], xt[:, T * b0:T * (b0 + nb)]).then_inc(rfull, 1)
                for g, (b0, nb) in enumerate(GROUPS):
                    for i in range(2):
                        k = 2 * g + i
                        if k >= 3:
                            pe.wait_ge(htaken, k - 2)
                        pe.matmul(bank[5 + k % 3][:, 0:T * nb], w1[:, 128 * i:128 * i + 128], xt[:, T * b0:T * (b0 + nb)])\
                          .then_inc(hfull, 1)
                pe.wait_ge(rtaken, NG)
                for g, (b0, nb) in enumerate(GROUPS):
                    pe.wait_ge(htaken, 2 * g + 2)
                    for i in range(2):
                        ins = pe.matmul(bank[g][0:S, 0:T * nb], w2[:, i, :], hid[:, i, T * b0:T * (b0 + nb)],
                                        start=(i == 0), stop=(i == 1))
                    ins.then_inc(yfull, 1)
                for g in range(B // VB):
                    pe.wait_ge(ytaken, min(NG, (VB * g + VB - 1) // GB + 1))
                    if g == 3:
                        pe.wait_ge(ytaken, NG)
                    for i in range(VB):
                        b = VB * g + i
                        ins = pe.transpose(bank[(5, 6, 7, 0)[g]][0:T, S * i:S * i + S], yt[:, T * b:T * b + T], ident[0:S, 0:S])
                    ins.then_inc(ofull, 1)

            @block.scalar
            def _(act):
                norm_scalar(act, n, 1, xn[:, :, :], sq[:, :, :], s)
                take_turned(act, xt, bank, tfull, ttaken)
                act.wait_ge(loads, 96)
                for g, (b0, nb) in enumerate(GROUPS):
                    for i in range(2):
                        k = 2 * g + i
                        act.wait_ge(hfull, k + 1)
                        act.activation(hid[:, i, T * b0:T * (b0 + nb)], bank[5 + k % 3][:, 0:T * nb], ACT.Gelu_apprx_tanh,
                                       bias=b1[:, i:i + 1]).then_inc(htaken, 1)
                for g, (b0, nb) in enumerate(GROUPS):
                    act.wait_ge(yfull, g + 1)
                    act.activation(yt[:, T * b0:T * (b0 + nb)], bank[g][0:S, 0:T * nb], ACT.Identity, bias=b2[:, 0:1])\
                       .then_inc(ytaken, 1)

            @block.vector
            def _(dve):
                link = Chain(dve, n["chain"])
                dve.wait_ge(loads, 96)
                dve.tensor_copy(wr_wide[:, :], wr[:, 0:1].to_broadcast([S, T])).then_inc(wide, 1)
                norm_vector(dve, n, 1, link, h[:, :, :], xn[:, :, :], sq[:, :, :], s)
                for g, (b0, nb) in enumerate(GROUPS):
                    dve.wait_ge(rfull, g + 1)
                    dve.tensor_scalar(probs[:, b0:b0 + nb, :].rearrange("p b t -> p (b t)"), bank[g][0:T, 0:T * nb], br[:, 0:1], None,
                                      ALU.add).then_inc(rtaken, 1)
                dve.wait_ge(rtaken, NG)
                own, rank, sel = s[:, 0:32], s[:, 32:64], s[:, 64:96]
                link(dve.tensor_tensor(ties[:, :, :], probs[:, :, :], grow(tc(m, "ident")[0:T, 0:T], 1, B), ALU.mult))
                link(dve.tensor_reduce(own, ties[:, :, :], AX.X, ALU.add))
                link(dve.tensor_tensor(ties[:, :, :], probs[:, :, :], grow(own, 2, T), ALU.is_equal))
                link(dve.tensor_tensor(ties[:, :, :], ties[:, :, :], grow(tc(m, "before"), 1, B), ALU.mult))
                link(dve.tensor_tensor(probs[:, :, :], probs[:, :, :], grow(own, 2, T), ALU.is_gt))
                link(dve.tensor_tensor(ties[:, :, :], ties[:, :, :], probs[:, :, :], ALU.add))
                link(dve.tensor_reduce(rank, ties[:, :, :], AX.X, ALU.add))
                link(dve.tensor_scalar(sel, rank, KK - 0.5, None, ALU.is_lt))
                link(dve.tensor_tensor(sel, sel, own, ALU.mult))
                for g in range(B // VB):
                    bs = slice(VB * g, VB * g + VB)
                    dve.wait_ge(ofull, g + 1)
                    link(dve.tensor_tensor(sq[:, bs, :], bank[(5, 6, 7, 0)[g]][0:T, :].rearrange("p (b d) -> p b d", d=S),
                                           grow(sel[:, bs], 2, S), ALU.mult))
                link(dve.tensor_tensor(sq[:, :, :], sq[:, :, :], xn[:, :, :], ALU.add))
                link(dve.tensor_tensor(h[:, :, :], h[:, :, :], sq[:, :, :], ALU.add))


KT = (TOK + 127) // 128
CHN = TOK // 5


def similarity_attention(nc, io, m):
    with ExitStack() as ctx:
        def sb(name, shape):
            return ctx.enter_context(nc.sbuf_tensor("sa_" + name, shape, F32))

        def sem(name):
            return ctx.enter_context(nc.semaphore("sa_" + name))

        h, xn, sq, s = (m[k] for k in ("h", "xn", "sq", "stats"))
        ft = sb("ft", [S, KT * 128])
        ftok = sb("ftok", [128, KT, T])
        e = sb("exp", [128, 3, CHN])
        att_t = sb("att_t", [T, TOK])
        att = sb("att", [T, B, T])
        rec = sb("rec", [T, B])
        bank = [ctx.enter_context(nc.psum_tensor(f"sa_bank{i}", [128, 512], F32)) for i in range(8)]
        tfull, ttaken, ffull, ftaken, zero = sem("tfull"), sem("ttaken"), sem("ffull"), sem("ftaken"), sem("zero")
        sfull, exped, afull, ataken, ofull, otaken = (sem(x) for x in ("sfull", "exped", "afull", "ataken", "ofull", "otaken"))
        n = norm_sems(ctx, nc, "sa_norm")
        ident = tc(m, "ident")
        REST = TOK - 128 * (KT - 1)

        with nc.Block() as block:
            @block.gpsimd
            def _(pool):
                pool.memset(ft[:, TOK:], 0.0)
                pool.memset(ftok[:, KT - 1, :], 0.0)
                pool.memset(ftok[:, 0:KT - 1, S:T], 1.0).then_inc(zero, 1)
                pool.wait_ge(zero, 1)
                pool.memset(ftok[0:REST, KT - 1, S:T], 1.0).then_inc(zero, 1)

            @block.tensor
            def _(pe):
                pe.wait_ge(n["done"], 2)
                turn_tokens(pe, ident, xn, bank, tfull)
                pe.wait_ge(ttaken, NG)
                for t in range(KT):
                    r = REST if t == KT - 1 else 128
                    ins = pe.transpose(bank[t // 8][0:r, S * (t % 8):S * (t % 8) + S], ft[:, 128 * t:128 * t + r], ident[0:S, 0:S])
                    if t % 8 == 7 or t == KT - 1:
                        ins.then_inc(ffull, 1)
                pe.wait_ge(ftaken, 3)
                pe.wait_ge(zero, 2)
                with pe.Fori(0, 5) as c:
                    q = ft[:, bass.ds(c * CHN, CHN)]

                    def score(t):
                        if t >= 3:
                            wait_for(m, pe, exped, c * KT + t - 1)
                        elif t == 0:
                            wait_for(m, pe, exped, c * KT + 1)
                        pe.matmul(bank[t % 3][:, 0:CHN], ft[:, 128 * t:128 * t + 128], q).then_inc(sfull, 1)

                    score(0)
                    score(1)
                    wait_for(m, pe, ataken, c + 1)
                    for t in range(KT):
                        if t + 2 < KT:
                            score(t + 2)
                        wait_for(m, pe, exped, c * KT + t + 2)
                        ins = pe.matmul(bank[4][0:T, 0:CHN], ftok[:, t, :], e[:, t % 3, :], start=(t == 0), stop=(t == KT - 1))
                    ins.then_inc(afull, 1)
                pe.wait_ge(ataken, 6)
                for g, (b0, nb) in enumerate(GROUPS):
                    if g == 1:
                        pe.wait_ge(exped, 5 * KT + 1)
                    for i in range(nb):
                        b = b0 + i
                        ins = pe.transpose(bank[g][0:T, T * i:T * i + T], att_t[:, T * b:T * b + T], ident[0:T, 0:T])
                    ins.then_inc(ofull, 1)

            @block.scalar
            def _(act):
                norm_scalar(act, n, 1, xn[:, :, :], sq[:, :, :], s)
                norm_scalar(act, n, 2, xn[:, :, :], sq[:, :, :], s)
                take_turned(act, ft, bank, tfull, ttaken)
                act.sem_inc(exped, 1)
                with act.Fori(0, 5) as c:
                    for t in range(KT):
                        act.wait_ge(sfull, c * KT + t + 1)
                        act.activation(e[:, t % 3, :], bank[t % 3][:, 0:CHN], ACT.Exp).then_inc(exped, 1)
                norm_scalar(act, n, 3, sq[:, :, :], m["probs"][:, :, 0:S], s)

            @block.vector
            def _(dve):
                link = Chain(dve, n["chain"])
                norm_vector(dve, n, 1, link, h[:, :, :], xn[:, :, :], sq[:, :, :], s)
                dve.engine_nop().then_inc(n["input"], 1)
                norm_vector(dve, n, 2, link, xn[:, :, :], xn[:, :, :], sq[:, :, :], s, centre=False)
                dve.wait_ge(zero, 2)
                for g in range(3):
                    dve.wait_ge(ffull, g + 1)
                    k = min(8, KT - 8 * g)
                    r = REST if g == 2 else 128
                    dve.tensor_copy(ftok[0:r, 8 * g:8 * g + k, 0:S], bank[g][0:r, 0:S * k].rearrange("p (t d) -> p t d", d=S))\
                       .then_inc(ftaken, 1)
                dve.sem_inc(ataken, 1)
                with dve.Fori(0, 5) as c:
                    dve.wait_ge(afull, c + 1)
                    dve.tensor_copy(att_t[:, bass.ds(c * CHN, CHN)], bank[4][0:T, 0:CHN]).then_inc(ataken, 1)
                for g, (b0, nb) in enumerate(GROUPS):
                    dve.wait_ge(ofull, g + 1)
                    link(dve.tensor_copy(att[:, b0:b0 + nb, :].rearrange("p b t -> p (b t)"), bank[g][0:T, 0:T * nb]))
                link(dve.reciprocal(rec[:, :], att[:, :, S]))
                link(dve.tensor_scalar(rec[:, :], rec[:, :], float(np.float32(1.0 - 0.8)), None, ALU.mult))
                link(dve.tensor_tensor(att[:, :, 0:S], att[:, :, 0:S], grow(rec[:, :], 2, S), ALU.mult))
                dve.scalar_tensor_tensor(out=sq[:, :, :], in0=xn[:, :, :], scalar=0.8, in1=att[:, :, 0:S],
                                         op0=ALU.mult, op1=ALU.add).then_inc(n["input"], 1)
                norm_vector(dve, n, 3, link, sq[:, :, :], sq[:, :, :], m["probs"][:, :, 0:S], s, centre=False)
                link(dve.tensor_tensor(h[:, :, :], h[:, :, :], sq[:, :, :], ALU.add))


HEADS = 8
KEYS = 64
TOP = 16
GROUPS_K = 2 * HEADS
TILES = B // 2
DENSE = 3
GH = HEADS - DENSE
SUM_PARTS = ((0, 3), (3, GH))
CHUNKS_K = KEYS ** 2 // 128
BATCHES = CHUNKS_K // 4
BIG = 1e4
UNITS = 2 * HEADS
UNIT_BANKS = ((0, 7), (7, 7), (14, 2))
Q_BANKS = ((0, 3), (3, 3), (6, 2))


def memory_attention(nc, io, m):
    with ExitStack() as ctx:
        def sb(name, shape, dt=F32):
            return ctx.enter_context(nc.sbuf_tensor("me_" + name, shape, dt))

        def sem(name):
            return ctx.enter_context(nc.semaphore("me_" + name))

        h, xn, sq, s, xt = (m[k] for k in ("h", "xn", "sq", "stats", "xt"))
        ident = tc(m, "ident")
        fold = sb("fold", [S, GROUPS_K * KEYS])
        wq = sb("wq", [S, HEADS, S])
        wo = sb("wo", [128, HEADS, S])
        numbers = sb("numbers", [128, TOP])
        first_row = sb("first_row", [128, HEADS])
        eye32 = sb("eye32", [128, 32])
        xtile = sb("xtile", [S, 128])
        xq = sb("xq", [S, 2 * T])
        sim = sb("sim", [128, GROUPS_K, KEYS])
        rest = sb("rest", [128, GROUPS_K, KEYS])
        vals = sb("vals", [128, GROUPS_K, TOP])
        pos = sb("pos", [128, GROUPS_K, TOP], U32)
        posf = sb("posf", [128, GROUPS_K, TOP])
        work = sb("work", [128, HEADS * TOP * TOP])
        pairs = work[:, :].rearrange("p (h c) -> p h c", h=HEADS)
        best = sb("best", [128, HEADS, TOP])
        cell = sb("cell", [128, HEADS, TOP], U32)
        half = sb("half", [128, 2, HEADS * TOP], U32)
        halff = sb("halff", [128, 2, HEADS * TOP])
        hot = work[:, :].rearrange("p (k i) -> p k i", i=TOP)
        picked = sb("picked", [128, 2, HEADS * TOP])
        total = sb("total", [128, HEADS])
        rows_next = sb("rows_next", [128, HEADS, TOP], U32)
        rows = sb("rows", [128, HEADS, TOP], U32)
        wts = sb("wts", [128, HEADS, TOP])
        rows_cls = sb("rows_cls", [128, HEADS, TOP // 4], U32)
        wts_cls = sb("wts_cls", [128, HEADS, TOP // 4])
        got = sb("got", [128, GH, TOP, 128])
        spread32 = got[:, 0:2].rearrange("p s j c -> p (s j c)")
        pk = got[0:32, 2].rearrange("p j c -> p (j c)").rearrange("p (w g k) -> p w g k", w=2, g=GROUPS_K)
        prod = work[:, :].rearrange("p (j c) -> p j c", c=128)
        tab = sb("tab", [128, DENSE, CHUNKS_K, 128])
        spread = sb("spread", [128, CHUNKS_K, 128], BF16)
        minus = sb("minus", [128, 128], BF16)
        keys64 = sb("keys64", [128, KEYS])
        ranks = sb("ranks", [128, DENSE, 2, TOP])
        threshold = sb("threshold", [128, 1])
        below = sb("below", [128, DENSE, 2, KEYS])
        steps = sb("steps", [128, DENSE, 2, KEYS])
        inv_z = sb("inv_z", [128, DENSE])
        left = sb("left", [128, DENSE * 128])
        split = [sb(f"split{i}", [128, DENSE * 128], BF16) for i in range(3)]
        steps_t = sb("steps_t", [128, DENSE * 128], BF16)
        penalty = sb("penalty", [128, 2, 512], BF16)
        wt = sb("wt", [128, 2, 512])
        kv = sb("kv", [128, HEADS, 128])
        kvt = sb("kvt", [128, HEADS, 2, T])
        kvt_cls = sb("kvt_cls", [128, HEADS, B])
        qt = sb("qt", [S, HEADS, 2 * T])
        vo = sb("vo", [T, UNITS, S])
        probs, probs_t = (m[k][:, :, :].rearrange("p b d -> p (b d)")[:, 0:UNITS * T].rearrange("p (u t) -> p u t", t=T)
                          for k in ("sq", "xn"))
        mx, z = sb("mx", [T, UNITS]), sb("z", [T, UNITS])
        bank = [ctx.enter_context(nc.psum_tensor(f"me_bank{i}", [128, 512], F32)) for i in range(8)]
        SIM = KVB = (0, 1)
        DS, ATT, OUT = (2, 3), (4, 5, 6), 7

        loads, tfull, ttaken, folded, fold_taken = (sem(x) for x in ("loads", "tfull", "ttaken", "folded", "fold_taken"))
        x_ready, sim_full, sim_ready, sim_used = (sem(x) for x in ("x_ready", "sim_full", "sim_ready", "sim_used"))
        w_shifted, w_exped, posted = sem("w_shifted"), sem("w_exped"), sem("rows_posted")
        slot_free, summed = sem("slot_free"), sem("summed")
        gathered = [sem(f"gathered{i}") for i in range(GH)]
        cls_posted, cls_gathered, cls_summed = sem("cls_posted"), sem("cls_gathered"), sem("cls_summed")
        spread_made, tab_loaded = sem("spread_made"), sem("table_loaded")
        LOADS = 9 + DENSE
        dense_ready, dense_turned, top_part, rest1, mid_part, low_part = (sem(x) for x in (
            "dense_ready", "dense_turned", "top_part", "rest1", "mid_part", "low_part"))
        marks_full, penalty_made, ds_full, wt_made, dense_summed, dense_taken = (sem(x) for x in (
            "marks_full", "penalty_made", "dense_scores_full", "wt_made", "dense_summed", "dense_taken"))
        cls_turned, cls_taken = sem("cls_turned"), sem("cls_taken")
        kv_turned, kvt_ready = sem("kv_turned"), sem("kvt_ready")
        xq_ready, q_full, q_taken = sem("xq_ready"), sem("q_full"), sem("q_taken")
        vo_full, vo_taken, s_full, s_taken = sem("vo_full"), sem("vo_taken"), sem("scores_full"), sem("scores_taken")
        shifted, exped, p_ready, p_turned, p_taken = (sem(x) for x in ("shifted", "exped", "probs", "probs_turned", "probs_taken"))
        out_full, out_added = sem("out_full"), sem("out_added")
        n = norm_sems(ctx, nc, "me_norm")
        chosen_cls, chosen = sem("class_choice_steps"), sem("choice_steps")
        attending = sem("attend_steps")
        CHOICE = 27


        def choose(dve, u, R, part):
            cls = R == B
            G = HEADS if cls else GH
            before = 0 if part == 1 else 3
            link = Chain(dve, chosen_cls, before) if cls else Chain(dve, chosen, (u - 1) * CHOICE + before, m)
            a, b = slice(0, 8), slice(8, TOP)
            if part == 1:
                wait_for(m, dve, sim_ready, u + 1)
                for g in range(GROUPS_K):
                    ins = dve.max(out=vals[0:R, g, a], in_=sim[0:R, g, :])
                link(ins)
                if not cls:
                    wait_for(m, dve, dense_turned, u)
                    for i in range(2):
                        g = slice(HEADS * i + GH, HEADS * i + HEADS)
                        dve.tensor_tensor(below[:, :, i, :], sim[:, g, :], grow(vals[:, g, 0], 2, KEYS), ALU.subtract)
                for g in range(GROUPS_K):
                    dve.max_index(out=pos[0:R, g, a], in_max=vals[0:R, g, a], in_values=sim[0:R, g, :])
                for g in range(GROUPS_K):
                    ins = dve.match_replace(out=rest[0:R, g, :], in_to_replace=vals[0:R, g, a], in_values=sim[0:R, g, :], imm_value=NEG)
                ins.then_inc(sim_used, 1)
                wait_for(m, dve, sim_used, u + 1)
                for g in range(GROUPS_K):
                    ins = dve.max(out=vals[0:R, g, b], in_=rest[0:R, g, :])
                link(ins)
                for g in range(GROUPS_K):
                    ins = dve.max_index(out=pos[0:R, g, b], in_max=vals[0:R, g, b], in_values=rest[0:R, g, :])
                link(ins)
                return
            link(dve.tensor_tensor(pairs[0:R].rearrange("p h (i j) -> p h i j", j=TOP),
                                   grow(vals[0:R, 0:HEADS, :], 3, TOP), grow(vals[0:R, HEADS:, :], 2, TOP), ALU.add))
            for g in range(HEADS):
                ins = dve.max(out=best[0:R, g, a], in_=pairs[0:R, g, :])
            link(ins)
            for g in range(HEADS):
                ins = dve.max_index(out=cell[0:R, g, a], in_max=best[0:R, g, a], in_values=pairs[0:R, g, :])
            link(ins)
            for g in range(HEADS):
                ins = dve.match_replace(out=pairs[0:R, g, :], in_to_replace=best[0:R, g, a], in_values=pairs[0:R, g, :], imm_value=NEG)
            link(ins)
            for g in range(HEADS):
                ins = dve.max(out=best[0:R, g, b], in_=pairs[0:R, g, :])
            link(ins)
            for g in range(HEADS):
                dve.max_index(out=cell[0:R, g, b], in_max=best[0:R, g, b], in_values=pairs[0:R, g, :])
            link(dve.tensor_copy(total[0:R, :], best[0:R, :, 0]))
            dve.tensor_tensor(best[0:R], best[0:R], grow(total[0:R, :], 2, TOP), ALU.subtract).then_inc(w_shifted, 1)
            c = cell[0:R].rearrange("p h k -> p (h k)")
            dve.tensor_scalar(half[0:R, 0, :], c, 4, None, ALU.logical_shift_right)
            dve.tensor_scalar(half[0:R, 1, :], c, TOP - 1, None, ALU.bitwise_and)
            link(dve.tensor_copy(posf[0:R], pos[0:R]))
            link(dve.tensor_copy(halff[0:R], half[0:R]))
            iota = numbers[0:R, :]
            for i in range(2):
                H = HEADS if i == 0 else G
                marks = hot[0:R, 0:H * TOP, :]
                link(dve.tensor_tensor(marks, grow(halff[0:R, i, 0:H * TOP], 2, TOP), grow(iota, 1, H * TOP), ALU.is_equal))
                if i == 0 and not cls:
                    link(dve.tensor_reduce(ranks[:, :, 0, :], hot[:, GH * TOP:, :].rearrange("p (h k) i -> p h i k", h=DENSE), AX.X, ALU.add))
                marks = hot[0:R, 0:G * TOP, :]
                marks4 = marks.rearrange("p (h k) i -> p h k i", h=G)
                link(dve.tensor_tensor(marks4, marks4, grow(posf[0:R, HEADS * i:HEADS * i + G, :], 2, TOP), ALU.mult))
                link(dve.tensor_reduce(picked[0:R, i, 0:G * TOP], marks, AX.X, ALU.add))
            if not cls:
                places = work[:, :].rearrange("p (i n k) -> p i n k", i=2, n=KEYS)
                numbered = grow(grow(keys64[:, :], 1, 2), 3, TOP)
                for d in range(DENSE):
                    at = posf[:, :, :].rearrange("p (i h) k -> p i h k", i=2)[:, :, GH + d, :]
                    link(dve.tensor_tensor(places, grow(at, 2, KEYS), numbered, ALU.is_equal))
                    link(dve.tensor_tensor(places, places, grow(ranks[:, d], 2, KEYS), ALU.mult))
                    dve.tensor_reduce(steps[:, d], places, AX.X, ALU.add).then_inc(dense_ready, 1)
                    wait_for(m, dve, dense_ready, DENSE * (u - 1) + d + 1)
            p0 = picked[0:R, 0, 0:G * TOP]
            wait_for(m, dve, w_exped, u + 1)
            dve.tensor_reduce(total[0:R, :], best[0:R], AX.X, ALU.add)
            link(dve.scalar_tensor_tensor(out=p0, in0=picked[0:R, 1, 0:G * TOP], scalar=float(KEYS), in1=p0, op0=ALU.mult, op1=ALU.add))
            dve.reciprocal(total[0:R, :], total[0:R, :])
            link(dve.tensor_tensor(rows_next[0:R, 0:G, :], p0.rearrange("p (h k) -> p h k", h=G), grow(first_row[0:R, 0:G], 2, TOP), ALU.add))
            link(dve.tensor_tensor(best[0:R], best[0:R], grow(total[0:R, :], 2, TOP), ALU.mult))
            assert cls or 3 + link.n == CHOICE, 3 + link.n

        def post(dve, u, f):
            hs = slice(*SUM_PARTS[f])
            dve.tensor_copy(wts[:, hs, :], best[:, hs, :])
            if f == 1:
                dve.tensor_copy(inv_z[:, :], total[:, GH:])
            dve.tensor_copy(rows[:, hs, :], rows_next[:, hs, :]).then_inc(posted, 1)

        def sum_rows(dve, t, f, post_next):
            if f == 0:
                dve.wait_ge(kv_turned, 2 * t)
            for hd in range(*SUM_PARTS[f]):
                dve.wait_ge(gathered[hd], 16 * TOP * (t + 1))
                dve.tensor_tensor(prod, got[:, hd], grow(wts[:, hd, :], 2, 128), ALU.mult).then_inc(slot_free, 1)
                dve.wait_ge(slot_free, GH + GH * t + hd + 1)
                dve.tensor_reduce(kv[:, hd, :], prod.rearrange("p j c -> p c j"), AX.X, ALU.add).then_inc(summed, 1)
                dve.wait_ge(summed, GH * t + hd + 1)
            if post_next:
                if f == 1:
                    dve.wait_ge(dense_taken, DENSE * t + DENSE)
                post(dve, t + 2, f)
                dve.wait_ge(posted, 2 * t + 2 + f + 1)

        def dense_turn(pe, t):
            wait_for(m, pe, dense_ready, DENSE * t + DENSE)
            for k, x in enumerate((below, steps)):
                for d in range(DENSE):
                    ins = pe.transpose(bank[DS[k]][:, 128 * d:128 * d + 128], x[:, d].rearrange("p i k -> p (i k)"), ident[:, :])
            ins.then_inc(dense_turned, 1)

        def split_scalar(act, t):
            D = DENSE * 128
            act.wait_ge(dense_turned, t + 2)
            act.activation(split[0][:, :], bank[DS[0]][:, 0:D], ACT.Copy).then_inc(top_part, 1)
            act.activation(steps_t[:, :], bank[DS[1]][:, 0:D], ACT.Copy)
            act.wait_ge(rest1, t + 1)
            act.activation(split[1][:, :], left[:, :], ACT.Copy).then_inc(mid_part, 1)

        def split_vector(dve, t):
            dve.wait_ge(top_part, t + 1)
            dve.tensor_tensor(left[:, :], bank[DS[0]][:, 0:DENSE * 128], split[0][:, :], ALU.subtract).then_inc(rest1, 1)
            dve.wait_ge(mid_part, t + 1)
            dve.tensor_tensor(split[2][:, :], left[:, :], split[1][:, :], ALU.subtract).then_inc(low_part, 1)

        def dense_tensor(pe, t, d, after_out=False):
            first = (DENSE * t + d) * BATCHES
            tokens = slice(128 * d, 128 * d + 128)

            def marks(b):
                if b >= 2:
                    wait_for(m, pe, penalty_made, first + b - 1)
                for i in range(4):
                    ins = pe.matmul(bank[SIM[b % 2]][:, 128 * i:128 * i + 128], spread[:, 4 * b + i, :], steps_t[:, tokens])
                ins.then_inc(marks_full, 1)

            def scores(b):
                if b >= 2:
                    wait_for(m, pe, wt_made, first + b - 1)
                for i in range(4):
                    for k in range(3):
                        pe.matmul(bank[DS[b % 2]][:, 128 * i:128 * i + 128], spread[:, 4 * b + i, :], split[k][:, tokens],
                                  start=(i == 0 and k == 0), stop=False)

            marks(0)
            if d == 0:
                wait_for(m, pe, low_part, t + 1)
            scores(0)
            for b in range(BATCHES):
                if b + 1 < BATCHES:
                    marks(b + 1)
                wait_for(m, pe, penalty_made, first + b + 1)
                pe.matmul(bank[DS[b % 2]][:, :], minus[:, :], penalty[:, b % 2], start=False, stop=True).then_inc(ds_full, 1)
                if b + 1 < BATCHES:
                    scores(b + 1)
                wait_for(m, pe, wt_made, first + b + 1)
                if b == 0:
                    wait_for(m, pe, dense_taken, DENSE * t + d)
                    if after_out:
                        wait_for(m, pe, out_added, t + 1)
                for i in range(4):
                    ins = pe.matmul(bank[OUT][:, 128 + 128 * d:256 + 128 * d], wt[:, b % 2, 128 * i:128 * i + 128], tab[:, d, 4 * b + i, :],
                                    start=(b == 0 and i == 0), stop=(b == BATCHES - 1 and i == 3))
                ins.then_inc(dense_summed, 1)

        def dense_scalar(act, t, d):
            first = (DENSE * t + d) * BATCHES

            def penal(b):
                act.wait_ge(marks_full, first + b + 1)
                act.activation(penalty[:, b % 2], bank[SIM[b % 2]][:, :], ACT.Relu, bias=threshold[:, 0:1], scale=-BIG).then_inc(penalty_made, 1)

            penal(0)
            for b in range(BATCHES):
                if b + 1 < BATCHES:
                    penal(b + 1)
                act.wait_ge(ds_full, first + b + 1)
                if b >= 2:
                    act.wait_ge(dense_summed, first + b - 1)
                act.activation(wt[:, b % 2], bank[DS[b % 2]][:, :], ACT.Exp).then_inc(wt_made, 1)
            act.wait_ge(dense_summed, first + BATCHES)
            act.activation(kv[:, GH + d, :], bank[OUT][:, 128 + 128 * d:256 + 128 * d], ACT.Copy, scale=inv_z[:, d:d + 1])\
               .then_inc(dense_taken, 1)

        def attend_a(dve, t):
            for g, (u0, nu) in enumerate(UNIT_BANKS):
                dve.wait_ge(s_full, 3 * t + g + 1)
                dve.tensor_tensor(probs[:, u0:u0 + nu, :], bank[ATT[g]][0:T, 0:T * nu].rearrange("p (u t) -> p u t", t=T),
                                  grow(tc(m, "causal"), 1, nu), ALU.add).then_inc(s_taken, 1)
            dve.wait_ge(s_taken, 3 * t + 3)
            dve.tensor_reduce(mx[:, :], probs[:, :, :], AX.X, ALU.max).then_inc(attending, 1)
            dve.wait_ge(attending, 3 * t + 1)
            dve.tensor_tensor(probs[:, :, :], probs[:, :, :], grow(mx[:, :], 2, T), ALU.subtract).then_inc(shifted, 1)

        def attend_b(dve, t):
            dve.wait_ge(exped, t + 1)
            dve.tensor_reduce(z[:, :], probs[:, :, :], AX.X, ALU.add).then_inc(attending, 1)
            dve.wait_ge(attending, 3 * t + 2)
            dve.reciprocal(z[:, :], z[:, :]).then_inc(attending, 1)
            dve.wait_ge(attending, 3 * t + 3)
            dve.tensor_tensor(probs[:, :, :], probs[:, :, :], grow(z[:, :], 2, T), ALU.mult).then_inc(p_ready, 1)

        def attend_c(dve, t):
            dve.wait_ge(out_full, t + 1)
            hb = h[:, bass.ds(2 * t, 2), :]
            dve.tensor_tensor(hb, bank[OUT][0:T, 0:2 * S].rearrange("p (b d) -> p b d", d=S), hb, ALU.add).then_inc(out_added, 1)

        def vector_tile(dve, t, choose_next=True, attend=True):
            split_vector(dve, t)
            if choose_next:
                choose(dve, t + 2, 128, 1)
            if attend:
                attend_a(dve, t - 1)
            if choose_next:
                choose(dve, t + 2, 128, 2)
            if attend:
                attend_b(dve, t - 1)
            sum_rows(dve, t, 0, choose_next)
            if attend:
                attend_c(dve, t - 1)
            sum_rows(dve, t, 1, choose_next)

        def similarities(pe, u, R, after_values=False):
            wait_for(m, pe, x_ready, u + 1)
            if after_values:
                wait_for(m, pe, vo_taken, 2 * u - 6)
            else:
                wait_for(m, pe, sim_ready, u)
            pe.matmul(bank[SIM[0]][0:R, :], xtile[:, 0:R], fold[:, 0:512])
            pe.matmul(bank[SIM[1]][0:R, :], xtile[:, 0:R], fold[:, 512:1024]).then_inc(sim_full, 1)

        def unit(g, u0, i):
            return bank[ATT[g]][0:T, T * i:T * i + T], (u0 + i) // 2, (u0 + i) % 2

        def tensor_scores(pe, t):
            wait_for(m, pe, kvt_ready, 2 * t + 2)
            for u in range(UNITS):
                ins = pe.matmul(bank[KVB[u // 8]][0:T, S * (u % 8):S * (u % 8) + S], kvt[S:128, u // 2, u % 2, :], wo[S:128, u // 2, :])
                if u % 8 == 7:
                    ins.then_inc(vo_full, 1)
            wait_for(m, pe, q_taken, 3 * t + 3)
            for g, (u0, nu) in enumerate(UNIT_BANKS):
                for i in range(nu):
                    o, hd, b = unit(g, u0, i)
                    ins = pe.matmul(o, qt[:, hd, T * b:T * b + T], kvt[0:S, hd, b, :])
                ins.then_inc(s_full, 1)

        def tensor_out(pe, t, taken_before):
            wait_for(m, pe, p_ready, t + 1)
            for g, (u0, nu) in enumerate(UNIT_BANKS):
                for i in range(nu):
                    ins = pe.transpose(unit(g, u0, i)[0], probs[:, u0 + i, :], ident[0:T, 0:T])
                ins.then_inc(p_turned, 1)
            wait_for(m, pe, p_taken, 3 * t + 3)
            wait_for(m, pe, vo_taken, 2 * t + 2)
            wait_for(m, pe, dense_taken, taken_before)
            wait_for(m, pe, out_added, t + 1)
            for b in range(2):
                for hd in range(HEADS):
                    ins = pe.matmul(bank[OUT][0:T, S * b:S * b + S], probs_t[:, 2 * hd + b, :], vo[:, 2 * hd + b, :],
                                    start=(hd == 0), stop=(hd == HEADS - 1))
            ins.then_inc(out_full, 1)

        def queries(pe, t):
            wait_for(m, pe, xq_ready, t + 1)
            for g, (h0, nh) in enumerate(Q_BANKS):
                for i in range(nh):
                    ins = pe.matmul(bank[ATT[g]][0:S, 2 * T * i:2 * T * i + 2 * T], wq[:, h0 + i, :], xq[:, :])
                ins.then_inc(q_full, 1)

        def turn_kv(pe, t):
            for f in range(2):
                wait_for(m, pe, summed, GH * t + min(4 * f + 4, GH))
                if f == 1:
                    wait_for(m, pe, dense_taken, DENSE * t + DENSE)
                for i in range(4):
                    ins = pe.transpose(bank[KVB[f]][:, 128 * i:128 * i + 128], kv[:, 4 * f + i, :], ident[:, :])
                ins.then_inc(kv_turned, 1)

        def tensor_tile(pe, t, ahead=True, attend=True):
            dense_turn(pe, t)
            if attend:
                tensor_scores(pe, t - 1)
            if ahead:
                similarities(pe, t + 3, 128, attend)
                wait_for(m, pe, sim_ready, t + 4)
            elif attend:
                wait_for(m, pe, vo_taken, 2 * t)
            dense_tensor(pe, t, 0)
            dense_tensor(pe, t, 1)
            if attend:
                tensor_out(pe, t - 1, DENSE * t + 2)
            queries(pe, t)
            dense_tensor(pe, t, 2, after_out=attend)
            turn_kv(pe, t)

        def copy_x(act, t):
            act.wait_ge(sim_full, t + 1)
            act.activation(xtile[:, :].rearrange("p (b t) -> p b t", b=2),
                           xt[:, bass.ds(2 * T * t, 2 * T)].rearrange("p (b t) -> p b t", b=2)[:, :, 0:S], ACT.Copy)\
               .then_inc(x_ready, 1)

        def copy_xq(act, t):
            act.wait_ge(q_full, 3 * t)
            act.activation(xq[:, :], xt[:, bass.ds(2 * T * t, 2 * T)], ACT.Copy).then_inc(xq_ready, 1)

        def copy_sim(act, u, R):
            act.wait_ge(sim_full, u + 1)
            act.wait_ge(sim_used, u)
            for i in range(2):
                ins = act.activation(sim[0:R, HEADS * i:HEADS * i + HEADS, :].rearrange("p g k -> p (g k)"), bank[SIM[i]][0:R, :], ACT.Copy)
            ins.then_inc(sim_ready, 1)

        def exp_weights(act, u, R):
            act.wait_ge(w_shifted, u + 1)
            act.activation(best[0:R], best[0:R], ACT.Exp).then_inc(w_exped, 1)

        def scalar_tile(act, t, ahead=True, choose_next=True, attend=True):
            if ahead:
                copy_x(act, t + 2)
            copy_xq(act, t)
            split_scalar(act, t)
            if attend:
                for i in range(2):
                    act.wait_ge(vo_full, 2 * (t - 1) + i + 1)
                    act.activation(vo[:, 8 * i:8 * i + 8, :].rearrange("p u d -> p (u d)"), bank[KVB[i]][0:T, :], ACT.Copy).then_inc(vo_taken, 1)
            if ahead:
                copy_sim(act, t + 3, 128)
            if attend:
                act.wait_ge(shifted, t)
                act.activation(probs[:, :, :], probs[:, :, :], ACT.Exp).then_inc(exped, 1)
            dense_scalar(act, t, 0)
            if choose_next:
                exp_weights(act, t + 2, 128)
            dense_scalar(act, t, 1)
            if attend:
                for g, (u0, nu) in enumerate(UNIT_BANKS):
                    act.wait_ge(p_turned, 3 * (t - 1) + g + 1)
                    act.activation(probs_t[:, u0:u0 + nu, :].rearrange("p u t -> p (u t)"), bank[ATT[g]][0:T, 0:T * nu], ACT.Copy)\
                       .then_inc(p_taken, 1)
            for g, (h0, nh) in enumerate(Q_BANKS):
                act.wait_ge(q_full, 3 * t + g + 1)
                act.activation(qt[:, h0:h0 + nh, :].rearrange("p h t -> p (h t)"), bank[ATT[g]][0:S, 0:2 * T * nh], ACT.Copy,
                               scale=S ** -0.5).then_inc(q_taken, 1)
            dense_scalar(act, t, 2)
            for f in range(2):
                hs = slice(4 * f, 4 * f + 4)
                act.wait_ge(kv_turned, 2 * t + f + 1)
                act.activation(kvt[:, hs, :, 0:S], bank[KVB[f]][:, :].rearrange("p (h b t) -> p h b t", h=4, b=2), ACT.Copy)
                act.activation(kvt[:, hs, :, S], kvt_cls[:, hs, bass.ds(2 * t, 2)], ACT.Copy).then_inc(kvt_ready, 1)

        def gather(pool, t):
            for hd in range(GH):
                if hd in (0, SUM_PARTS[1][0]):
                    wait_for(m, pool, posted, 2 * t + (1 if hd == 0 else 2))
                wait_for(m, pool, slot_free, GH * t + hd + 1)
                for j in range(TOP):
                    pool.indirect_dma_start(got[:, hd, j, :], None, io["table"],
                                            bass.IndirectOffsetOnAxis(rows[:, hd, j:j + 1], 0)).then_inc(gathered[hd], 16)

        with nc.Block() as block:
            @block.sync
            def _(sp):
                sp.dma_start(pk[:, 0], io["pk_w"]).then_inc(loads, 16)
                sp.dma_start(pk[:, 1], io["pk_k"]).then_inc(loads, 16)
                sp.dma_start(spread32, io["spread"]).then_inc(loads, 16)
                sp.dma_start(keys64[:, :], io["keys64"].partition_broadcast(128).rearrange("p a b -> p (a b)")).then_inc(loads, 16)
                for d in range(DENSE):
                    sp.dma_start(ranks[:, d, 1, :], io["second_rank"].partition_broadcast(128).rearrange("p a b -> p (a b)")).then_inc(loads, 16)
                sp.dma_start(wq[:, :, :], io["me_wq"]).then_inc(loads, 16)
                sp.dma_start(wo[S:128, :, :], io["me_wo"]).then_inc(loads, 16)
                sp.dma_start(numbers[:, :], io["numbers"].partition_broadcast(128).rearrange("p a b -> p (a b)")).then_inc(loads, 16)
                sp.dma_start(first_row[:, :], io["first_row"].partition_broadcast(128).rearrange("p a b -> p (a b)")).then_inc(loads, 16)
                sp.dma_start(eye32[:, :], io["eye32"]).then_inc(loads, 16)
                for d in range(DENSE):
                    r = KEYS ** 2 * (GH + d)
                    sp.dma_start(tab[:, d], io["table"][r:r + KEYS ** 2, :].rearrange("(c r) k -> r c k", r=128)).then_inc(tab_loaded, 16)
                sp.wait_ge(loads, LOADS * 16)
                sp.wait_ge(tab_loaded, DENSE * 16)

            @block.gpsimd
            def _(pool):
                pool.memset(threshold[:, :], BIG * (TOP + 0.5)).then_inc(spread_made, 1)
                wait_for(m, pool, cls_posted, 1)
                for hd in range(HEADS):
                    for j in range(TOP // 4):
                        k = TOP // 4 * hd + j
                        pool.indirect_dma_start(got[:, 3 + k // TOP, k % TOP, :], None, io["table"],
                                                bass.IndirectOffsetOnAxis(rows_cls[:, hd, j:j + 1], 0)).then_inc(cls_gathered, 16)
                pool.wait_ge(folded, GROUPS_K)
                pool.wait_ge(spread_made, 2)
                with pool.Fori(0, TILES) as t:
                    gather(pool, t)

            @block.tensor
            def _(pe):
                pe.sem_inc(dense_turned, 1)
                wait_for(m, pe, loads, LOADS * 16)
                for g in range(GROUPS_K):
                    pe.matmul(bank[5 + g // 8][0:S, KEYS * (g % 8):KEYS * (g % 8) + KEYS], pk[:, 0, g, :], pk[:, 1, g, :]).then_inc(folded, 1)
                wait_for(m, pe, n["done"], 1)
                turn_tokens(pe, ident, xn, bank, tfull)
                wait_for(m, pe, fold_taken, 2)
                wait_for(m, pe, ttaken, NG)
                similarities(pe, 0, B)
                similarities(pe, 1, 128)
                similarities(pe, 2, 128)
                wait_for(m, pe, sim_ready, 3)
                wait_for(m, pe, cls_summed, 2)
                for hd in range(HEADS):
                    ins = pe.matmul(bank[KVB[0]][:, B * hd:B * hd + B], kv[:, hd, :], eye32[:, :])
                ins.then_inc(cls_turned, 1)
                wait_for(m, pe, cls_taken, 1)
                pe.wait_ge(tab_loaded, DENSE * 16)
                tensor_tile(pe, 0, attend=False)
                with pe.Fori(1, TILES - 2) as t:
                    tensor_tile(pe, t)
                tensor_tile(pe, TILES - 2, ahead=False)
                tensor_tile(pe, TILES - 1, ahead=False)
                tensor_scores(pe, TILES - 1)
                tensor_out(pe, TILES - 1, DENSE * TILES)

            @block.scalar
            def _(act):
                norm_scalar(act, n, 1, xn[:, :, :], sq[:, :, :], s)
                act.wait_ge(folded, GROUPS_K)
                for i in range(2):
                    act.activation(fold[:, 512 * i:512 * i + 512], bank[5 + i][0:S, :], ACT.Copy).then_inc(fold_taken, 1)
                take_turned(act, xt, bank, tfull, ttaken)
                act.wait_ge(ttaken, NG)
                act.activation(xtile[:, 0:B], xt[:, 0:TOK].rearrange("p (b t) -> p b t", t=T)[:, :, S], ACT.Copy).then_inc(x_ready, 1)
                copy_sim(act, 0, B)
                copy_x(act, 0)
                copy_sim(act, 1, 128)
                act.activation(minus[:, :], ident[:, :], ACT.Copy, scale=-1.0)
                act.activation(spread[:, :, :].rearrange("p c r -> p (c r)"), spread32, ACT.Copy).then_inc(spread_made, 1)
                exp_weights(act, 0, B)
                copy_x(act, 1)
                exp_weights(act, 1, 128)
                copy_sim(act, 2, 128)
                act.wait_ge(cls_turned, 1)
                act.activation(kvt_cls[:, :, :].rearrange("p h b -> p (h b)"), bank[KVB[0]][:, 0:B * HEADS], ACT.Copy).then_inc(cls_taken, 1)
                act.wait_ge(cls_taken, 1)
                act.wait_ge(spread_made, 2)
                scalar_tile(act, 0, attend=False)
                with act.Fori(1, TILES - 2) as t:
                    scalar_tile(act, t)
                scalar_tile(act, TILES - 2, ahead=False)
                scalar_tile(act, TILES - 1, ahead=False, choose_next=False)
                t = TILES - 1
                for i in range(2):
                    act.wait_ge(vo_full, 2 * t + i + 1)
                    act.activation(vo[:, 8 * i:8 * i + 8, :].rearrange("p u d -> p (u d)"), bank[KVB[i]][0:T, :], ACT.Copy).then_inc(vo_taken, 1)
                act.wait_ge(shifted, t + 1)
                act.activation(probs[:, :, :], probs[:, :, :], ACT.Exp).then_inc(exped, 1)
                for g, (u0, nu) in enumerate(UNIT_BANKS):
                    act.wait_ge(p_turned, 3 * t + g + 1)
                    act.activation(probs_t[:, u0:u0 + nu, :].rearrange("p u t -> p (u t)"), bank[ATT[g]][0:T, 0:T * nu], ACT.Copy)\
                       .then_inc(p_taken, 1)

            @block.vector
            def _(dve):
                link = Chain(dve, n["chain"])
                norm_vector(dve, n, 1, link, h[:, :, :], xn[:, :, :], sq[:, :, :], s)
                dve.wait_ge(loads, LOADS * 16)
                dve.sem_inc(out_added, 1)
                choose(dve, 0, B, 1)
                choose(dve, 0, B, 2)
                for q in range(4):
                    r, c = slice(B * q, B * q + B), slice(4 * q, 4 * q + 4)
                    dve.tensor_copy(wts_cls[r], best[0:B, :, c])
                    ins = dve.tensor_copy(rows_cls[r], rows_next[0:B, :, c])
                ins.then_inc(cls_posted, 1)
                dve.wait_ge(cls_posted, 1)
                dve.engine_nop().then_inc(slot_free, 3)
                choose(dve, 1, 128, 1)
                choose(dve, 1, 128, 2)
                post(dve, 1, 0)
                post(dve, 1, 1)
                dve.wait_ge(cls_gathered, 2 * 16 * TOP)
                for i in range(2):
                    hs = slice(4 * i, 4 * i + 4)
                    dve.tensor_tensor(prod.rearrange("p (h j) c -> p h j c", h=4),
                                      got[:, 3 + i].rearrange("p (h j) c -> p h j c", h=4), grow(wts_cls[:, hs, :], 3, 128), ALU.mult)\
                       .then_inc(slot_free, 1)
                    dve.wait_ge(slot_free, 4 + i)
                    dve.tensor_reduce(kv[:, hs, :], prod.rearrange("p (h j) c -> p h c j", h=4), AX.X, ALU.add).then_inc(cls_summed, 1)
                    dve.wait_ge(cls_summed, i + 1)
                dve.wait_ge(posted, 2)
                dve.wait_ge(cls_turned, 1)
                vector_tile(dve, 0, attend=False)
                with dve.Fori(1, TILES - 2) as t:
                    vector_tile(dve, t)
                vector_tile(dve, TILES - 2)
                vector_tile(dve, TILES - 1, choose_next=False)
                attend_a(dve, TILES - 1)
                attend_b(dve, TILES - 1)
                attend_c(dve, TILES - 1)


def program(nc, io, out):
    with ExitStack() as ctx:
        def sb(name, shape):
            return ctx.enter_context(nc.sbuf_tensor(name, shape, F32))

        m = {"h": sb("h", [T, B, S]), "waits": ctx.enter_context(nc.semaphore("waits"))}
        with ExitStack() as tower:
            def tsb(name, shape):
                return tower.enter_context(nc.sbuf_tensor(name, shape, F32))

            m["const"] = tsb("const", [128, CONST_COLS])
            m["mix1"] = tsb("mix1", [128, LAYERS, 128])
            m["mix2"] = tsb("mix2", [128, LAYERS, 128])
            m["dc1"] = tsb("dc1", [CH, LAYERS])
            m["dc2"] = tsb("dc2", [CH, LAYERS])
            m["q2col"] = tsb("q2col", [128, 1])
            m["head_w"] = tsb("head_w", [128, LAYERS, OG * NQ])
            m["qacc"] = tsb("qacc", [128, YH, B * S])
            m["spec"] = tsb("spec", [128, KYP, KX, B])
            m["inv_in"] = tsb("inv_in", [128, PAIRS, KY, CH])
            spectrum_of_input(nc, io, m)
            fourier_layers(nc, io, m)
            tower_head(nc, io, m)
        m["tok_const"] = sb("tok_const", [128, TOKC_COLS])
        m["xn"] = sb("xn", [T, B, S])
        m["sq"] = sb("sq", [T, B, S])
        m["stats"] = sb("stats", [T, 5 * B])
        m["xt"] = sb("xt", [S, KT * 128])
        release = ctx.enter_context(ExitStack())
        for name in ("probs", "probs_t"):
            m[name] = release.enter_context(nc.sbuf_tensor(name, [T, B, T], F32))
        latent_attention(nc, io, m)
        routed_feed_forward(nc, io, m)
        similarity_attention(nc, io, m)
        release.close()
        memory_attention(nc, io, m)
        store(nc, m, out)


def store(nc, m, out):
    with nc.semaphore("stored") as stored, nc.Block() as block:
        @block.sync
        def _(sp):
            h = m["h"]
            sp.dma_start(out[:, 1:T, :].rearrange("b t d -> t b d"), h[0:S, :, :]).then_inc(stored, 16)
            sp.dma_start(out[:, 0:1, :].rearrange("b t d -> t b d"), h[S:T, :, :]).then_inc(stored, 16)
            sp.wait_ge(stored, 32)


def laid_out(i):
    f = {k: np.asarray(v) for k, v in i.items()}
    ones = np.ones((1, B * S), np.float32)
    grid = np.tile(np.linspace(0.0, 1.0, S).astype(np.float32), B)[None]
    a = {"const": const_table()}
    a["xin"] = np.concatenate([f["x"][..., 0].transpose(2, 0, 1).reshape(S, -1), grid, ones, ones])
    p, pb = f["L0_tok_p_w"], f["L0_tok_p_b"]
    top = np.concatenate([np.repeat(p[:, 0:1], S, 1), p[:, 1:2], pb[:, None], p[:, 2:3]], 1)
    a["lift"] = np.concatenate([top, np.eye(67, dtype=np.float32)[65:66]])
    a["q1t"] = np.concatenate([f["L0_tok_q1_w"].T, f["L0_tok_q1_b"][None]])
    a["w2"] = f["L0_tok_w2_w"]
    a["w1t"] = f["L0_tok_w1_w"].transpose(0, 2, 1)
    a["w2t"] = f["L0_tok_w2_w"].transpose(0, 2, 1)
    a["b1t"] = f["L0_tok_w1_b"].T
    a["b2t"] = f["L0_tok_w2_b"].T
    a["lift_x"] = p[:, 0][None]
    a["lift_c"] = np.tile(np.stack([p[:, 1], p[:, 2], pb]), (4, 1))
    a["q2col"] = np.repeat(f["L0_tok_q2_w"][0], 32)[:, None]
    a["q2b"] = f["L0_tok_q2_b"][None]
    a["cls"] = f["cls_tok"][0]
    w = f["L0_tok_fw"].transpose(0, 6, 5, 2, 1, 4, 3)
    w = w.reshape(LAYERS, 2, KYP, 2, CH, KX, CH)
    w = w.transpose(0, 3, 1, 4, 2, 5, 6)
    w = np.stack([w, w[:, :, ::-1]], 6)
    a["mixw"] = w.reshape(LAYERS, 128, -1)
    a["tok_const"] = token_table()
    swap = np.arange(16).reshape(8, 2)[:, ::-1].reshape(-1)
    q, k = (np.concatenate([f["L0_attn_W" + x + "c"], f["L0_attn_W" + x + "r"], f["L0_attn_W" + x + "c"],
                            f["L0_attn_W" + x + "r"][:, swap]], 1) for x in "qk")
    a["la_up"] = np.concatenate([q, k, f["L0_attn_Wv"]], 1)
    a["la_down"] = np.stack([f["L0_attn_Wq_comp"].T, f["L0_attn_Wkv_comp"].T], 1)
    a["ff_wr"], a["ff_br"] = f["L0_ffn_wr"], f["L0_ffn_br"][None]
    a["ff_w1"], a["ff_w2"] = f["L0_ffn_w1"], f["L0_ffn_w2"]
    a["ff_b1"] = f["L0_ffn_b1"].reshape(2, 128).T
    a["ff_b2"] = f["L0_ffn_b2"][:, None]
    w = f["L1_ffn_Wq_pk"].reshape(S, GROUPS_K, 32)
    a["pk_w"] = w.transpose(2, 1, 0)
    a["pk_k"] = f["L1_ffn_pk_keys"].transpose(3, 0, 2, 1).reshape(32, GROUPS_K, KEYS)
    a["table"] = np.concatenate([f["L1_ffn_keys_table"], f["L1_ffn_values_table"]], 1)
    a["me_wq"] = f["L1_ffn_Wq"].reshape(S, HEADS, S)
    a["me_wo"] = f["L1_ffn_Wo"].reshape(HEADS, S, S).transpose(1, 0, 2)
    i1, i0 = np.divmod(np.arange(KEYS ** 2), KEYS)
    meet = np.arange(KEYS)[:, None]
    a["spread"] = np.concatenate([meet == i0, meet == i1]).astype(np.float32)
    a["keys64"] = np.arange(KEYS, dtype=np.float32)[None]
    a["second_rank"] = TOP - np.arange(TOP, dtype=np.float32)[None]
    a["numbers"] = np.arange(TOP, dtype=np.float32)[None]
    a["first_row"] = np.arange(HEADS, dtype=np.float32)[None] * KEYS ** 2
    a["eye32"] = np.tile(np.eye(B, dtype=np.float32), (4, 1))
    return {k: np.ascontiguousarray(v) for k, v in a.items()}


def kernel(**inputs):
    import concourse.bacc as bacc
    from concourse.bass_utils import run_bass_kernel_spmd

    nc = bacc.Bacc("TRN2", target_bir_lowering=False, num_devices=1)
    arrays = laid_out(inputs)
    io = {k: nc.dram_tensor("in_" + k, v.shape, mybir.dt.from_np(v.dtype), kind="ExternalInput").ap() for k, v in arrays.items()}
    out = nc.dram_tensor("out_h", (B, T, S), F32, kind="ExternalOutput").ap()
    program(nc, io, out)
    got = run_bass_kernel_spmd(nc, [{"in_" + k: v for k, v in arrays.items()}], core_ids=[0])
    return got.results[0]["out_h"]
```

```python
from contextlib import ExitStack

import numpy as np
import concourse.bass as bass
from concourse import mybir

F32 = mybir.dt.float32
U32 = mybir.dt.uint32
BF16 = mybir.dt.bfloat16
ALU = mybir.AluOpType
ACT = mybir.ActivationFunctionType
AX = mybir.AxisListType

B = 32
S = 64
CH = 32
LAYERS = 4
KY = 12
KX = 24
NQ = 4
T = S + 1
PAIRS = B // 2
CHUNKS = 4
PPC = PAIRS // CHUNKS
BPC = B // CHUNKS
OG = CH // 4
YH = 2
KYP = KY // 2
MODES = KYP * KX
N = BPC * S

CONSTS = {}


def _part(name, array):
    CONSTS[name] = np.asarray(array, np.float64)


def _tables():
    kx = np.array(list(range(KX // 2)) + list(range(S - KX // 2, S)))
    ky = np.arange(KY)
    px = np.arange(S)
    ax = 2 * np.pi * np.outer(kx, px) / S
    ay = 2 * np.pi * np.outer(ky, px) / S
    _part("ident", np.eye(128))
    ixr, ixi = np.zeros((128, 128)), np.zeros((128, 128))
    for b in range(2):
        r, c = slice(24 * b, 24 * b + 24), slice(64 * b, 64 * b + 64)
        ixr[r, c], ixi[r, c] = np.cos(ax), np.sin(ax)
        r = slice(64 + 24 * b, 64 + 24 * b + 24)
        ixr[r, c], ixi[r, c] = -np.sin(ax), np.cos(ax)
    _part("inv_x_re", ixr)
    _part("inv_x_im", ixi)
    w = np.where(ky == 0, 1.0, 2.0)[:, None] / S
    for h in range(YH):
        ys = slice(32 * h, 32 * h + 32)
        inv, fwd = np.zeros((96, 128)), np.zeros((128, 96))
        for o in range(4):
            inv[24 * o:24 * o + 12, 32 * o:32 * o + 32] = (w * np.cos(ay))[:, ys]
            inv[24 * o + 12:24 * o + 24, 32 * o:32 * o + 32] = (-w * np.sin(ay))[:, ys]
            fwd[32 * o:32 * o + 32, 24 * o:24 * o + 12] = np.cos(ay)[:, ys].T / S
            fwd[32 * o:32 * o + 32, 24 * o + 12:24 * o + 24] = -np.sin(ay)[:, ys].T / S
        _part(f"inv_y{h}", inv)
        _part(f"fwd_y{h}", fwd)
    _part("fwd_y_in", np.concatenate([np.cos(ay).T, -np.sin(ay).T], 1) / S)
    cos, sin = np.zeros((128, 64)), np.zeros((128, 64))
    for b in range(2):
        cos[64 * b:64 * b + 64, 32 * b:32 * b + 24] = np.cos(ax).T
        sin[64 * b:64 * b + 64, 32 * b:32 * b + 24] = np.sin(ax).T
    _part("fwd_x_cos", cos)
    _part("fwd_x_sin", sin)
    _part("fwd_x_nsin", -sin)
    _part("eye32", np.tile(np.eye(32), (4, 1)))
    grid = np.linspace(0.0, 1.0, S).astype(np.float32)
    for h in range(YH):
        m = np.zeros((67, 32))
        m[32 * h:32 * h + 32] = np.eye(32)
        m[64:66] = 1.0
        m[66] = grid[32 * h:32 * h + 32]
        _part(f"base{h}", m)
    sign = np.ones((128, 1))
    sign[32:64] = sign[96:128] = -1.0
    _part("sign", sign)
    sel = np.zeros((24, KYP, 2, 2))
    for p in range(KYP):
        for m in range(2):
            for c in range(2):
                sel[12 * c + 2 * p + m, p, m, c] = 1.0
    _part("pick_mode", sel.reshape(24, -1))
    _part("pick_part", np.kron(np.eye(4), np.ones((3, 1))))
    one = np.ones(S)
    fy = np.exp(-1j * ay) / S
    fx = np.exp(-1j * ax)
    gx = np.outer(fx @ grid, fy @ one)
    gy = np.outer(fx @ one, fy @ grid)
    g1 = np.outer(fx @ one, fy @ one)
    k = np.zeros((2, 2, 3, KYP, KX))
    for m in range(2):
        for j, g in enumerate((gx, gy, g1)):
            k[m, 0, j] = g.real[:, m::2].T
            k[m, 1, j] = g.imag[:, m::2].T
    _part("coords_hat", k.reshape(12, -1))


_tables()
COL = {}
_at = 0
for _n, _a in CONSTS.items():
    COL[_n] = (_at, _a.shape[0], _a.shape[1])
    _at += _a.shape[1]
CONST_COLS = _at


def const_table():
    t = np.zeros((128, CONST_COLS), np.float32)
    for n, a in CONSTS.items():
        c, r, w = COL[n]
        t[:r, c:c + w] = a
    return t


def grow(ap, axis, n):
    shape = list(ap.shape)
    return ap.unsqueeze(axis).to_broadcast(shape[:axis] + [n] + shape[axis:])


def wait_for(m, eng, sem, value):
    eng.wait_ge(sem, value)
    if not isinstance(value, int):
        eng.sem_inc(m["waits"], 1)


def spectrum_of_input(nc, io, m):
    with ExitStack() as ctx:
        def sb(name, shape):
            return ctx.enter_context(nc.sbuf_tensor(name, shape, F32))

        def sem(name):
            return ctx.enter_context(nc.semaphore(name))

        cst = m["const"]
        xin = sb("xin", [67, B * S])
        w2raw = sb("w2raw", [CH, LAYERS, CH])
        w2wide = sb("w2wide", [CH, LAYERS, CH, 32])
        q1t = sb("q1t", [CH + 1, NQ])
        lift = sb("lift", [CH + 1, 67])
        b2all = sb("b2all", [CH, LAYERS])
        b2sum = sb("b2sum", [CH, 1])
        head_in = sb("head_in", [67, NQ])
        base = sb("base", [67, YH, NQ, 32])
        lift_x = sb("lift_x", [24, CH])
        lift_c = sb("lift_c", [12, CH])
        pick_x = sb("pick_x", [24, KYP, 4, CH])
        pick_c = sb("pick_c", [12, 4, CH])
        a0 = sb("a0", [24, B * S])
        a0t = sb("a0t", [128, PAIRS, 2, KY])
        x0 = sb("x0", [64, PAIRS, 2, KY])
        x0t = sb("x0t", [24, KX, B])
        bank = [ctx.enter_context(nc.psum_tensor(f"prep_bank{i}", [128, 512], F32)) for i in range(2)]

        loads = sem("small_loads")
        zeroed = sem("mixers_zeroed")
        blocks = sem("mixer_blocks_loaded")
        filled = sem("prep_bank_filled")
        taken = sem("prep_bank_taken")
        made = sem("prep_weights_made")
        SMALL = 11

        HEAD_IN, HEAD_W, SHARE, FWD_Y, TURN_X, FWD_X, TURN_K, SPREAD = 0, 1, 2, 10, 14, 15, 17, 19

        with nc.Block() as block:
            @block.sync
            def _(sp):
                sp.dma_start(cst[:, :], io["const"]).then_inc(loads, 16)
                sp.dma_start(xin[:, :], io["xin"]).then_inc(loads, 16)
                sp.dma_start(lift[:, :], io["lift"]).then_inc(loads, 16)
                sp.dma_start(q1t[:, :], io["q1t"]).then_inc(loads, 16)
                sp.dma_start(w2raw[:, :, :], io["w2"].rearrange("l p o -> p l o")).then_inc(loads, 16)
                sp.dma_start(b2all[:, :], io["b2t"]).then_inc(loads, 16)
                sp.dma_start(lift_x[:, :], io["lift_x"].partition_broadcast(24).rearrange("p a o -> p (a o)")).then_inc(loads, 16)
                sp.dma_start(lift_c[:, :], io["lift_c"]).then_inc(loads, 16)
                sp.dma_start(m["dc1"][:, :], io["b1t"]).then_inc(loads, 16)
                sp.dma_start(m["dc2"][:, :], io["b2t"]).then_inc(loads, 16)
                sp.dma_start(m["q2col"][:, :], io["q2col"]).then_inc(loads, 16)
                sp.wait_ge(zeroed, 1)
                for i in range(4):
                    r = slice(32 * i, 32 * i + 32)
                    sp.dma_start(m["mix1"][r, :, r], io["w1t"].rearrange("l p o -> p l o")).then_inc(blocks, 16)
                    sp.dma_start(m["mix2"][r, :, r], io["w2t"].rearrange("l p o -> p l o")).then_inc(blocks, 16)
                load_mixing_weights(sp, io, m, 0)
                sp.wait_ge(loads, 16 * SMALL)
                sp.wait_ge(blocks, 16 * 8)

            @block.gpsimd
            def _(pool):
                nc.gpsimd.memset(m["mix1"][:, :, :], 0.0)
                nc.gpsimd.memset(m["inv_in"][:, :, :, :], 0.0)
                nc.gpsimd.memset(m["mix2"][:, :, :], 0.0).then_inc(zeroed, 1)
                pool.wait_ge(loads, 16 * SMALL)
                pool.wait_ge(m["weights_in"], 16)
                sign_mixing_weights(pool, m)

            @block.tensor
            def _(pe):
                pe.wait_ge(loads, 16 * SMALL)
                pe.wait_ge(made, 2)
                pe.matmul(bank[HEAD_IN % 2][0:67, 0:NQ], lift[:, :], q1t[:, :]).then_inc(filled, 1)
                for l in range(LAYERS):
                    for g in range(OG):
                        c = (l * OG + g) * NQ
                        ins = pe.matmul(bank[HEAD_W % 2][:, c:c + NQ], w2wide[:, l, 4 * g:4 * g + 4].rearrange("p o y -> p (o y)"), q1t[0:CH, :])
                ins.then_inc(filled, 1)
                pe.wait_ge(made, 4)
                for h in range(YH):
                    for n in range(4):
                        step = SHARE + 4 * h + n
                        pe.wait_ge(taken, step - 1)
                        pe.matmul(bank[step % 2][:, :], base[:, h].rearrange("p q y -> p (q y)"), xin[:, 512 * n:512 * n + 512])\
                          .then_inc(filled, 1)
                c, r, w = COL["fwd_y_in"]
                for n in range(4):
                    step = FWD_Y + n
                    pe.wait_ge(taken, step - 1)
                    pe.matmul(bank[step % 2][0:24, :], cst[0:64, c:c + w], xin[0:64, 512 * n:512 * n + 512]).then_inc(filled, 1)
                pe.wait_ge(taken, TURN_X)
                for q in range(PAIRS):
                    ins = pe.transpose(bank[TURN_X % 2][:, 24 * q:24 * q + 24], a0[:, 128 * q:128 * q + 128], cst[0:24, 0:24])
                ins.then_inc(filled, 1)
                pe.wait_ge(taken, FWD_X)
                for part, names in enumerate(((("fwd_x_cos", 0), ("fwd_x_sin", 1)), (("fwd_x_cos", 1), ("fwd_x_nsin", 0)))):
                    for i, (name, src) in enumerate(names):
                        k = COL[name][0]
                        ins = pe.matmul(bank[(FWD_X + part) % 2][0:64, 0:PAIRS * KY], cst[:, k:k + 64], a0t[:, :, src, :],
                                        start=(i == 0), stop=(i == 1))
                    ins.then_inc(filled, 1)
                pe.wait_ge(taken, TURN_K)
                for half in range(2):
                    for q in range(8):
                        ins = pe.transpose(bank[(TURN_K + half) % 2][0:24, 64 * q:64 * q + 64],
                                           x0[0:64, 8 * half + q].rearrange("p c k -> p (c k)"), cst[0:64, 0:64])
                    ins.then_inc(filled, 1)
                pe.wait_ge(taken, SPREAD)
                k = COL["coords_hat"][0]
                for y in range(KYP):
                    for half in range(2):
                        step = SPREAD + 2 * y + half
                        pe.wait_ge(taken, step - 1)
                        pe.matmul(bank[step % 2][:, 0:384], pick_x[:, y].rearrange("p a o -> p (a o)"),
                                  x0t[:, 12 * half:12 * half + 12, :].rearrange("p k b -> p (k b)"), start=True, stop=False)
                        kk = k + y * KX + 12 * half
                        pe.matmul(bank[step % 2][:, 0:384], pick_c[:, :, :].rearrange("p a o -> p (a o)"),
                                  grow(cst[0:12, kk:kk + 12], 2, B), start=False, stop=True).then_inc(filled, 1)

            @block.vector
            def _(dve):
                dve.wait_ge(loads, 16 * SMALL)
                dve.tensor_reduce(b2sum[:, :], b2all[:, :], AX.X, ALU.add).then_inc(made, 1)
                dve.wait_ge(made, 1)
                dve.tensor_copy(w2wide[:, :, :, :].rearrange("p l o y -> p (l o) y"),
                                grow(w2raw[:, :, :].rearrange("p l o -> p (l o)"), 2, 32))
                dve.tensor_tensor(lift[0:CH, 65:66], lift[0:CH, 65:66], b2sum[:, :], ALU.add).then_inc(made, 1)
                dve.wait_ge(filled, HEAD_IN + 1)
                dve.tensor_copy(head_in[:, :], bank[HEAD_IN % 2][0:67, 0:NQ]).then_inc(taken, 1)
                dve.wait_ge(taken, 1)
                for h in range(YH):
                    c = COL[f"base{h}"][0]
                    ins = dve.tensor_tensor(base[:, h], grow(cst[0:67, c:c + 32], 1, NQ), grow(head_in[:, :], 2, 32), ALU.mult)
                ins.then_inc(made, 1)
                c = COL["pick_mode"][0]
                dve.tensor_tensor(pick_x[:, :, :, :].rearrange("p y a o -> p (y a) o"),
                                  grow(cst[0:24, c:c + 24], 2, CH), grow(lift_x[:, :], 1, 24), ALU.mult)
                c = COL["pick_part"][0]
                dve.tensor_tensor(pick_c[:, :, :], grow(cst[0:12, c:c + 4], 2, CH), grow(lift_c[:, :], 1, 4), ALU.mult).then_inc(made, 1)
                dve.wait_ge(filled, HEAD_W + 1)
                dve.tensor_copy(m["head_w"][:, :, :], bank[HEAD_W % 2][:, 0:128].rearrange("p (l c) -> p l c", l=LAYERS)).then_inc(taken, 1)
                for h in range(YH):
                    for n in range(4):
                        step = SHARE + 4 * h + n
                        dve.wait_ge(filled, step + 1)
                        dve.tensor_copy(m["qacc"][:, h, 512 * n:512 * n + 512], bank[step % 2][:, :]).then_inc(taken, 1)
                for n in range(4):
                    step = FWD_Y + n
                    dve.wait_ge(filled, step + 1)
                    dve.tensor_copy(a0[:, 512 * n:512 * n + 512], bank[step % 2][0:24, :]).then_inc(taken, 1)
                dve.wait_ge(filled, TURN_X + 1)
                dve.tensor_copy(a0t[:, :, :, :].rearrange("p q c k -> p (q c k)"), bank[TURN_X % 2][:, 0:384]).then_inc(taken, 1)
                for part in range(2):
                    dve.wait_ge(filled, FWD_X + part + 1)
                    dve.tensor_copy(x0[:, :, part, :], bank[(FWD_X + part) % 2][0:64, 0:PAIRS * KY].rearrange("p (q k) -> p q k", k=KY))\
                       .then_inc(taken, 1)
                for half in range(2):
                    dve.wait_ge(filled, TURN_K + half + 1)
                    dve.tensor_copy(x0t[:, :, 16 * half:16 * half + 16],
                                    bank[(TURN_K + half) % 2][0:24, :].rearrange("p (b k) -> p k b", k=32)[:, 0:KX]).then_inc(taken, 1)
                for y in range(KYP):
                    for half in range(2):
                        step = SPREAD + 2 * y + half
                        dve.wait_ge(filled, step + 1)
                        dve.tensor_copy(m["spec"][:, y, 12 * half:12 * half + 12, :].rearrange("p k b -> p (k b)"), bank[step % 2][:, 0:384])\
                           .then_inc(taken, 1)


BLOCKS = 12
BM = MODES // BLOCKS
BN = BM * B
PLAN_MIX, PLAN_TURN = 2 * BLOCKS, 2 * PAIRS
HEADPART = PLAN_MIX + BLOCKS + PLAN_TURN
LEAD = 16
FULL, SHORT = 40, 32
TAIL = BLOCKS
ITEMS = HEADPART + CHUNKS * FULL + TAIL
ACT_ITEMS = (HEADPART + 1) // 2 + CHUNKS * FULL // 2
DVE_ITEMS = ITEMS - ACT_ITEMS


def by_act(j):
    return j // 2 + 1


def by_dve(j):
    return (j + 1) // 2


def load_mixing_weights(sp, io, m, l):
    src = io["mixw"][bass.ds(l, 1)].rearrange("l p m -> p (l m)")
    sp.dma_start(m["mixw"][:, :, :, :].rearrange("p m c o -> p (m c o)"), src).then_inc(m["weights_in"], 16)


def sign_mixing_weights(pool, m):
    c = COL["sign"][0]
    real = m["mixw"][:, :, 0, :]
    pool.tensor_scalar(real, real, m["const"][:, c:c + 1], None, ALU.mult).then_inc(m["signed"], 1)


def fourier_layers(nc, io, m):
    with ExitStack() as ctx:
        def sb(name, shape):
            return ctx.enter_context(nc.sbuf_tensor(name, shape, F32))

        def sem(name):
            return ctx.enter_context(nc.semaphore(name))

        cst, spec, inv_in, qacc = m["const"], m["spec"], m["inv_in"], m["qacc"]
        mixw = m["mixw"]
        g = sb("mixed", [128, MODES * B])
        g2 = sb("mixed_w1", [128, MODES * B])
        z = sb("z", [128, PPC, CH, 2, KY])
        zt = sb("zt", [96, OG, N])
        r = sb("relu", [128, 4, N])
        at = sb("act_t", [128, PPC, OG * 4, 2, KY])
        fx = sb("act_x", [128, 2, KY, 2, CH])
        w1 = sb("w1_now", [128, 128])
        w2 = sb("w2_now", [128, 128])
        hw = sb("head_now", [128, OG * NQ, 32])
        dc = sb("dc_now", [CH, 2])
        bank = [ctx.enter_context(nc.psum_tensor(f"bank{i}", [128, 512], F32)) for i in range(8)]
        qb, yb, ring = bank[0:2], bank[2:4], bank[4:8]

        weights_in, signed = m["weights_in"], m["signed"]
        ready = sem("layer_weights_ready")
        full = sem("ring_filled")
        ta = sem("ring_taken_by_act")
        td = sem("ring_taken_by_dve")
        dc_in = sem("dc_bias_added")
        y_full = sem("fwd_y_filled")
        ya = sem("fwd_y_taken_by_act")
        yd = sem("fwd_y_taken_by_dve")
        q_full = sem("head_filled")
        q_in = sem("head_added")

        gv = g2[:, :].rearrange("p (k b x) -> p k b x", k=KYP, b=B)
        ft = g[:, :].rearrange("p (k x b) -> p k x b", k=KYP, b=B)
        specf = spec[:, :, :, :].rearrange("p k x b -> p (k x b)")
        mixf = mixw[:, :, :, :].rearrange("p m c o -> p m (c o)")

        def C(name, rows=128):
            c, _, w = COL[name]
            return cst[0:rows, c:c + w]

        def bases(l):
            return l * ITEMS, l * ACT_ITEMS + 1, l * DVE_ITEMS + 1

        def chunk_bases(l, ch, size):
            f, a, d = bases(l)
            j = HEADPART + LEAD
            return f + j + ch * size, a + by_act(j - 1) + ch * (size // 2), d + by_dve(j - 1) + ch * (size // 2)

        def pe_layer(pe, l, last):
            f, a, d = bases(l)

            def taken(j, a=a, d=d):
                wait_for(m, pe, ta, a + by_act(j))
                if j > 0:
                    wait_for(m, pe, td, d + by_dve(j))

            def slot(j, a=a, d=d):
                if j < 4:
                    if j == 0:
                        wait_for(m, pe, ta, a)
                        wait_for(m, pe, td, d)
                elif j % 2 == 0:
                    wait_for(m, pe, ta, a + by_act(j - 4))
                else:
                    wait_for(m, pe, td, d + by_dve(j - 4))

            wait_for(m, pe, signed, l + 1)
            wait_for(m, pe, ready, l + 1)
            j = 0
            for blk in range(BLOCKS):
                slot(j)
                slot(j + 1)
                for i in range(BM):
                    mode = BM * blk + i
                    for mem in range(2):
                        rows = slice(64 * mem, 64 * mem + 64)
                        ins = pe.matmul(ring[(j + mem) % 4][rows, B * i:B * i + B], mixf[rows, mode], specf[rows, B * mode:B * mode + B])
                        if i == BM - 1:
                            ins.then_inc(full, 1)
                j += 2
            for blk in range(BLOCKS):
                slot(j)
                taken(2 * blk + 1)
                ins = pe.matmul(ring[j % 4][:, 0:BN], w1[:, :], g[:, BN * blk:BN * blk + BN])
                ins.then_inc(full, 1)
                j += 1
            taken(j - 1)
            wait_for(m, pe, dc_in, 2 * l + 2)
            for p in range(PAIRS):
                for half in range(2):
                    slot(j)
                    for i in range(3):
                        ins = pe.transpose(ring[j % 4][0:48, 128 * i:128 * i + 128],
                                           gv[:, 3 * half + i, 2 * p:2 * p + 2, :].rearrange("p b x -> p (b x)"), C("ident"))
                    ins.then_inc(full, 1)
                    j += 1
            assert j == HEADPART
            size = SHORT if last else FULL
            w = ring_waits(pe, *chunk_bases(l, 0, size)[1:])
            inverse_x(pe, w, -LEAD, 0)
            turn_z(pe, w, -LEAD // 2, -LEAD // 2 - 1)
            with pe.Fori(0, CHUNKS - 1) as ch:
                pe_chunk(pe, l, ch, last, size, True)
            pe_chunk(pe, l, CHUNKS - 1, last, size, False)
            if last:
                return
            fc, ac, dcount = after_chunks(l)
            wait_for(m, pe, ta, ac)
            wait_for(m, pe, td, dcount)
            for blk in range(TAIL):
                if blk >= 4:
                    wait_for(m, pe, td, dcount + blk - 3)
                pe.matmul(ring[blk % 4][:, 0:BN], w2[:, :], g[:, BN * blk:BN * blk + BN]).then_inc(full, 1)

        def ring_waits(pe, a, d):
            def taken(j):
                wait_for(m, pe, ta, a + by_act(j))
                wait_for(m, pe, td, d + by_dve(j))

            def slot(j):
                if j % 2 == 0:
                    wait_for(m, pe, ta, a + by_act(j - 4))
                else:
                    wait_for(m, pe, td, d + by_dve(j - 4))

            return taken, slot

        def inverse_x(pe, w, j, ch):
            for p in range(PPC):
                rhs = inv_in[0:112, bass.ds(ch * PPC + p, 1)].rearrange("p a k o -> p (a k o)")
                for c in range(2):
                    w[1](j)
                    pe.matmul(ring[j % 4][:, 0:384], C("inv_x_im" if c else "inv_x_re", 112), rhs).then_inc(full, 1)
                    j += 1

        def turn_z(pe, w, j, z_last):
            w[0](z_last)
            for og in range(OG):
                w[1](j)
                for p in range(PPC):
                    ins = pe.transpose(ring[j % 4][0:96, 128 * p:128 * p + 128],
                                       z[:, p, 4 * og:4 * og + 4].rearrange("p o c k -> p (o c k)"), C("ident"))
                ins.then_inc(full, 1)
                j += 1

        def after_chunks(l):
            f, a, d = bases(l)
            j = HEADPART + CHUNKS * FULL
            return f + j, a + by_act(j - 1), d + by_dve(j - 1)

        def pe_chunk(pe, l, ch, last, size, ahead):
            f, a, d = chunk_bases(l, ch, size)
            n = l * CHUNKS + ch
            w = taken, slot = ring_waits(pe, a, d)

            def b(j):
                return ring[j % 4]

            def inv_y(k):
                slot(k)
                if k % 2 == 0:
                    taken(k // 2 - 8)
                pe.matmul(b(k)[:, :], C(f"inv_y{k % 2}", 96), zt[:, k // 2]).then_inc(full, 1)

            wait_for(m, pe, q_in, 2 * n + 1)
            inv_y(0)
            inv_y(1)
            for k in range(2 * OG):
                if k + 2 < 2 * OG:
                    inv_y(k + 2)
                og, h = k // 2, k % 2
                taken(k)
                ins = pe.matmul(qb[h][:, :], hw[:, NQ * og:NQ * og + NQ].rearrange("p q y -> p (q y)"), r[:, k % 4],
                                start=(og == 0), stop=(og == OG - 1))
                if og == OG - 1:
                    ins.then_inc(q_full, 1)
                if not last:
                    if h == 0 and og >= 2:
                        wait_for(m, pe, ya if og % 2 == 0 else yd, (l * CHUNKS + ch) * 4 + og // 2)
                    for p in range(PPC):
                        ins = pe.matmul(yb[og % 2][:, 96 * p:96 * p + 96], r[:, k % 4, 128 * p:128 * p + 128], C(f"fwd_y{h}"),
                                        start=(h == 0 and p == 0), stop=(h == 1 and p == PPC - 1))
                    if h == 1:
                        ins.then_inc(y_full, 1)
            j = 2 * OG
            z_last = j + 7
            if ahead:
                inverse_x(pe, w, j, ch + 1)
                j += 8
            if last:
                if ahead:
                    turn_z(pe, w, j, z_last)
                return
            wait_for(m, pe, ya, n * 4 + 4)
            wait_for(m, pe, yd, n * 4 + 4)
            for pp in range(2):
                for c in range(2):
                    slot(j)
                    names = ("fwd_x_cos", "fwd_x_sin") if c == 0 else ("fwd_x_nsin", "fwd_x_cos")
                    for src in range(2):
                        for mem in range(2):
                            ins = pe.matmul(b(j)[64 * mem:64 * mem + 64, 0:384], C(names[src]),
                                            at[:, 2 * pp + mem, :, src, :], start=(src == 0), stop=(src == 1))
                    ins.then_inc(full, 1)
                    j += 1
            fx_first = j - 4
            if ahead:
                turn_z(pe, w, j, z_last)
                j += 8
            for pp in range(2):
                taken(fx_first + 2 * pp + 1)
                for half in range(2):
                    slot(j)
                    for i in range(3):
                        k = 2 * (3 * half + i)
                        ins = pe.transpose(b(j)[:, 128 * i:128 * i + 128],
                                           fx[:, pp, k:k + 2].rearrange("p k c o -> p (k c o)"), C("ident"))
                    ins.then_inc(full, 1)
                    j += 1
            assert j == FULL or not ahead

        def take_layer(e, copy, relu, me, l, last):
            done = (ta, td)[me]
            f, a, d = bases(l)

            def item(j, steps, f=f):
                if j % 2 != me:
                    return
                e.wait_ge(full, f + j + 1)
                for s in steps[:-1]:
                    s()
                steps[-1]().then_inc(done, 1)

            j = 0
            for blk in range(BLOCKS):
                for mem in range(2):
                    rows = slice(64 * mem, 64 * mem + 64)
                    item(j, [lambda j=j, rows=rows, blk=blk: copy(g[rows, BN * blk:BN * blk + BN], ring[j % 4][rows, 0:BN])])
                    j += 1
            for blk in range(BLOCKS):
                item(j, [lambda j=j, blk=blk: copy(
                    gv[:, blk // 2, :, BM * (blk % 2):BM * (blk % 2) + BM].rearrange("p b x -> p x b"),
                    ring[j % 4][:, 0:BN].rearrange("p (x b) -> p x b", b=B))])
                if blk == 0 and me == 1:
                    e.wait_ge(ta, a + by_act(j))
                    e.wait_ge(ready, l + 1)
                    e.tensor_scalar(gv[0:CH, 0, :, 0], gv[0:CH, 0, :, 0], dc[:, 0:1], None, ALU.add).then_inc(dc_in, 1)
                j += 1
            for p in range(PAIRS):
                for half in range(2):
                    steps = []
                    for c in range(2):
                        steps.append(lambda j=j, c=c, p=p, half=half: copy(
                            inv_in[64 * c:64 * c + 48, p, 6 * half:6 * half + 6, :],
                            ring[j % 4][0:48, 0:384].rearrange("p (k c o) -> p k c o", c=2, o=CH)[:, :, c, :]))
                    item(j, steps)
                    j += 1
            size = SHORT if last else FULL
            f0 = chunk_bases(l, 0, size)[0]
            take_z(e, copy, me, f0, -LEAD)
            take_zt(e, copy, me, f0, -LEAD // 2)
            with e.Fori(0, CHUNKS - 1) as ch:
                take_chunk(e, copy, relu, me, l, ch, last, size, True)
            take_chunk(e, copy, relu, me, l, CHUNKS - 1, last, size, False)
            if last or me == 0:
                return
            fc, ac, dcount = after_chunks(l)
            for blk in range(TAIL):
                e.wait_ge(full, fc + blk + 1)
                e.tensor_tensor(specf[:, BN * blk:BN * blk + BN], ring[blk % 4][:, 0:BN],
                                specf[:, BN * blk:BN * blk + BN], ALU.add).then_inc(td, 1)
            e.wait_ge(td, dcount + 1)
            e.tensor_scalar(specf[0:CH, 0:B], specf[0:CH, 0:B], dc[:, 1:2], None, ALU.add).then_inc(dc_in, 1)

        def take_z(e, copy, me, f, j):
            for p in range(PPC):
                for c in range(2):
                    if j % 2 == me:
                        e.wait_ge(full, f + j + 1)
                        copy(z[:, p, :, c, :].rearrange("p o k -> p k o"),
                             ring[j % 4][:, 0:384].rearrange("p (k o) -> p k o", o=CH)).then_inc((ta, td)[me], 1)
                    j += 1

        def take_zt(e, copy, me, f, j):
            for og in range(OG):
                if j % 2 == me:
                    e.wait_ge(full, f + j + 1)
                    copy(zt[:, og], ring[j % 4][0:96, :]).then_inc((ta, td)[me], 1)
                j += 1

        def take_chunk(e, copy, relu, me, l, ch, last, size, ahead):
            f, a, d = chunk_bases(l, ch, size)
            done = (ta, td)[me]
            n = l * CHUNKS + ch

            def b(j):
                return ring[j % 4]

            def item(j, step):
                if j % 2 != me:
                    return
                e.wait_ge(full, f + j + 1)
                step().then_inc(done, 1)

            j = 0

            def take_y(og):
                if last or og % 2 != me:
                    return
                e.wait_ge(y_full, n * OG + og + 1)
                copy(at[:, :, 4 * og:4 * og + 4].rearrange("p q o c k -> p q (o c k)"),
                     yb[og % 2][:, 0:384].rearrange("p (q n) -> p q n", q=PPC)).then_inc((ya, yd)[me], 1)

            for k in range(2 * OG):
                item(j, lambda: relu(r[:, k % 4], b(j)[:, :]))
                j += 1
                if k % 2 == 1 and k >= 3:
                    take_y(k // 2 - 1)
            take_y(OG - 1)
            if me == 1:
                for h in range(2):
                    e.wait_ge(q_full, 2 * n + h + 1)
                    e.tensor_tensor(qacc[:, h, bass.ds(ch * N, N)], qb[h][:, :], qacc[:, h, bass.ds(ch * N, N)],
                                    ALU.add).then_inc(q_in, 1)
            if ahead:
                take_z(e, copy, me, f, j)
                j += 8
            if last:
                if ahead:
                    take_zt(e, copy, me, f, j)
                return
            for pp in range(2):
                for c in range(2):
                    item(j, lambda: copy(fx[:, pp, :, c, :].rearrange("p k o -> p o k"),
                                         b(j)[:, 0:384].rearrange("p (o k) -> p o k", k=KY)))
                    j += 1
            if ahead:
                take_zt(e, copy, me, f, j)
                j += 8
            for pp in range(2):
                for half in range(2):
                    item(j, lambda: copy(
                        ft[:, 3 * half:3 * half + 3, :, bass.ds(ch * BPC + 4 * pp, 4)].rearrange("p k x b -> p k b x"),
                        b(j)[:, 0:384].rearrange("p (k b x) -> p k b x", k=3, b=4)[:, :, :, 0:KX]))
                    j += 1

        with nc.Block() as block:
            @block.sync
            def _(sp):
                with sp.Fori(1, LAYERS) as l:
                    sp.wait_ge(full, (l - 1) * ITEMS + PLAN_MIX)
                    load_mixing_weights(sp, io, m, l)

            @block.gpsimd
            def _(pool):
                with pool.Fori(1, LAYERS) as l:
                    wait_for(m, pool, weights_in, 16 * l + 16)
                    sign_mixing_weights(pool, m)

            @block.tensor
            def _(pe):
                with pe.Fori(0, LAYERS - 1) as l:
                    pe_layer(pe, l, False)
                pe_layer(pe, LAYERS - 1, True)

            @block.scalar
            def _(act):
                def copy(o, i):
                    return act.activation(o, i, ACT.Copy)

                def relu(o, i):
                    return act.activation(o, i, ACT.Relu)

                act.sem_inc(ta, 1)
                with act.Fori(0, LAYERS - 1) as l:
                    take_layer(act, copy, relu, 0, l, False)
                take_layer(act, copy, relu, 0, LAYERS - 1, True)

            @block.vector
            def _(dve):
                def relu(o, i):
                    return dve.tensor_scalar(o, i, 0.0, None, ALU.max)

                def small_weights(l):
                    at_l = bass.ds(l, 1)
                    dve.wait_ge(dc_in, 2 * l + 1)
                    dve.tensor_copy(w1[:, :], m["mix1"][:, at_l, :].rearrange("p l o -> p (l o)"))
                    dve.tensor_copy(w2[:, :], m["mix2"][:, at_l, :].rearrange("p l o -> p (l o)"))
                    dve.tensor_scalar(dc[:, 0:1], m["dc1"][:, at_l], float(S), None, ALU.mult)
                    dve.tensor_scalar(dc[:, 1:2], m["dc2"][:, at_l], float(S), None, ALU.mult)
                    dve.tensor_tensor(hw[:, :, :], grow(C("eye32"), 1, OG * NQ),
                                      grow(m["head_w"][:, at_l, :].rearrange("p l c -> p (l c)"), 2, 32), ALU.mult).then_inc(ready, 1)

                for start_at_one in (td, dc_in, q_in):
                    dve.sem_inc(start_at_one, 1)
                with dve.Fori(0, LAYERS - 1) as l:
                    small_weights(l)
                    take_layer(dve, dve.tensor_copy, relu, 1, l, False)
                small_weights(LAYERS - 1)
                take_layer(dve, dve.tensor_copy, relu, 1, LAYERS - 1, True)


def tower_head(nc, io, m):
    with ExitStack() as ctx:
        h, qacc = m["h"], m["qacc"]
        wq = ctx.enter_context(nc.sbuf_tensor("head_out_w", [128, 32], F32))
        q2b = ctx.enter_context(nc.sbuf_tensor("q2b", [S, 1], F32))
        bank = [ctx.enter_context(nc.psum_tensor(f"tok{i}", [128, 512], F32)) for i in range(4)]
        loads = ctx.enter_context(nc.semaphore("head_loads"))
        wready = ctx.enter_context(nc.semaphore("head_w_ready"))
        relued = ctx.enter_context(nc.semaphore("head_relued"))
        full = ctx.enter_context(nc.semaphore("tok_filled"))
        taken = ctx.enter_context(nc.semaphore("tok_taken"))
        with nc.Block() as block:
            @block.sync
            def _(sp):
                sp.dma_start(q2b[:, :], io["q2b"].partition_broadcast(S).rearrange("p a b -> p (a b)")).then_inc(loads, 16)
                sp.dma_start(h[S:T, :, :], grow(io["cls"], 1, B)).then_inc(loads, 16)
                sp.wait_ge(loads, 32)

            @block.vector
            def _(dve):
                c = COL["eye32"][0]
                dve.tensor_scalar(wq[:, :], m["const"][:, c:c + 32], m["q2col"][:, 0:1], None, ALU.mult).then_inc(wready, 1)
                for i in range(4):
                    cols = slice(512 * i, 512 * i + 512)
                    dve.tensor_scalar(qacc[:, :, cols], qacc[:, :, cols], 0.0, None, ALU.max).then_inc(relued, 1)
                dve.wait_ge(loads, 32)
                for i in range(4):
                    dve.wait_ge(full, i + 1)
                    dve.tensor_scalar(h[0:S, 8 * i:8 * i + 8, :].rearrange("p b y -> p (b y)"), bank[i][0:S, :], q2b[:, 0:1], None,
                                      ALU.add).then_inc(taken, 1)

            @block.tensor
            def _(pe):
                pe.wait_ge(wready, 1)
                for i in range(4):
                    pe.wait_ge(relued, i + 1)
                    for b in range(8):
                        for yh in range(2):
                            c = 64 * (8 * i + b)
                            ins = pe.matmul(bank[i][0:S, 64 * b + 32 * yh:64 * b + 32 * yh + 32], qacc[:, yh, c:c + 64], wq[:, :])
                    ins.then_inc(full, 1)


TOK = B * T
GB = 7
GROUPS = [(b, min(GB, B - b)) for b in range(0, B, GB)]
NG = len(GROUPS)
VB = 512 // S
EPS = 1e-5
TINY = 1e-24
NEG = -1e30
KK = T // 2 - 1
HID = 256
TOKC = {}


def _token_tables():
    pos = np.concatenate([np.arange(1, T), [0]])
    TOKC["ident"] = np.eye(128)
    TOKC["causal"] = np.where(pos[None, :] <= pos[:, None], 0.0, NEG)
    TOKC["before"] = (pos[None, :] < pos[:, None]) * 1.0
    half = 8
    theta = (1.0 / 10000.0 ** (np.arange(half, dtype=np.float32) / half)).astype(np.float32)
    ang = np.outer(theta, pos.astype(np.float32)).astype(np.float32).astype(np.float64)
    cos, sin = np.ones((64, T)), np.zeros((64, T))
    cos[48:] = np.repeat(np.cos(ang), 2, 0)
    sin[48:] = np.repeat(np.sin(ang), 2, 0) * np.tile([[-1.0], [1.0]], (half, 1))
    TOKC["rope_cos"] = np.tile(cos, (2, 1))
    TOKC["rope_sin"] = np.tile(sin, (2, 1))


_token_tables()
TCOL = {}
_at = 0
for _n, _a in TOKC.items():
    TCOL[_n] = (_at, _a.shape[0], _a.shape[1])
    _at += _a.shape[1]
TOKC_COLS = _at


def token_table():
    t = np.zeros((128, TOKC_COLS), np.float32)
    for n, a in TOKC.items():
        c, r, w = TCOL[n]
        t[:r, c:c + w] = a
    return t


def tc(m, name, rows=None):
    c, r, w = TCOL[name]
    return m["tok_const"][0:rows or r, c:c + w]


class Chain:

    def __init__(self, eng, sem, base=0, m=None):
        self.eng, self.sem, self.base, self.n, self.m = eng, sem, base, 0, m

    def __call__(self, ins):
        self.n += 1
        ins.then_inc(self.sem, 1)
        self.eng.wait_ge(self.sem, self.base + self.n)
        if self.m:
            self.eng.sem_inc(self.m["waits"], 1)


def norm_sems(ctx, nc, name):
    return {k: ctx.enter_context(nc.semaphore(f"{name}_{k}")) for k in ("input", "squared", "spread", "rooted", "done", "chain")}


def norm_vector(dve, n, k, link, x, y, sq, s, centre=True):
    mean, v, root, rec, tmp = (s[:, 32 * i:32 * i + 32] for i in range(5))
    if centre:
        link(dve.tensor_reduce(mean, x, AX.X, ALU.add))
        link(dve.tensor_scalar(mean, mean, 1.0 / S, None, ALU.mult))
        dve.tensor_tensor(y, x, grow(mean, 2, S), ALU.subtract).then_inc(n["input"], 1)
    dve.wait_ge(n["squared"], k)
    link(dve.tensor_reduce(v, sq, AX.X, ALU.add))
    if centre:
        dve.tensor_scalar(v, v, 1.0 / S, EPS, ALU.mult, ALU.add).then_inc(n["spread"], 1)
    else:
        dve.tensor_scalar(v, v, TINY, None, ALU.max).then_inc(n["spread"], 1)
    dve.wait_ge(n["rooted"], k)
    link(dve.reciprocal(rec, root))
    link(dve.tensor_tensor(tmp, v, rec, ALU.mult))
    link(dve.tensor_tensor(tmp, tmp, root, ALU.add))
    link(dve.tensor_scalar(tmp, tmp, 0.5, None, ALU.mult))
    link(dve.reciprocal(rec, tmp))
    dve.tensor_tensor(y, y if centre else x, grow(rec, 2, S), ALU.mult).then_inc(n["done"], 1)
    dve.wait_ge(n["done"], k)


def norm_scalar(act, n, k, y, sq, s):
    act.wait_ge(n["input"], k)
    act.activation(sq, y, ACT.Square).then_inc(n["squared"], 1)
    act.wait_ge(n["spread"], k)
    act.activation(s[:, 64:96], s[:, 32:64], ACT.Sqrt).then_inc(n["rooted"], 1)


def turn_tokens(pe, ident, x, bank, full, n=0):
    for g, (b0, nb) in enumerate(GROUPS):
        for i in range(nb):
            ins = pe.transpose(bank[g][0:S, T * i:T * i + T], x[:, b0 + i, :], ident[0:T, 0:T])
        ins.then_inc(full, 1)


def take_turned(act, xt, bank, full, taken):
    for g, (b0, nb) in enumerate(GROUPS):
        act.wait_ge(full, g + 1)
        act.activation(xt[:, T * b0:T * (b0 + nb)], bank[g][0:S, 0:T * nb], ACT.Copy).then_inc(taken, 1)


def attend_sems(ctx, nc, name):
    names = ("scores_full", "scores_taken", "maxed", "shifted", "exped", "summed", "inverted", "probs",
             "turned_full", "turned_taken", "out_full", "out_taken")
    return {k: ctx.enter_context(nc.semaphore(f"{name}_{k}")) for k in names}


def attend_tensor(pe, a, k, ident, qt, kt, v, probs, probs_t, bank):
    pe.wait_ge(a["out_taken"], 4 * k)
    for g, (b0, nb) in enumerate(GROUPS):
        for i in range(nb):
            ins = pe.matmul(bank[g][0:T, T * i:T * i + T], qt(b0 + i), kt(b0 + i))
        ins.then_inc(a["scores_full"], 1)
    pe.wait_ge(a["probs"], k + 1)
    for g, (b0, nb) in enumerate(GROUPS):
        for i in range(nb):
            ins = pe.transpose(bank[g][0:T, T * i:T * i + T], probs[:, b0 + i, :], ident[0:T, 0:T])
        ins.then_inc(a["turned_full"], 1)
    pe.wait_ge(a["turned_taken"], NG * k + NG)
    for g in range(B // VB):
        for i in range(VB):
            b = VB * g + i
            ins = pe.matmul(bank[(5, 6, 7, 0)[g]][0:T, S * i:S * i + S], probs_t[:, b, :], v(b))
        ins.then_inc(a["out_full"], 1)


def attend_vector(dve, a, k, m, scale, h, probs, s, bank):
    mx, z = s[:, 0:32], s[:, 32:64]
    for g, (b0, nb) in enumerate(GROUPS):
        dve.wait_ge(a["scores_full"], NG * k + g + 1)
        dve.scalar_tensor_tensor(out=probs[:, b0:b0 + nb, :], in0=bank[g][0:T, 0:T * nb].rearrange("p (b t) -> p b t", t=T),
                                 scalar=scale, in1=grow(tc(m, "causal"), 1, nb), op0=ALU.mult, op1=ALU.add)\
           .then_inc(a["scores_taken"], 1)
    dve.wait_ge(a["scores_taken"], NG * k + NG)
    dve.tensor_reduce(mx, probs, AX.X, ALU.max).then_inc(a["maxed"], 1)
    dve.wait_ge(a["maxed"], k + 1)
    dve.tensor_tensor(probs, probs, grow(mx, 2, T), ALU.subtract).then_inc(a["shifted"], 1)
    dve.wait_ge(a["exped"], k + 1)
    dve.tensor_reduce(z, probs, AX.X, ALU.add).then_inc(a["summed"], 1)
    dve.wait_ge(a["summed"], k + 1)
    dve.reciprocal(z, z).then_inc(a["inverted"], 1)
    dve.wait_ge(a["inverted"], k + 1)
    dve.tensor_tensor(probs, probs, grow(z, 2, T), ALU.mult).then_inc(a["probs"], 1)
    for g in range(B // VB):
        dve.wait_ge(a["out_full"], B // VB * k + g + 1)
        dve.tensor_tensor(h[:, VB * g:VB * g + VB, :].rearrange("p b d -> p (b d)"), bank[(5, 6, 7, 0)[g]][0:T, :],
                          h[:, VB * g:VB * g + VB, :].rearrange("p b d -> p (b d)"), ALU.add).then_inc(a["out_taken"], 1)
    dve.wait_ge(a["out_taken"], B // VB * k + B // VB)


def attend_scalar(act, a, k, probs, probs_t, bank):
    act.wait_ge(a["shifted"], k + 1)
    act.activation(probs[:, :, :], probs[:, :, :], ACT.Exp).then_inc(a["exped"], 1)
    for g, (b0, nb) in enumerate(GROUPS):
        act.wait_ge(a["turned_full"], NG * k + g + 1)
        act.activation(probs_t[:, b0:b0 + nb, :].rearrange("p b t -> p (b t)"), bank[g][0:T, 0:T * nb], ACT.Copy)\
           .then_inc(a["turned_taken"], 1)


def latent_attention(nc, io, m):
    with ExitStack() as ctx:
        def sb(name, shape):
            return ctx.enter_context(nc.sbuf_tensor("la_" + name, shape, F32))

        def sem(name):
            return ctx.enter_context(nc.semaphore("la_" + name))

        h, xn, sq, s, xt, probs, probs_t = (m[k] for k in ("h", "xn", "sq", "stats", "xt", "probs", "probs_t"))
        wdown = sb("wdown", [S, 2, S])
        wup = sb("wup", [S, 320])
        wq = sb("wq", [S, 320])
        qt, kt = sb("qt", [S, TOK]), sb("kt", [S, TOK])
        v = sb("v", [T, B, S])
        rot = sb("rot", [128, 2, GB * T])
        bank = [ctx.enter_context(nc.psum_tensor(f"la_bank{i}", [128, 512], F32)) for i in range(8)]
        loads, wfull, wtaken, tfull, ttaken = sem("loads"), sem("wfull"), sem("wtaken"), sem("tfull"), sem("ttaken")
        qfull, qrot, qtaken, vfull, vtaken, halves = sem("qfull"), sem("qrot"), sem("qtaken"), sem("vfull"), sem("vtaken"), sem("halves")
        n = norm_sems(ctx, nc, "la_norm")
        a = attend_sems(ctx, nc, "la")
        ident = tc(m, "ident")

        with nc.Block() as block:
            @block.sync
            def _(sp):
                sp.dma_start(m["tok_const"][:, :], io["tok_const"]).then_inc(loads, 16)
                sp.dma_start(wdown[:, :, :], io["la_down"]).then_inc(loads, 16)
                sp.dma_start(wup[:, :], io["la_up"]).then_inc(loads, 16)
                sp.wait_ge(loads, 48)

            @block.tensor
            def _(pe):
                pe.wait_ge(loads, 48)
                pe.matmul(bank[7][0:S, 0:128], wdown[:, 0, :], wup[:, 0:128])
                pe.matmul(bank[7][0:S, 128:320], wdown[:, 1, :], wup[:, 128:320]).then_inc(wfull, 1)
                pe.wait_ge(n["done"], 1)
                turn_tokens(pe, ident, xn, bank, tfull)
                pe.wait_ge(wtaken, 1)
                for g, (b0, nb) in enumerate(GROUPS):
                    c = slice(T * b0, T * (b0 + nb))
                    if g == 0:
                        pe.wait_ge(ttaken, NG)
                    p = 2 * (g % 2)
                    if g >= 2:
                        pe.wait_ge(halves, g - 1)
                    for w in range(2):
                        ins = pe.matmul(bank[p + w][:, 0:T * nb], wq[:, 128 * w:128 * w + 128], xt[:, c])
                    ins.then_inc(qfull, 1)
                for g in range(B // VB):
                    if g == 1:
                        pe.wait_ge(halves, NG)
                    for i in range(VB):
                        b = VB * g + i
                        ins = pe.matmul(bank[4 + g][0:T, S * i:S * i + S], xt[:, T * b:T * b + T], wq[:, 256:320])
                    ins.then_inc(vfull, 1)
                pe.wait_ge(vtaken, B // VB)
                pe.wait_ge(qtaken, 2 * NG)
                attend_tensor(pe, a, 0, ident, lambda b: qt[:, T * b:T * b + T], lambda b: kt[:, T * b:T * b + T],
                              lambda b: v[:, b, :], probs, probs_t, bank)

            @block.vector
            def _(dve):
                link = Chain(dve, n["chain"])
                norm_vector(dve, n, 1, link, h[:, :, :], xn[:, :, :], sq[:, :, :], s)
                dve.wait_ge(loads, 48)
                for g, (b0, nb) in enumerate(GROUPS):
                    dve.wait_ge(qfull, g + 1)
                    if g >= 2:
                        dve.wait_ge(qtaken, 2 * g - 2)
                    p = 2 * (g % 2)
                    for w, table in enumerate(("rope_cos", "rope_sin")):
                        ins = dve.tensor_tensor(rot[:, w, 0:T * nb].rearrange("p (b t) -> p b t", t=T),
                                                bank[p + w][:, 0:T * nb].rearrange("p (b t) -> p b t", t=T),
                                                grow(tc(m, table), 1, nb), ALU.mult)
                    ins.then_inc(halves, 1)
                    dve.wait_ge(halves, g + 1)
                    c = slice(T * b0, T * (b0 + nb))
                    dve.tensor_tensor(qt[:, c], rot[0:S, 0, 0:T * nb], rot[0:S, 1, 0:T * nb], ALU.add).then_inc(qtaken, 1)
                    dve.tensor_tensor(kt[:, c], rot[S:128, 0, 0:T * nb], rot[S:128, 1, 0:T * nb], ALU.add).then_inc(qtaken, 1)
                    dve.wait_ge(qtaken, 2 * g + 2)
                attend_vector(dve, a, 0, m, 0.125, h, probs[:, :, :], s, bank)

            @block.scalar
            def _(act):
                norm_scalar(act, n, 1, xn[:, :, :], sq[:, :, :], s)
                act.wait_ge(wfull, 1)
                for i, o in enumerate((0, 128, 64, 192)):
                    act.activation(wq[:, o:o + 64], bank[7][0:S, 64 * i:64 * i + 64], ACT.Copy)
                act.activation(wq[:, 256:320], bank[7][0:S, 256:320], ACT.Copy).then_inc(wtaken, 1)
                take_turned(act, xt, bank, tfull, ttaken)
                for g in range(B // VB):
                    act.wait_ge(vfull, g + 1)
                    act.activation(v[:, VB * g:VB * g + VB, :].rearrange("p b d -> p (b d)"), bank[4 + g][0:T, :], ACT.Copy)\
                       .then_inc(vtaken, 1)
                attend_scalar(act, a, 0, probs, probs_t, bank)


def routed_feed_forward(nc, io, m):
    with ExitStack() as ctx:
        def sb(name, shape):
            return ctx.enter_context(nc.sbuf_tensor("ff_" + name, shape, F32))

        def sem(name):
            return ctx.enter_context(nc.semaphore("ff_" + name))

        h, xn, sq, s, xt, probs = (m[k] for k in ("h", "xn", "sq", "stats", "xt", "probs"))
        wr, wr_wide, br = sb("wr", [S, 1]), sb("wr_wide", [S, T]), sb("br", [T, 1])
        w1, b1, w2, b2 = sb("w1", [S, HID]), sb("b1", [128, 2]), sb("w2", [128, 2, S]), sb("b2", [S, 1])
        hid = sb("hid", [128, 2, TOK])
        yt = sb("yt", [S, TOK])
        ties = sb("ties", [T, B, T])
        bank = [ctx.enter_context(nc.psum_tensor(f"ff_bank{i}", [128, 512], F32)) for i in range(8)]
        loads, tfull, ttaken, wide = sem("loads"), sem("tfull"), sem("ttaken"), sem("wide")
        rfull, rtaken, hfull, htaken, yfull, ytaken, ofull, otaken = (sem(x) for x in (
            "rfull", "rtaken", "hfull", "htaken", "yfull", "ytaken", "ofull", "otaken"))
        n = norm_sems(ctx, nc, "ff_norm")
        ident = tc(m, "ident")

        with nc.Block() as block:
            @block.sync
            def _(sp):
                sp.dma_start(wr[:, :], io["ff_wr"]).then_inc(loads, 16)
                sp.dma_start(br[:, :], io["ff_br"].partition_broadcast(T).rearrange("p a b -> p (a b)")).then_inc(loads, 16)
                sp.dma_start(w1[:, :], io["ff_w1"]).then_inc(loads, 16)
                sp.dma_start(b1[:, :], io["ff_b1"]).then_inc(loads, 16)
                sp.dma_start(w2[:, :, :], io["ff_w2"].rearrange("(i p) d -> p i d", i=2)).then_inc(loads, 16)
                sp.dma_start(b2[:, :], io["ff_b2"]).then_inc(loads, 16)
                sp.wait_ge(loads, 96)

            @block.tensor
            def _(pe):
                pe.wait_ge(loads, 96)
                pe.wait_ge(wide, 1)
                pe.wait_ge(n["done"], 1)
                turn_tokens(pe, ident, xn, bank, tfull)
                pe.wait_ge(ttaken, NG)
                for g, (b0, nb) in enumerate(GROUPS):
                    pe.matmul(bank[g][0:T, 0:T * nb], wr_wide[:, :], xt[:, T * b0:T * (b0 + nb)]).then_inc(rfull, 1)
                for g, (b0, nb) in enumerate(GROUPS):
                    for i in range(2):
                        k = 2 * g + i
                        if k >= 3:
                            pe.wait_ge(htaken, k - 2)
                        pe.matmul(bank[5 + k % 3][:, 0:T * nb], w1[:, 128 * i:128 * i + 128], xt[:, T * b0:T * (b0 + nb)])\
                          .then_inc(hfull, 1)
                pe.wait_ge(rtaken, NG)
                for g, (b0, nb) in enumerate(GROUPS):
                    pe.wait_ge(htaken, 2 * g + 2)
                    for i in range(2):
                        ins = pe.matmul(bank[g][0:S, 0:T * nb], w2[:, i, :], hid[:, i, T * b0:T * (b0 + nb)],
                                        start=(i == 0), stop=(i == 1))
                    ins.then_inc(yfull, 1)
                for g in range(B // VB):
                    pe.wait_ge(ytaken, min(NG, (VB * g + VB - 1) // GB + 1))
                    if g == 3:
                        pe.wait_ge(ytaken, NG)
                    for i in range(VB):
                        b = VB * g + i
                        ins = pe.transpose(bank[(5, 6, 7, 0)[g]][0:T, S * i:S * i + S], yt[:, T * b:T * b + T], ident[0:S, 0:S])
                    ins.then_inc(ofull, 1)

            @block.scalar
            def _(act):
                norm_scalar(act, n, 1, xn[:, :, :], sq[:, :, :], s)
                take_turned(act, xt, bank, tfull, ttaken)
                act.wait_ge(loads, 96)
                for g, (b0, nb) in enumerate(GROUPS):
                    for i in range(2):
                        k = 2 * g + i
                        act.wait_ge(hfull, k + 1)
                        act.activation(hid[:, i, T * b0:T * (b0 + nb)], bank[5 + k % 3][:, 0:T * nb], ACT.Gelu_apprx_tanh,
                                       bias=b1[:, i:i + 1]).then_inc(htaken, 1)
                for g, (b0, nb) in enumerate(GROUPS):
                    act.wait_ge(yfull, g + 1)
                    act.activation(yt[:, T * b0:T * (b0 + nb)], bank[g][0:S, 0:T * nb], ACT.Identity, bias=b2[:, 0:1])\
                       .then_inc(ytaken, 1)

            @block.vector
            def _(dve):
                link = Chain(dve, n["chain"])
                dve.wait_ge(loads, 96)
                dve.tensor_copy(wr_wide[:, :], wr[:, 0:1].to_broadcast([S, T])).then_inc(wide, 1)
                norm_vector(dve, n, 1, link, h[:, :, :], xn[:, :, :], sq[:, :, :], s)
                for g, (b0, nb) in enumerate(GROUPS):
                    dve.wait_ge(rfull, g + 1)
                    dve.tensor_scalar(probs[:, b0:b0 + nb, :].rearrange("p b t -> p (b t)"), bank[g][0:T, 0:T * nb], br[:, 0:1], None,
                                      ALU.add).then_inc(rtaken, 1)
                dve.wait_ge(rtaken, NG)
                own, rank, sel = s[:, 0:32], s[:, 32:64], s[:, 64:96]
                link(dve.tensor_tensor(ties[:, :, :], probs[:, :, :], grow(tc(m, "ident")[0:T, 0:T], 1, B), ALU.mult))
                link(dve.tensor_reduce(own, ties[:, :, :], AX.X, ALU.add))
                link(dve.tensor_tensor(ties[:, :, :], probs[:, :, :], grow(own, 2, T), ALU.is_equal))
                link(dve.tensor_tensor(ties[:, :, :], ties[:, :, :], grow(tc(m, "before"), 1, B), ALU.mult))
                link(dve.tensor_tensor(probs[:, :, :], probs[:, :, :], grow(own, 2, T), ALU.is_gt))
                link(dve.tensor_tensor(ties[:, :, :], ties[:, :, :], probs[:, :, :], ALU.add))
                link(dve.tensor_reduce(rank, ties[:, :, :], AX.X, ALU.add))
                link(dve.tensor_scalar(sel, rank, KK - 0.5, None, ALU.is_lt))
                link(dve.tensor_tensor(sel, sel, own, ALU.mult))
                for g in range(B // VB):
                    bs = slice(VB * g, VB * g + VB)
                    dve.wait_ge(ofull, g + 1)
                    link(dve.tensor_tensor(sq[:, bs, :], bank[(5, 6, 7, 0)[g]][0:T, :].rearrange("p (b d) -> p b d", d=S),
                                           grow(sel[:, bs], 2, S), ALU.mult))
                link(dve.tensor_tensor(sq[:, :, :], sq[:, :, :], xn[:, :, :], ALU.add))
                link(dve.tensor_tensor(h[:, :, :], h[:, :, :], sq[:, :, :], ALU.add))


KT = (TOK + 127) // 128
CHN = TOK // 5


def similarity_attention(nc, io, m):
    with ExitStack() as ctx:
        def sb(name, shape):
            return ctx.enter_context(nc.sbuf_tensor("sa_" + name, shape, F32))

        def sem(name):
            return ctx.enter_context(nc.semaphore("sa_" + name))

        h, xn, sq, s = (m[k] for k in ("h", "xn", "sq", "stats"))
        ft = sb("ft", [S, KT * 128])
        ftok = sb("ftok", [128, KT, T])
        e = sb("exp", [128, 3, CHN])
        att_t = sb("att_t", [T, TOK])
        att = sb("att", [T, B, T])
        rec = sb("rec", [T, B])
        bank = [ctx.enter_context(nc.psum_tensor(f"sa_bank{i}", [128, 512], F32)) for i in range(8)]
        tfull, ttaken, ffull, ftaken, zero = sem("tfull"), sem("ttaken"), sem("ffull"), sem("ftaken"), sem("zero")
        sfull, exped, afull, ataken, ofull, otaken = (sem(x) for x in ("sfull", "exped", "afull", "ataken", "ofull", "otaken"))
        n = norm_sems(ctx, nc, "sa_norm")
        ident = tc(m, "ident")
        REST = TOK - 128 * (KT - 1)

        with nc.Block() as block:
            @block.gpsimd
            def _(pool):
                pool.memset(ft[:, TOK:], 0.0)
                pool.memset(ftok[:, KT - 1, :], 0.0)
                pool.memset(ftok[:, 0:KT - 1, S:T], 1.0).then_inc(zero, 1)
                pool.wait_ge(zero, 1)
                pool.memset(ftok[0:REST, KT - 1, S:T], 1.0).then_inc(zero, 1)

            @block.tensor
            def _(pe):
                pe.wait_ge(n["done"], 2)
                turn_tokens(pe, ident, xn, bank, tfull)
                pe.wait_ge(ttaken, NG)
                for t in range(KT):
                    r = REST if t == KT - 1 else 128
                    ins = pe.transpose(bank[t // 8][0:r, S * (t % 8):S * (t % 8) + S], ft[:, 128 * t:128 * t + r], ident[0:S, 0:S])
                    if t % 8 == 7 or t == KT - 1:
                        ins.then_inc(ffull, 1)
                pe.wait_ge(ftaken, 3)
                pe.wait_ge(zero, 2)
                with pe.Fori(0, 5) as c:
                    q = ft[:, bass.ds(c * CHN, CHN)]

                    def score(t):
                        if t >= 3:
                            wait_for(m, pe, exped, c * KT + t - 1)
                        elif t == 0:
                            wait_for(m, pe, exped, c * KT + 1)
                        pe.matmul(bank[t % 3][:, 0:CHN], ft[:, 128 * t:128 * t + 128], q).then_inc(sfull, 1)

                    score(0)
                    score(1)
                    wait_for(m, pe, ataken, c + 1)
                    for t in range(KT):
                        if t + 2 < KT:
                            score(t + 2)
                        wait_for(m, pe, exped, c * KT + t + 2)
                        ins = pe.matmul(bank[4][0:T, 0:CHN], ftok[:, t, :], e[:, t % 3, :], start=(t == 0), stop=(t == KT - 1))
                    ins.then_inc(afull, 1)
                pe.wait_ge(ataken, 6)
                for g, (b0, nb) in enumerate(GROUPS):
                    if g == 1:
                        pe.wait_ge(exped, 5 * KT + 1)
                    for i in range(nb):
                        b = b0 + i
                        ins = pe.transpose(bank[g][0:T, T * i:T * i + T], att_t[:, T * b:T * b + T], ident[0:T, 0:T])
                    ins.then_inc(ofull, 1)

            @block.scalar
            def _(act):
                norm_scalar(act, n, 1, xn[:, :, :], sq[:, :, :], s)
                norm_scalar(act, n, 2, xn[:, :, :], sq[:, :, :], s)
                take_turned(act, ft, bank, tfull, ttaken)
                act.sem_inc(exped, 1)
                with act.Fori(0, 5) as c:
                    for t in range(KT):
                        act.wait_ge(sfull, c * KT + t + 1)
                        act.activation(e[:, t % 3, :], bank[t % 3][:, 0:CHN], ACT.Exp).then_inc(exped, 1)
                norm_scalar(act, n, 3, sq[:, :, :], m["probs"][:, :, 0:S], s)

            @block.vector
            def _(dve):
                link = Chain(dve, n["chain"])
                norm_vector(dve, n, 1, link, h[:, :, :], xn[:, :, :], sq[:, :, :], s)
                dve.engine_nop().then_inc(n["input"], 1)
                norm_vector(dve, n, 2, link, xn[:, :, :], xn[:, :, :], sq[:, :, :], s, centre=False)
                dve.wait_ge(zero, 2)
                for g in range(3):
                    dve.wait_ge(ffull, g + 1)
                    k = min(8, KT - 8 * g)
                    r = REST if g == 2 else 128
                    dve.tensor_copy(ftok[0:r, 8 * g:8 * g + k, 0:S], bank[g][0:r, 0:S * k].rearrange("p (t d) -> p t d", d=S))\
                       .then_inc(ftaken, 1)
                dve.sem_inc(ataken, 1)
                with dve.Fori(0, 5) as c:
                    dve.wait_ge(afull, c + 1)
                    dve.tensor_copy(att_t[:, bass.ds(c * CHN, CHN)], bank[4][0:T, 0:CHN]).then_inc(ataken, 1)
                for g, (b0, nb) in enumerate(GROUPS):
                    dve.wait_ge(ofull, g + 1)
                    link(dve.tensor_copy(att[:, b0:b0 + nb, :].rearrange("p b t -> p (b t)"), bank[g][0:T, 0:T * nb]))
                link(dve.reciprocal(rec[:, :], att[:, :, S]))
                link(dve.tensor_scalar(rec[:, :], rec[:, :], float(np.float32(1.0 - 0.8)), None, ALU.mult))
                link(dve.tensor_tensor(att[:, :, 0:S], att[:, :, 0:S], grow(rec[:, :], 2, S), ALU.mult))
                dve.scalar_tensor_tensor(out=sq[:, :, :], in0=xn[:, :, :], scalar=0.8, in1=att[:, :, 0:S],
                                         op0=ALU.mult, op1=ALU.add).then_inc(n["input"], 1)
                norm_vector(dve, n, 3, link, sq[:, :, :], sq[:, :, :], m["probs"][:, :, 0:S], s, centre=False)
                link(dve.tensor_tensor(h[:, :, :], h[:, :, :], sq[:, :, :], ALU.add))


HEADS = 8
KEYS = 64
TOP = 16
GROUPS_K = 2 * HEADS
TILES = B // 2
DENSE = 3
GH = HEADS - DENSE
SUM_PARTS = ((0, 3), (3, GH))
CHUNKS_K = KEYS ** 2 // 128
BATCHES = CHUNKS_K // 4
CLASS = "class"
CH_HEADS = HEADS // 4
BIG = 1e4
UNITS = 2 * HEADS
UNIT_BANKS = ((0, 7), (7, 7), (14, 2))
Q_BANKS = ((0, 3), (3, 3), (6, 2))


def memory_attention(nc, io, m):
    with ExitStack() as ctx:
        def sb(name, shape, dt=F32):
            return ctx.enter_context(nc.sbuf_tensor("me_" + name, shape, dt))

        def sem(name):
            return ctx.enter_context(nc.semaphore("me_" + name))

        h, xn, sq, s, xt = (m[k] for k in ("h", "xn", "sq", "stats", "xt"))
        ident = tc(m, "ident")
        fold = sb("fold", [S, GROUPS_K * KEYS])
        wq = sb("wq", [S, HEADS, S])
        wo = sb("wo", [128, HEADS, S])
        numbers = sb("numbers", [128, TOP])
        first_row = sb("first_row", [128, HEADS])
        first_row_cls = sb("first_row_cls", [128, CH_HEADS])
        xtile = sb("xtile", [S, 128])
        xq = sb("xq", [S, 2 * T])
        sim = sb("sim", [128, GROUPS_K, KEYS])
        vals = sb("vals", [128, GROUPS_K, TOP])
        pos = sb("pos", [128, GROUPS_K, TOP], U32)
        work = sb("work", [128, HEADS * TOP * TOP])
        rest = work[:, 0:GROUPS_K * KEYS].rearrange("p (g k) -> p g k", k=KEYS)
        pairs = work[:, :].rearrange("p (h c) -> p h c", h=HEADS)
        best = sb("best", [128, HEADS, TOP])
        cell = sb("cell", [128, HEADS, TOP], U32)
        half = sb("half", [128, 2, HEADS * TOP], U32)
        halff = sb("halff", [128, 2, HEADS * TOP])
        hot = sb("hot", [128, HEADS * TOP, TOP], BF16)
        picked = sb("picked", [128, 2, HEADS * TOP])
        total = sb("total", [128, HEADS])
        rows_next = sb("rows_next", [128, HEADS, TOP], U32)
        rows = sb("rows", [128, HEADS, TOP], U32)
        wts = sb("wts", [128, HEADS, TOP])
        rows_cls = sb("rows_cls", [128, CH_HEADS, TOP], U32)
        wts_cls = sb("wts_cls", [128, CH_HEADS, TOP])
        got = sb("got", [128, GH, TOP, 128])
        spread32 = got[:, 0:2].rearrange("p s j c -> p (s j c)")
        pk = got[0:32, 2].rearrange("p j c -> p (j c)").rearrange("p (w g k) -> p w g k", w=2, g=GROUPS_K)
        prod = work[:, :].rearrange("p (j c) -> p j c", c=128)
        tab = sb("tab", [128, DENSE, CHUNKS_K, 128])
        spread = sb("spread", [128, CHUNKS_K, 128], BF16)
        minus = sb("minus", [128, 128], BF16)
        keys64 = sb("keys64", [128, KEYS])
        key_grid = sb("key_grid", [128, KEYS, TOP], BF16)
        posb = sb("posb", [128, GROUPS_K, TOP], BF16)
        one = sb("one", [128, 128], BF16)
        ranks = sb("ranks", [128, DENSE, 2, TOP], BF16)
        threshold = sb("threshold", [128, 1])
        second = sb("second", [128, TOP])
        below = sb("below", [128, DENSE, 2, KEYS])
        places = sb("places", [128, DENSE, 2 * KEYS, TOP], BF16)
        inv_z = sb("inv_z", [128, DENSE])
        left = sb("left", [128, DENSE * 128])
        split = [sb(f"split{i}", [128, DENSE * 128], BF16) for i in range(3)]
        steps_t = sb("steps_t", [128, DENSE * 128], BF16)
        penalty = sb("penalty", [128, 2, 512], BF16)
        wt = sb("wt", [128, 2, 512])
        kv = sb("kv", [128, HEADS, 128])
        kvt = sb("kvt", [128, HEADS, 2, T])
        kvt_cls = sb("kvt_cls", [128, HEADS, B])
        qt = sb("qt", [S, HEADS, 2 * T])
        probs, probs_t = (m[k][:, :, :].rearrange("p b d -> p (b d)")[:, 0:UNITS * T].rearrange("p (u t) -> p u t", t=T)
                          for k in ("sq", "xn"))
        vo = [m[k][:, :, :].rearrange("p b d -> p (b d)")[:, UNITS * T:UNITS * T + 512] for k in ("sq", "xn")]
        mx, z = sb("mx", [T, UNITS]), sb("z", [T, UNITS])
        bank = [ctx.enter_context(nc.psum_tensor(f"me_bank{i}", [128, 512], F32)) for i in range(8)]
        SIM = KVB = (0, 1)
        DS, ATT, OUT = (2, 3), (4, 5, 6), 7

        loads, tfull, ttaken, folded, fold_taken = (sem(x) for x in ("loads", "tfull", "ttaken", "folded", "fold_taken"))
        x_ready, sim_full, sim_ready, sim_used = (sem(x) for x in ("x_ready", "sim_full", "sim_ready", "sim_used"))
        w_shifted, w_exped, posted = sem("w_shifted"), sem("w_exped"), sem("rows_posted")
        slot_free, summed = sem("slot_free"), sem("summed")
        gathered = [sem(f"gathered{i}") for i in range(GH)]
        cls_posted, cls_gathered, cls_summed = sem("cls_posted"), sem("cls_gathered"), sem("cls_summed")
        spread_made, tab_loaded = sem("spread_made"), sem("table_loaded")
        LOADS = 10
        dense_ready, dense_turned, top_part, rest1, mid_part, low_part = (sem(x) for x in (
            "dense_ready", "dense_turned", "top_part", "rest1", "mid_part", "low_part"))
        inv_ready = sem("inv_z_ready")
        marks_full, penalty_made, ds_full, wt_made, dense_summed, dense_taken = (sem(x) for x in (
            "marks_full", "penalty_made", "dense_scores_full", "wt_made", "dense_summed", "dense_taken"))
        cls_turned, cls_taken = sem("cls_turned"), sem("cls_taken")
        kv_turned, kvt_ready = sem("kv_turned"), sem("kvt_ready")
        xq_ready, q_full, q_taken = sem("xq_ready"), sem("q_full"), sem("q_taken")
        vo_full, vo_taken, s_full, s_taken = sem("vo_full"), sem("vo_taken"), sem("scores_full"), sem("scores_taken")
        shifted, exped, p_ready, p_turned, p_taken = (sem(x) for x in ("shifted", "exped", "probs", "probs_turned", "probs_taken"))
        out_full, out_added = sem("out_full"), sem("out_added")
        n = norm_sems(ctx, nc, "me_norm")
        chosen_cls, chosen = sem("class_choice_steps"), sem("choice_steps")
        attending = sem("attend_steps")
        CHOICE = 24


        def choose(dve, u, part):
            cls = u is CLASS
            H, G = (CH_HEADS, CH_HEADS) if cls else (HEADS, GH)
            if cls:
                u = 0
            before = 0 if part == 1 else 3
            link = Chain(dve, chosen_cls, before) if cls else Chain(dve, chosen, (u - 1) * CHOICE + before, m)
            a, b = slice(0, 8), slice(8, TOP)
            if part == 1:
                wait_for(m, dve, sim_ready, u + 1)
                for g in range(2 * H):
                    ins = dve.max(out=vals[:, g, a], in_=sim[:, g, :])
                link(ins)
                if not cls:
                    wait_for(m, dve, dense_turned, u)
                    for i in range(2):
                        g = slice(HEADS * i + GH, HEADS * i + HEADS)
                        dve.tensor_tensor(below[:, :, i, :], sim[:, g, :], grow(vals[:, g, 0], 2, KEYS), ALU.subtract)
                for g in range(2 * H):
                    dve.max_index(out=pos[:, g, a], in_max=vals[:, g, a], in_values=sim[:, g, :])
                for g in range(2 * H):
                    ins = dve.match_replace(out=rest[:, g, :], in_to_replace=vals[:, g, a], in_values=sim[:, g, :], imm_value=NEG)
                ins.then_inc(sim_used, 1)
                wait_for(m, dve, sim_used, u + 1)
                for g in range(2 * H):
                    ins = dve.max(out=vals[:, g, b], in_=rest[:, g, :])
                link(ins)
                for g in range(2 * H):
                    ins = dve.max_index(out=pos[:, g, b], in_max=vals[:, g, b], in_values=rest[:, g, :])
                link(ins)
                return
            link(dve.tensor_tensor(pairs[:, 0:H, :].rearrange("p h (i j) -> p h i j", j=TOP),
                                   grow(vals[:, 0:H, :], 3, TOP), grow(vals[:, H:2 * H, :], 2, TOP), ALU.add))
            for g in range(H):
                ins = dve.max(out=best[:, g, a], in_=pairs[:, g, :])
            link(ins)
            for g in range(H):
                ins = dve.max_index(out=cell[:, g, a], in_max=best[:, g, a], in_values=pairs[:, g, :])
            link(ins)
            for g in range(H):
                ins = dve.match_replace(out=pairs[:, g, :], in_to_replace=best[:, g, a], in_values=pairs[:, g, :], imm_value=NEG)
            link(ins)
            for g in range(H):
                ins = dve.max(out=best[:, g, b], in_=pairs[:, g, :])
            link(ins)
            for g in range(H):
                dve.max_index(out=cell[:, g, b], in_max=best[:, g, b], in_values=pairs[:, g, :])
            top, sums = best[:, 0:H, :], total[:, 0:H]
            link(dve.tensor_copy(sums, top[:, :, 0]))
            dve.tensor_tensor(top, top, grow(sums, 2, TOP), ALU.subtract).then_inc(w_shifted, 1)
            c = cell[:, 0:H, :].rearrange("p h k -> p (h k)")
            dve.tensor_scalar(half[:, 0, 0:H * TOP], c, 4, None, ALU.logical_shift_right)
            dve.tensor_scalar(half[:, 1, 0:H * TOP], c, TOP - 1, None, ALU.bitwise_and)
            link(dve.tensor_copy(posb[:, 0:2 * H, :], pos[:, 0:2 * H, :]))
            link(dve.tensor_copy(halff[:, :, 0:H * TOP], half[:, :, 0:H * TOP]))
            iota = numbers[:, :]
            for i in range(2):
                n_marks = (H if i == 0 else G) * TOP
                link(dve.tensor_tensor(hot[:, 0:n_marks, :], grow(halff[:, i, 0:n_marks], 2, TOP), grow(iota, 1, n_marks), ALU.is_equal))
                if i == 0 and not cls:
                    with nc.allow_low_precision(reason="counts up to TOP are exact"):
                        link(dve.tensor_reduce(ranks[:, :, 0, :], hot[:, GH * TOP:, :].rearrange("p (h k) i -> p h i k", h=DENSE), AX.X, ALU.add))
                marks = hot[:, 0:G * TOP, :]
                marks4 = marks.rearrange("p (h k) i -> p h k i", h=G)
                link(dve.tensor_tensor(marks4, marks4, grow(posb[:, H * i:H * i + G, :], 2, TOP), ALU.mult))
                link(dve.tensor_reduce(picked[:, i, 0:G * TOP], marks, AX.X, ALU.add))
            if not cls:
                for d in range(DENSE):
                    at = posb[:, :, :].rearrange("p (i h) k -> p i h k", i=2)[:, :, GH + d, :]
                    place = places[:, d].rearrange("p (i n) k -> p i n k", i=2)
                    link(dve.tensor_tensor(place, grow(at, 2, KEYS), grow(key_grid[:, :, :], 1, 2), ALU.is_equal))
                    dve.tensor_tensor(place, place, grow(ranks[:, d], 2, KEYS), ALU.mult).then_inc(dense_ready, 1)
            p0 = picked[:, 0, 0:G * TOP]
            wait_for(m, dve, w_exped, u + 1)
            dve.tensor_reduce(sums, top, AX.X, ALU.add)
            link(dve.scalar_tensor_tensor(out=p0, in0=picked[:, 1, 0:G * TOP], scalar=float(KEYS), in1=p0, op0=ALU.mult, op1=ALU.add))
            dve.reciprocal(sums, sums)
            link(dve.tensor_tensor(rows_next[:, 0:G, :], p0.rearrange("p (h k) -> p h k", h=G), grow((first_row_cls if cls else first_row)[:, 0:G], 2, TOP), ALU.add))
            link(dve.tensor_tensor(top, top, grow(sums, 2, TOP), ALU.mult))
            assert cls or 3 + link.n == CHOICE, 3 + link.n

        def post(dve, u, f):
            hs = slice(*SUM_PARTS[f])
            dve.tensor_copy(wts[:, hs, :], best[:, hs, :])
            dve.tensor_copy(rows[:, hs, :], rows_next[:, hs, :]).then_inc(posted, 1)

        def sum_rows(dve, t, f, post_next):
            if f == 0:
                dve.wait_ge(kv_turned, 2 * t)
            for hd in range(*SUM_PARTS[f]):
                dve.wait_ge(gathered[hd], 16 * TOP * (t + 1))
                dve.tensor_tensor(prod, got[:, hd], grow(wts[:, hd, :], 2, 128), ALU.mult).then_inc(slot_free, 1)
                dve.wait_ge(slot_free, GH + GH * t + hd + 1)
                dve.tensor_reduce(kv[:, hd, :], prod.rearrange("p j c -> p c j"), AX.X, ALU.add).then_inc(summed, 1)
                dve.wait_ge(summed, GH * t + hd + 1)
            if post_next:
                post(dve, t + 2, f)
                dve.wait_ge(posted, 2 * t + 2 + f + 1)

        def dense_turn(pe, t):
            wait_for(m, pe, dense_ready, DENSE * t + DENSE)
            for d in range(DENSE):
                o = slice(128 * d, 128 * d + 128)
                pe.transpose(bank[DS[0]][:, o], below[:, d].rearrange("p i k -> p (i k)"), ident[:, :])
                for k in range(TOP):
                    ins = pe.matmul(bank[DS[1]][:, o], places[:, d, :, k], one[:, :], start=(k == 0), stop=(k == TOP - 1))
            ins.then_inc(dense_turned, 1)

        def split_scalar(act, t):
            D = DENSE * 128
            act.wait_ge(dense_turned, t + 2)
            act.activation(split[0][:, :], bank[DS[0]][:, 0:D], ACT.Copy).then_inc(top_part, 1)
            act.activation(steps_t[:, :], bank[DS[1]][:, 0:D], ACT.Copy)

        def split_vector(dve, t):
            dve.wait_ge(top_part, t + 1)
            dve.tensor_tensor(left[:, :], bank[DS[0]][:, 0:DENSE * 128], split[0][:, :], ALU.subtract).then_inc(rest1, 1)

        def split_scalar_low(act, t):
            act.wait_ge(rest1, t + 1)
            act.activation(split[1][:, :], left[:, :], ACT.Copy).then_inc(mid_part, 1)

        def split_vector_low(dve, t):
            dve.wait_ge(mid_part, t + 1)
            dve.tensor_tensor(split[2][:, :], left[:, :], split[1][:, :], ALU.subtract).then_inc(low_part, 1)
            if not isinstance(t, int) or t > 0:
                dve.wait_ge(dense_taken, DENSE * t)
            dve.tensor_copy(inv_z[:, :], total[:, GH:]).then_inc(inv_ready, 1)
            dve.wait_ge(inv_ready, t + 1)

        def dense_tensor(pe, t, d):
            first = (DENSE * t + d) * BATCHES
            tokens = slice(128 * d, 128 * d + 128)

            def marks(b):
                if b >= 2:
                    wait_for(m, pe, penalty_made, first + b - 1)
                for i in range(4):
                    ins = pe.matmul(bank[SIM[b % 2]][:, 128 * i:128 * i + 128], spread[:, 4 * b + i, :], steps_t[:, tokens])
                ins.then_inc(marks_full, 1)

            def scores(b):
                if b >= 2:
                    wait_for(m, pe, wt_made, first + b - 1)
                for i in range(4):
                    for k in range(3):
                        pe.matmul(bank[DS[b % 2]][:, 128 * i:128 * i + 128], spread[:, 4 * b + i, :], split[k][:, tokens],
                                  start=(i == 0 and k == 0), stop=False)

            if d == 0:
                wait_for(m, pe, low_part, t + 1)
            marks(0)
            marks(1)
            scores(0)
            for b in range(BATCHES):
                wait_for(m, pe, penalty_made, first + b + 1)
                pe.matmul(bank[DS[b % 2]][:, :], minus[:, :], penalty[:, b % 2], start=False, stop=True).then_inc(ds_full, 1)
                if b + 1 < BATCHES:
                    scores(b + 1)
                if b + 2 < BATCHES:
                    marks(b + 2)
                wait_for(m, pe, wt_made, first + b + 1)
                if b == 0:
                    wait_for(m, pe, dense_taken, DENSE * t + d)
                    wait_for(m, pe, out_added, t)
                for i in range(4):
                    ins = pe.matmul(bank[OUT][:, 128 + 128 * d:256 + 128 * d], wt[:, b % 2, 128 * i:128 * i + 128], tab[:, d, 4 * b + i, :],
                                    start=(b == 0 and i == 0), stop=(b == BATCHES - 1 and i == 3))
                ins.then_inc(dense_summed, 1)

        def dense_scalar(act, t, d, choice=None):
            first = (DENSE * t + d) * BATCHES

            def penal(b):
                act.wait_ge(marks_full, first + b + 1)
                act.activation(penalty[:, b % 2], bank[SIM[b % 2]][:, :], ACT.Relu, bias=threshold[:, 0:1], scale=-BIG).then_inc(penalty_made, 1)

            penal(0)
            penal(1)
            for b in range(BATCHES):
                if b == BATCHES // 2 and choice is not None:
                    exp_weights(act, choice)
                act.wait_ge(ds_full, first + b + 1)
                if b >= 2:
                    act.wait_ge(dense_summed, first + b - 1)
                act.activation(wt[:, b % 2], bank[DS[b % 2]][:, :], ACT.Exp).then_inc(wt_made, 1)
                if b + 2 < BATCHES:
                    penal(b + 2)
            act.wait_ge(dense_summed, first + BATCHES)
            act.wait_ge(inv_ready, t + 1)
            act.activation(kv[:, GH + d, :], bank[OUT][:, 128 + 128 * d:256 + 128 * d], ACT.Copy, scale=inv_z[:, d:d + 1])\
               .then_inc(dense_taken, 1)

        def attend_a(dve, t):
            for g, (u0, nu) in enumerate(UNIT_BANKS):
                dve.wait_ge(s_full, 3 * t + g + 1)
                dve.tensor_tensor(probs[:, u0:u0 + nu, :], bank[ATT[g]][0:T, 0:T * nu].rearrange("p (u t) -> p u t", t=T),
                                  grow(tc(m, "causal"), 1, nu), ALU.add).then_inc(s_taken, 1)
            dve.wait_ge(s_taken, 3 * t + 3)
            dve.tensor_reduce(mx[:, :], probs[:, :, :], AX.X, ALU.max).then_inc(attending, 1)
            dve.wait_ge(attending, 3 * t + 1)
            dve.tensor_tensor(probs[:, :, :], probs[:, :, :], grow(mx[:, :], 2, T), ALU.subtract).then_inc(shifted, 1)

        def attend_b(dve, t):
            dve.wait_ge(exped, t + 1)
            dve.tensor_reduce(z[:, :], probs[:, :, :], AX.X, ALU.add).then_inc(attending, 1)
            dve.wait_ge(attending, 3 * t + 2)
            dve.reciprocal(z[:, :], z[:, :]).then_inc(attending, 1)
            dve.wait_ge(attending, 3 * t + 3)
            dve.tensor_tensor(probs[:, :, :], probs[:, :, :], grow(z[:, :], 2, T), ALU.mult).then_inc(p_ready, 1)

        def attend_c(dve, t):
            dve.wait_ge(out_full, t + 1)
            hb = h[:, bass.ds(2 * t, 2), :]
            dve.tensor_tensor(hb, bank[OUT][0:T, 0:2 * S].rearrange("p (b d) -> p b d", d=S), hb, ALU.add).then_inc(out_added, 1)

        def vector_tile(dve, t, choose_next=True, attend=True):
            split_vector(dve, t)
            split_vector_low(dve, t)
            if choose_next:
                choose(dve, t + 2, 1)
            if attend:
                attend_a(dve, t - 1)
            if choose_next:
                choose(dve, t + 2, 2)
            if attend:
                attend_b(dve, t - 1)
            sum_rows(dve, t, 0, choose_next)
            if attend:
                attend_c(dve, t - 1)
            sum_rows(dve, t, 1, choose_next)

        def similarities(pe, u):
            wait_for(m, pe, x_ready, u + 1)
            wait_for(m, pe, sim_ready, u)
            pe.matmul(bank[SIM[0]][:, :], xtile[:, :], fold[:, 0:512])
            pe.matmul(bank[SIM[1]][:, :], xtile[:, :], fold[:, 512:1024]).then_inc(sim_full, 1)

        def unit(g, u0, i):
            return bank[ATT[g]][0:T, T * i:T * i + T], (u0 + i) // 2, (u0 + i) % 2

        def tensor_scores(pe, t):
            wait_for(m, pe, kvt_ready, 2 * t + 2)
            for u in range(UNITS):
                ins = pe.matmul(bank[KVB[u // 8]][0:T, S * (u % 8):S * (u % 8) + S], kvt[S:128, u // 2, u % 2, :], wo[S:128, u // 2, :])
                if u % 8 == 7:
                    ins.then_inc(vo_full, 1)
            wait_for(m, pe, q_taken, 3 * t + 3)
            for g, (u0, nu) in enumerate(UNIT_BANKS):
                for i in range(nu):
                    o, hd, b = unit(g, u0, i)
                    ins = pe.matmul(o, qt[:, hd, T * b:T * b + T], kvt[0:S, hd, b, :])
                ins.then_inc(s_full, 1)

        def tensor_out(pe, t, taken_before):
            wait_for(m, pe, p_ready, t + 1)
            for g, (u0, nu) in enumerate(UNIT_BANKS):
                for i in range(nu):
                    ins = pe.transpose(unit(g, u0, i)[0], probs[:, u0 + i, :], ident[0:T, 0:T])
                ins.then_inc(p_turned, 1)
            wait_for(m, pe, p_taken, 3 * t + 3)
            wait_for(m, pe, vo_taken, 2 * t + 2)
            wait_for(m, pe, dense_taken, taken_before)
            wait_for(m, pe, out_added, t + 1)
            for b in range(2):
                for hd in range(HEADS):
                    ins = pe.matmul(bank[OUT][0:T, S * b:S * b + S], probs_t[:, 2 * hd + b, :], vo[hd // 4][:, S * ((2 * hd + b) % 8):S * ((2 * hd + b) % 8) + S],
                                    start=(hd == 0), stop=(hd == HEADS - 1))
            ins.then_inc(out_full, 1)

        def queries(pe, t):
            wait_for(m, pe, xq_ready, t + 1)
            for g, (h0, nh) in enumerate(Q_BANKS):
                for i in range(nh):
                    ins = pe.matmul(bank[ATT[g]][0:S, 2 * T * i:2 * T * i + 2 * T], wq[:, h0 + i, :], xq[:, :])
                ins.then_inc(q_full, 1)

        def turn_kv(pe, t):
            for f in range(2):
                wait_for(m, pe, summed, GH * t + min(4 * f + 4, GH))
                if f == 1:
                    wait_for(m, pe, dense_taken, DENSE * t + DENSE)
                for i in range(4):
                    ins = pe.transpose(bank[KVB[f]][:, 128 * i:128 * i + 128], kv[:, 4 * f + i, :], ident[:, :])
                ins.then_inc(kv_turned, 1)

        def tensor_tile(pe, t, ahead=True, attend=True, more=True):
            if attend:
                tensor_scores(pe, t - 1)
                wait_for(m, pe, vo_taken, 2 * t)
            dense_tensor(pe, t, 0)
            if ahead:
                similarities(pe, t + 3)
                wait_for(m, pe, sim_ready, t + 4)
            dense_tensor(pe, t, 1)
            dense_tensor(pe, t, 2)
            if attend:
                tensor_out(pe, t - 1, DENSE * t + DENSE)
            queries(pe, t)
            if more:
                dense_turn(pe, t + 1)
            turn_kv(pe, t)

        def copy_x(act, t):
            act.wait_ge(sim_full, t + 1)
            act.activation(xtile[:, :].rearrange("p (b t) -> p b t", b=2),
                           xt[:, bass.ds(2 * T * t, 2 * T)].rearrange("p (b t) -> p b t", b=2)[:, :, 0:S], ACT.Copy)\
               .then_inc(x_ready, 1)

        def copy_xq(act, t):
            act.wait_ge(q_full, 3 * t)
            act.activation(xq[:, :], xt[:, bass.ds(2 * T * t, 2 * T)], ACT.Copy).then_inc(xq_ready, 1)

        def copy_sim(act, u):
            act.wait_ge(sim_full, u + 1)
            act.wait_ge(sim_used, u)
            for i in range(2):
                ins = act.activation(sim[:, HEADS * i:HEADS * i + HEADS, :].rearrange("p g k -> p (g k)"), bank[SIM[i]][:, :], ACT.Copy)
            ins.then_inc(sim_ready, 1)

        def exp_weights(act, u, heads=HEADS):
            act.wait_ge(w_shifted, u + 1)
            act.activation(best[:, 0:heads, :], best[:, 0:heads, :], ACT.Exp).then_inc(w_exped, 1)

        def scalar_tile(act, t, ahead=True, choose_next=True, attend=True):
            if ahead:
                copy_x(act, t + 2)
            copy_xq(act, t)
            split_scalar_low(act, t)
            if attend:
                for i in range(2):
                    act.wait_ge(vo_full, 2 * (t - 1) + i + 1)
                    act.activation(vo[i], bank[KVB[i]][0:T, :], ACT.Copy).then_inc(vo_taken, 1)
            dense_scalar(act, t, 0)
            if attend:
                act.wait_ge(shifted, t)
                act.activation(probs[:, :, :], probs[:, :, :], ACT.Exp).then_inc(exped, 1)
            if ahead:
                copy_sim(act, t + 3)
            dense_scalar(act, t, 1, t + 2 if choose_next else None)
            dense_scalar(act, t, 2)
            if attend:
                for g, (u0, nu) in enumerate(UNIT_BANKS):
                    act.wait_ge(p_turned, 3 * (t - 1) + g + 1)
                    act.activation(probs_t[:, u0:u0 + nu, :].rearrange("p u t -> p (u t)"), bank[ATT[g]][0:T, 0:T * nu], ACT.Copy)\
                       .then_inc(p_taken, 1)
            for g, (h0, nh) in enumerate(Q_BANKS):
                act.wait_ge(q_full, 3 * t + g + 1)
                act.activation(qt[:, h0:h0 + nh, :].rearrange("p h t -> p (h t)"), bank[ATT[g]][0:S, 0:2 * T * nh], ACT.Copy,
                               scale=S ** -0.5).then_inc(q_taken, 1)
            if choose_next:
                split_scalar(act, t + 1)
            for f in range(2):
                hs = slice(4 * f, 4 * f + 4)
                act.wait_ge(kv_turned, 2 * t + f + 1)
                act.activation(kvt[:, hs, :, 0:S], bank[KVB[f]][:, :].rearrange("p (h b t) -> p h b t", h=4, b=2), ACT.Copy)
                act.activation(kvt[:, hs, :, S], kvt_cls[:, hs, bass.ds(2 * t, 2)], ACT.Copy).then_inc(kvt_ready, 1)

        def gather(pool, t):
            for hd in range(GH):
                if hd in (0, SUM_PARTS[1][0]):
                    wait_for(m, pool, posted, 2 * t + (1 if hd == 0 else 2))
                wait_for(m, pool, slot_free, GH * t + hd + 1)
                for j in range(TOP):
                    pool.indirect_dma_start(got[:, hd, j, :], None, io["table"],
                                            bass.IndirectOffsetOnAxis(rows[:, hd, j:j + 1], 0)).then_inc(gathered[hd], 16)

        with nc.Block() as block:
            @block.sync
            def _(sp):
                sp.dma_start(pk[:, 0], io["pk_w"]).then_inc(loads, 16)
                sp.dma_start(pk[:, 1], io["pk_k"]).then_inc(loads, 16)
                sp.dma_start(spread32, io["spread"]).then_inc(loads, 16)
                sp.dma_start(keys64[:, :], io["keys64"].partition_broadcast(128).rearrange("p a b -> p (a b)")).then_inc(loads, 16)
                sp.dma_start(second[:, :], io["second_rank"].partition_broadcast(128).rearrange("p a b -> p (a b)")).then_inc(loads, 16)
                sp.dma_start(wq[:, :, :], io["me_wq"]).then_inc(loads, 16)
                sp.dma_start(wo[S:128, :, :], io["me_wo"]).then_inc(loads, 16)
                sp.dma_start(numbers[:, :], io["numbers"].partition_broadcast(128).rearrange("p a b -> p (a b)")).then_inc(loads, 16)
                sp.dma_start(first_row[:, :], io["first_row"].partition_broadcast(128).rearrange("p a b -> p (a b)")).then_inc(loads, 16)
                sp.dma_start(first_row_cls[:, :], io["first_row_cls"]).then_inc(loads, 16)
                for d in range(DENSE):
                    r = KEYS ** 2 * (GH + d)
                    sp.dma_start(tab[:, d], io["table"][r:r + KEYS ** 2, :].rearrange("(c r) k -> r c k", r=128)).then_inc(tab_loaded, 16)
                sp.wait_ge(loads, LOADS * 16)
                sp.wait_ge(tab_loaded, DENSE * 16)

            @block.gpsimd
            def _(pool):
                pool.memset(threshold[:, :], BIG * (TOP + 0.5)).then_inc(spread_made, 1)
                wait_for(m, pool, cls_posted, 1)
                for i in range(CH_HEADS):
                    for j in range(TOP):
                        pool.indirect_dma_start(got[:, 3 + i, j, :], None, io["table"],
                                                bass.IndirectOffsetOnAxis(rows_cls[:, i, j:j + 1], 0)).then_inc(cls_gathered, 16)
                pool.wait_ge(folded, GROUPS_K)
                pool.wait_ge(spread_made, 2)
                with pool.Fori(0, TILES) as t:
                    gather(pool, t)

            @block.tensor
            def _(pe):
                pe.sem_inc(dense_turned, 1)
                wait_for(m, pe, loads, LOADS * 16)
                for g in range(GROUPS_K):
                    pe.matmul(bank[5 + g // 8][0:S, KEYS * (g % 8):KEYS * (g % 8) + KEYS], pk[:, 0, g, :], pk[:, 1, g, :]).then_inc(folded, 1)
                wait_for(m, pe, n["done"], 1)
                turn_tokens(pe, ident, xn, bank, tfull)
                wait_for(m, pe, fold_taken, 2)
                wait_for(m, pe, ttaken, NG)
                wait_for(m, pe, x_ready, 1)
                for q in range(4):
                    for i in range(2):
                        g = KEYS * (HEADS * i + CH_HEADS * q)
                        ins = pe.matmul(bank[SIM[0]][B * q:B * q + B, 128 * i:128 * i + 128], xtile[:, 0:B], fold[:, g:g + CH_HEADS * KEYS])
                ins.then_inc(sim_full, 1)
                similarities(pe, 1)
                similarities(pe, 2)
                wait_for(m, pe, sim_ready, 3)
                wait_for(m, pe, cls_summed, 2)
                for i in range(CH_HEADS):
                    ins = pe.transpose(bank[KVB[0]][:, 128 * i:128 * i + 128], kv[:, i, :], ident[:, :])
                ins.then_inc(cls_turned, 1)
                wait_for(m, pe, cls_taken, 1)
                pe.wait_ge(tab_loaded, DENSE * 16)
                dense_turn(pe, 0)
                tensor_tile(pe, 0, attend=False)
                with pe.Fori(1, TILES - 2) as t:
                    tensor_tile(pe, t)
                tensor_tile(pe, TILES - 2, ahead=False)
                tensor_tile(pe, TILES - 1, ahead=False, more=False)
                tensor_scores(pe, TILES - 1)
                tensor_out(pe, TILES - 1, DENSE * TILES)

            @block.scalar
            def _(act):
                norm_scalar(act, n, 1, xn[:, :, :], sq[:, :, :], s)
                act.wait_ge(folded, GROUPS_K)
                for i in range(2):
                    act.activation(fold[:, 512 * i:512 * i + 512], bank[5 + i][0:S, :], ACT.Copy).then_inc(fold_taken, 1)
                take_turned(act, xt, bank, tfull, ttaken)
                act.wait_ge(ttaken, NG)
                act.activation(xtile[:, 0:B], xt[:, 0:TOK].rearrange("p (b t) -> p b t", t=T)[:, :, S], ACT.Copy).then_inc(x_ready, 1)
                act.wait_ge(sim_full, 1)
                act.activation(sim[:, 0:2 * CH_HEADS, :].rearrange("p g k -> p (g k)"), bank[SIM[0]][:, 0:2 * CH_HEADS * KEYS], ACT.Copy)\
                   .then_inc(sim_ready, 1)
                copy_x(act, 0)
                copy_sim(act, 1)
                act.activation(minus[:, :], ident[:, :], ACT.Copy, scale=-1.0)
                act.activation(one[:, :], ident[:, :], ACT.Copy)
                act.activation(spread[:, :, :].rearrange("p c r -> p (c r)"), spread32, ACT.Copy).then_inc(spread_made, 1)
                exp_weights(act, 0, CH_HEADS)
                copy_x(act, 1)
                exp_weights(act, 1)
                copy_sim(act, 2)
                act.wait_ge(cls_turned, 1)
                act.activation(kvt_cls[:, :, :].rearrange("p (q i) b -> p i q b", i=CH_HEADS),
                               bank[KVB[0]][:, 0:128 * CH_HEADS].rearrange("p (i q b) -> p i q b", i=CH_HEADS, q=4), ACT.Copy).then_inc(cls_taken, 1)
                act.wait_ge(cls_taken, 1)
                act.wait_ge(spread_made, 2)
                split_scalar(act, 0)
                scalar_tile(act, 0, attend=False)
                with act.Fori(1, TILES - 2) as t:
                    scalar_tile(act, t)
                scalar_tile(act, TILES - 2, ahead=False)
                scalar_tile(act, TILES - 1, ahead=False, choose_next=False)
                t = TILES - 1
                for i in range(2):
                    act.wait_ge(vo_full, 2 * t + i + 1)
                    act.activation(vo[i], bank[KVB[i]][0:T, :], ACT.Copy).then_inc(vo_taken, 1)
                act.wait_ge(shifted, t + 1)
                act.activation(probs[:, :, :], probs[:, :, :], ACT.Exp).then_inc(exped, 1)
                for g, (u0, nu) in enumerate(UNIT_BANKS):
                    act.wait_ge(p_turned, 3 * t + g + 1)
                    act.activation(probs_t[:, u0:u0 + nu, :].rearrange("p u t -> p (u t)"), bank[ATT[g]][0:T, 0:T * nu], ACT.Copy)\
                       .then_inc(p_taken, 1)

            @block.vector
            def _(dve):
                link = Chain(dve, n["chain"])
                norm_vector(dve, n, 1, link, h[:, :, :], xn[:, :, :], sq[:, :, :], s)
                dve.wait_ge(loads, LOADS * 16)
                dve.sem_inc(out_added, 1)
                dve.tensor_copy(key_grid[:, :, :], grow(keys64[:, :], 2, TOP))
                dve.tensor_copy(ranks[:, :, 1, :], grow(second[:, :], 1, DENSE))
                choose(dve, CLASS, 1)
                choose(dve, CLASS, 2)
                dve.tensor_copy(wts_cls[:, :, :], best[:, 0:CH_HEADS, :])
                dve.tensor_copy(rows_cls[:, :, :], rows_next[:, 0:CH_HEADS, :]).then_inc(cls_posted, 1)
                dve.wait_ge(cls_posted, 1)
                dve.engine_nop().then_inc(slot_free, 3)
                choose(dve, 1, 1)
                choose(dve, 1, 2)
                post(dve, 1, 0)
                post(dve, 1, 1)
                dve.wait_ge(cls_gathered, 2 * 16 * TOP)
                for i in range(CH_HEADS):
                    dve.tensor_tensor(prod, got[:, 3 + i], grow(wts_cls[:, i, :], 2, 128), ALU.mult).then_inc(slot_free, 1)
                    dve.wait_ge(slot_free, 4 + i)
                    dve.tensor_reduce(kv[:, i, :], prod.rearrange("p j c -> p c j"), AX.X, ALU.add).then_inc(cls_summed, 1)
                    dve.wait_ge(cls_summed, i + 1)
                dve.wait_ge(posted, 2)
                dve.wait_ge(cls_turned, 1)
                vector_tile(dve, 0, attend=False)
                with dve.Fori(1, TILES - 2) as t:
                    vector_tile(dve, t)
                vector_tile(dve, TILES - 2)
                vector_tile(dve, TILES - 1, choose_next=False)
                attend_a(dve, TILES - 1)
                attend_b(dve, TILES - 1)
                attend_c(dve, TILES - 1)


def program(nc, io, out):
    with ExitStack() as ctx:
        def sb(name, shape):
            return ctx.enter_context(nc.sbuf_tensor(name, shape, F32))

        m = {"h": sb("h", [T, B, S]), "waits": ctx.enter_context(nc.semaphore("waits"))}
        with ExitStack() as tower:
            def tsb(name, shape):
                return tower.enter_context(nc.sbuf_tensor(name, shape, F32))

            m["const"] = tsb("const", [128, CONST_COLS])
            m["mix1"] = tsb("mix1", [128, LAYERS, 128])
            m["mix2"] = tsb("mix2", [128, LAYERS, 128])
            m["dc1"] = tsb("dc1", [CH, LAYERS])
            m["dc2"] = tsb("dc2", [CH, LAYERS])
            m["q2col"] = tsb("q2col", [128, 1])
            m["head_w"] = tsb("head_w", [128, LAYERS, OG * NQ])
            m["qacc"] = tsb("qacc", [128, YH, B * S])
            m["spec"] = tsb("spec", [128, KYP, KX, B])
            m["mixw"] = tsb("mixw", [128, MODES, 2, CH])
            m["weights_in"] = tower.enter_context(nc.semaphore("mix_weights_loaded"))
            m["signed"] = tower.enter_context(nc.semaphore("mix_weights_signed"))
            m["inv_in"] = tsb("inv_in", [128, PAIRS, KY, CH])
            spectrum_of_input(nc, io, m)
            fourier_layers(nc, io, m)
            tower_head(nc, io, m)
        m["tok_const"] = sb("tok_const", [128, TOKC_COLS])
        m["xn"] = sb("xn", [T, B, S])
        m["sq"] = sb("sq", [T, B, S])
        m["stats"] = sb("stats", [T, 5 * B])
        m["xt"] = sb("xt", [S, KT * 128])
        release = ctx.enter_context(ExitStack())
        for name in ("probs", "probs_t"):
            m[name] = release.enter_context(nc.sbuf_tensor(name, [T, B, T], F32))
        latent_attention(nc, io, m)
        routed_feed_forward(nc, io, m)
        similarity_attention(nc, io, m)
        release.close()
        memory_attention(nc, io, m)
        store(nc, m, out)


def store(nc, m, out):
    with nc.semaphore("stored") as stored, nc.Block() as block:
        @block.sync
        def _(sp):
            h = m["h"]
            sp.dma_start(out[:, 1:T, :].rearrange("b t d -> t b d"), h[0:S, :, :]).then_inc(stored, 16)
            sp.dma_start(out[:, 0:1, :].rearrange("b t d -> t b d"), h[S:T, :, :]).then_inc(stored, 16)
            sp.wait_ge(stored, 32)


def laid_out(i):
    f = {k: np.asarray(v) for k, v in i.items()}
    ones = np.ones((1, B * S), np.float32)
    grid = np.tile(np.linspace(0.0, 1.0, S).astype(np.float32), B)[None]
    a = {"const": const_table()}
    a["xin"] = np.concatenate([f["x"][..., 0].transpose(2, 0, 1).reshape(S, -1), grid, ones, ones])
    p, pb = f["L0_tok_p_w"], f["L0_tok_p_b"]
    top = np.concatenate([np.repeat(p[:, 0:1], S, 1), p[:, 1:2], pb[:, None], p[:, 2:3]], 1)
    a["lift"] = np.concatenate([top, np.eye(67, dtype=np.float32)[65:66]])
    a["q1t"] = np.concatenate([f["L0_tok_q1_w"].T, f["L0_tok_q1_b"][None]])
    a["w2"] = f["L0_tok_w2_w"]
    a["w1t"] = f["L0_tok_w1_w"].transpose(0, 2, 1)
    a["w2t"] = f["L0_tok_w2_w"].transpose(0, 2, 1)
    a["b1t"] = f["L0_tok_w1_b"].T
    a["b2t"] = f["L0_tok_w2_b"].T
    a["lift_x"] = p[:, 0][None]
    a["lift_c"] = np.tile(np.stack([p[:, 1], p[:, 2], pb]), (4, 1))
    a["q2col"] = np.repeat(f["L0_tok_q2_w"][0], 32)[:, None]
    a["q2b"] = f["L0_tok_q2_b"][None]
    a["cls"] = f["cls_tok"][0]
    w = f["L0_tok_fw"].transpose(0, 6, 5, 2, 1, 4, 3)
    w = w.reshape(LAYERS, 2, KYP, 2, CH, KX, CH)
    w = w.transpose(0, 3, 1, 4, 2, 5, 6)
    w = np.stack([w, w[:, :, ::-1]], 6)
    a["mixw"] = w.reshape(LAYERS, 128, -1)
    a["tok_const"] = token_table()
    swap = np.arange(16).reshape(8, 2)[:, ::-1].reshape(-1)
    q, k = (np.concatenate([f["L0_attn_W" + x + "c"], f["L0_attn_W" + x + "r"], f["L0_attn_W" + x + "c"],
                            f["L0_attn_W" + x + "r"][:, swap]], 1) for x in "qk")
    a["la_up"] = np.concatenate([q, k, f["L0_attn_Wv"]], 1)
    a["la_down"] = np.stack([f["L0_attn_Wq_comp"].T, f["L0_attn_Wkv_comp"].T], 1)
    a["ff_wr"], a["ff_br"] = f["L0_ffn_wr"], f["L0_ffn_br"][None]
    a["ff_w1"], a["ff_w2"] = f["L0_ffn_w1"], f["L0_ffn_w2"]
    a["ff_b1"] = f["L0_ffn_b1"].reshape(2, 128).T
    a["ff_b2"] = f["L0_ffn_b2"][:, None]
    w = f["L1_ffn_Wq_pk"].reshape(S, GROUPS_K, 32)
    a["pk_w"] = w.transpose(2, 1, 0)
    a["pk_k"] = f["L1_ffn_pk_keys"].transpose(3, 0, 2, 1).reshape(32, GROUPS_K, KEYS)
    a["table"] = np.concatenate([f["L1_ffn_keys_table"], f["L1_ffn_values_table"]], 1)
    a["me_wq"] = f["L1_ffn_Wq"].reshape(S, HEADS, S)
    a["me_wo"] = f["L1_ffn_Wo"].reshape(HEADS, S, S).transpose(1, 0, 2)
    i1, i0 = np.divmod(np.arange(KEYS ** 2), KEYS)
    meet = np.arange(KEYS)[:, None]
    a["spread"] = np.concatenate([meet == i0, meet == i1]).astype(np.float32)
    a["keys64"] = np.arange(KEYS, dtype=np.float32)[None]
    a["second_rank"] = TOP - np.arange(TOP, dtype=np.float32)[None]
    a["numbers"] = np.arange(TOP, dtype=np.float32)[None]
    a["first_row"] = np.arange(HEADS, dtype=np.float32)[None] * KEYS ** 2
    a["first_row_cls"] = np.repeat(a["first_row"].reshape(4, CH_HEADS), B, 0)
    return {k: np.ascontiguousarray(v) for k, v in a.items()}


def kernel(**inputs):
    import concourse.bacc as bacc
    from concourse.bass_utils import run_bass_kernel_spmd

    nc = bacc.Bacc("TRN2", target_bir_lowering=False, num_devices=1)
    arrays = laid_out(inputs)
    io = {k: nc.dram_tensor("in_" + k, v.shape, mybir.dt.from_np(v.dtype), kind="ExternalInput").ap() for k, v in arrays.items()}
    out = nc.dram_tensor("out_h", (B, T, S), F32, kind="ExternalOutput").ap()
    program(nc, io, out)
    got = run_bass_kernel_spmd(nc, [{"in_" + k: v for k, v in arrays.items()}], core_ids=[0])
    return got.results[0]["out_h"]
```
